# Optimizing a Trainium2 kernel written in Bass

```python
import numpy as np
import jax
import jax.numpy as jnp

def _softmax(x, axis=-1):
    return jax.nn.softmax(x, axis=axis)

def _gelu(x):
    return jax.nn.gelu(x, approximate=True)

def _silu(x):
    return jax.nn.silu(x)

def _sigmoid(x):
    return jax.nn.sigmoid(x)

def _layernorm(x, axis=-1, eps=1e-05):
    m = jnp.mean(x, axis=axis, keepdims=True)
    v = jnp.var(x, axis=axis, keepdims=True)
    return (x - m) / jnp.sqrt(v + eps)

def _scatter_add(tgt, idx, src, axis=0):
    return tgt.at[idx].add(src)

def _segment_sum(src, seg, n):
    return jax.ops.segment_sum(src, seg, n)
kernel_name = 'mk_gnn_ffn_d2_gnn_r8_d2d9ce'

def setup_inputs(seed: int=0):
    np.random.seed(seed)
    _w = jnp.asarray

    def _rec_inputs():
        import jax
        import jax.numpy as jnp
        _gk = jax.random.key(seed)
        x = -0.0001394 + 0.9999 * jax.random.normal(jax.random.fold_in(_gk, 1), (1250, 768), jnp.float32)
        src = jax.random.randint(jax.random.fold_in(_gk, 2), (20000,), 0, 1250, jnp.int32)
        dst = jax.random.randint(jax.random.fold_in(_gk, 3), (20000,), 0, 1250, jnp.int32)
        _o = jnp.argsort(dst, stable=True)
        src = src[_o]
        dst = dst[_o]
        edge_weight = jax.random.uniform(jax.random.fold_in(_gk, 12), (20000,), jnp.float32, 0.0, 0.999998)
        return (x, src, dst, edge_weight)
    x, src, dst, edge_weight = _rec_inputs()

    def _L0_gnn_setup():
        import jax, jax.numpy as jnp
        import numpy as np
        N = 6250
        E = 62500
        D = 768
        H = 256
        R = 32

        def _gcn(x, W, b, row, col, ew):
            x = x @ W
            n = x.shape[0]
            deg = jax.ops.segment_sum(ew, col, num_segments=n) + 1.0
            dinv = jax.lax.rsqrt(deg)
            norm = dinv[row] * ew * dinv[col]
            agg = jax.ops.segment_sum(norm[:, None] * x[row], col, num_segments=n)
            return agg + (dinv * dinv)[:, None] * x + b
        key = jax.random.key(seed)
        ks = jax.random.split(key, 8)
        d = D // R
        w = lambda k, sh: jax.random.normal(k, sh, jnp.float32) * 0.05
        return {'x': jax.random.normal(ks[0], (N, D), jnp.float32), 'edge_index': jax.random.randint(ks[1], (2, E), 0, N), 'edge_weight': jax.random.uniform(ks[2], (E,), jnp.float32), 'Wd': w(ks[3], (D, d)), 'bd': jnp.zeros((d,), jnp.float32), 'Wu': w(ks[4], (d, D)), 'bu': jnp.zeros((D,), jnp.float32), 'W1': w(ks[5], (D, H)), 'b1': jnp.zeros((H,), jnp.float32), 'W2': w(ks[6], (H, D)), 'b2': jnp.zeros((D,), jnp.float32)}
    _L0_gnn_all = _L0_gnn_setup()
    _L0_gnn_in = {k: v for k, v in _L0_gnn_all.items() if k in ('Wd', 'bd', 'Wu', 'bu', 'W1', 'b1', 'W2', 'b2')}
    del _L0_gnn_all

    def _L0_ffn_setup():
        import jax, jax.numpy as jnp
        import numpy as np
        DIM = 768
        HEADS = 12
        HD = DIM // HEADS
        MLP = 384
        RHD = 512
        RANK = 256
        BS = 2
        RESERVE = 1
        EPS = 1e-05

        def _ln(x, g, b):
            m = jnp.mean(x, axis=-1, keepdims=True)
            v = jnp.var(x, axis=-1, keepdims=True)
            return (x - m) / jnp.sqrt(v + EPS) * g + b

        def _gelu(t):
            return jax.nn.gelu(t, approximate=False)

        def _forward(x, wq, bq, wk, bk, wv, bv, wo, bo, ln1_g, ln1_b, ln2_g, ln2_b, fc1_w, fc1_b, fc2_w, fc2_b, r_ln_g, r_ln_b, r_in_w, r_in_b, r_o1_w, r_o1_b, r_o2_w, r_o2_b, r_o3_w, r_o3_b, lra_down, lra_up):
            B, N, _ = x.shape
            e = _gelu(_ln(x, r_ln_g, r_ln_b) @ r_in_w.T + r_in_b)
            g = jnp.mean(e[:, RESERVE:, :], axis=1, keepdims=True)
            f = jnp.concatenate([e, jnp.broadcast_to(g, e.shape)], axis=-1)
            h1 = _gelu(f @ r_o1_w.T + r_o1_b)
            h2 = _gelu(h1 @ r_o2_w.T + r_o2_b)
            logits = (h2 @ r_o3_w.T + r_o3_b).reshape(B, N, BS, 2)
            hard = jax.nn.one_hot(jnp.argmax(logits, axis=-1), 2, dtype=x.dtype)
            keep = jnp.broadcast_to(jnp.array([0.0, 1.0], dtype=x.dtype), hard[:, :RESERVE].shape)
            hard = hard.at[:, :RESERVE].set(keep)
            hard = jax.lax.stop_gradient(hard)
            bits = hard[..., 1]
            indices = (bits * jnp.array([2.0, 1.0], dtype=x.dtype)).sum(-1).astype(jnp.int32)
            indices = jax.lax.stop_gradient(indices)
            xa = _ln(x, ln1_g, ln1_b)
            q = (xa @ wq.T + bq).reshape(B, N, HEADS, HD).transpose(0, 2, 1, 3)
            k = (xa @ wk.T + bk).reshape(B, N, HEADS, HD).transpose(0, 2, 1, 3)
            v = (xa @ wv.T + bv).reshape(B, N, HEADS, HD).transpose(0, 2, 1, 3)
            s = jax.nn.softmax(jnp.einsum('bhqd,bhkd->bhqk', q, k) / np.float32(np.sqrt(HD)), axis=-1)
            o = jnp.einsum('bhqk,bhkd->bhqd', s, v).transpose(0, 2, 1, 3).reshape(B, N, DIM)
            o = o @ wo.T + bo
            h = x + bits[:, :, 0:1] * o
            xf = _ln(h, ln2_g, ln2_b)
            ff = _gelu(xf @ fc1_w.T + fc1_b) @ fc2_w.T + fc2_b
            out = h + bits[:, :, 1:2] * ff
            down = jnp.einsum('bnd,krd->bknr', out, lra_down)
            up = jnp.einsum('bknr,kdr->bknd', down, lra_up)
            sel = jax.nn.one_hot(indices, 3, dtype=x.dtype)
            out = out + jnp.einsum('bknd,bnk->bnd', up, sel)
            return out
        key = jax.random.key(seed)
        ks = iter(jax.random.split(key, 40))

        def w(shape, std=0.02):
            return (jax.random.normal(next(ks), shape) * std).astype(jnp.float32)
        B, N = (128, 197)
        inp = {'x': jax.random.normal(next(ks), (B, N, DIM), dtype=jnp.float32)}
        inp.update(wq=w((DIM, DIM)), bq=jnp.zeros((DIM,), jnp.float32), wk=w((DIM, DIM)), bk=jnp.zeros((DIM,), jnp.float32), wv=w((DIM, DIM)), bv=jnp.zeros((DIM,), jnp.float32), wo=w((DIM, DIM)), bo=jnp.zeros((DIM,), jnp.float32), ln1_g=jnp.ones((DIM,), jnp.float32), ln1_b=jnp.zeros((DIM,), jnp.float32), ln2_g=jnp.ones((DIM,), jnp.float32), ln2_b=jnp.zeros((DIM,), jnp.float32), fc1_w=w((MLP, DIM)), fc1_b=jnp.zeros((MLP,), jnp.float32), fc2_w=w((DIM, MLP)), fc2_b=jnp.zeros((DIM,), jnp.float32), r_ln_g=jnp.ones((DIM,), jnp.float32), r_ln_b=jnp.zeros((DIM,), jnp.float32), r_in_w=w((RHD, DIM)), r_in_b=jnp.zeros((RHD,), jnp.float32), r_o1_w=w((RHD, 2 * RHD)), r_o1_b=jnp.zeros((RHD,), jnp.float32), r_o2_w=w((RHD // 2, RHD)), r_o2_b=jnp.zeros((RHD // 2,), jnp.float32), r_o3_w=w((2 * BS, RHD // 2), 0.01), r_o3_b=jnp.array([0.0, 5.0, 0.0, 5.0], dtype=jnp.float32), lra_down=w((3, RANK, DIM), 0.01), lra_up=w((3, DIM, RANK), 0.01))
        return inp
    _L0_ffn_all = _L0_ffn_setup()
    _L0_ffn_in = {k: v for k, v in _L0_ffn_all.items() if k in ('wq', 'bq', 'wk', 'bk', 'wv', 'bv', 'wo', 'bo', 'ln1_g', 'ln1_b', 'ln2_g', 'ln2_b', 'fc1_w', 'fc1_b', 'fc2_w', 'fc2_b', 'r_ln_g', 'r_ln_b', 'r_in_w', 'r_in_b', 'r_o1_w', 'r_o1_b', 'r_o2_w', 'r_o2_b', 'r_o3_w', 'r_o3_b', 'lra_down', 'lra_up')}
    del _L0_ffn_all

    def _L1_gnn_setup():
        import jax, jax.numpy as jnp
        import numpy as np
        N_NODES = 1250
        N_EDGES = 12500
        DIM = 768
        NEG_SLOPE = 0.2

        def gat_conv(x, src, dst, W, att_src, att_dst, bias, num_nodes):
            h = x @ W
            a_s = h @ att_src
            a_d = h @ att_dst
            e = jax.nn.leaky_relu(a_s[src] + a_d[dst], NEG_SLOPE)
            m = jax.ops.segment_max(e, dst, num_segments=num_nodes)
            e = jnp.exp(e - m[dst])
            denom = jax.ops.segment_sum(e, dst, num_segments=num_nodes)
            alpha = e / denom[dst]
            msg = alpha[:, None] * h[src]
            out = jax.ops.segment_sum(msg, dst, num_segments=num_nodes)
            return out + bias
        key = jax.random.key(seed)
        ks = jax.random.split(key, 12)
        s = 1.0 / np.sqrt(DIM)
        inp = {'x': jax.random.normal(ks[0], (N_NODES, DIM), dtype=jnp.float32), 'edge_index': jax.random.randint(ks[1], (2, N_EDGES), 0, N_NODES, dtype=jnp.int64), 'W1': jax.random.normal(ks[2], (DIM, DIM), dtype=jnp.float32) * s, 'att_src1': jax.random.normal(ks[3], (DIM,), dtype=jnp.float32) * s, 'att_dst1': jax.random.normal(ks[4], (DIM,), dtype=jnp.float32) * s, 'b1': jnp.zeros((DIM,), dtype=jnp.float32), 'W2': jax.random.normal(ks[5], (DIM, DIM), dtype=jnp.float32) * s, 'att_src2': jax.random.normal(ks[6], (DIM,), dtype=jnp.float32) * s, 'att_dst2': jax.random.normal(ks[7], (DIM,), dtype=jnp.float32) * s, 'b2': jnp.zeros((DIM,), dtype=jnp.float32)}
        return inp
    _L1_gnn_all = _L1_gnn_setup()
    _L1_gnn_in = {k: v for k, v in _L1_gnn_all.items() if k in ('W1', 'att_src1', 'att_dst1', 'b1', 'W2', 'att_src2', 'att_dst2', 'b2')}
    del _L1_gnn_all

    def _L1_ffn_setup():
        import jax, jax.numpy as jnp
        import numpy as np
        B, S, H, D, E = (4, 256, 768, 1024, 8)
        TOP_K = 2
        EPS = 1e-08
        LN_EPS = 1e-05

        def _gelu(t):
            return jax.nn.gelu(t, approximate=False)

        def _layer_norm(t, gamma, beta):
            mu = jnp.mean(t, axis=-1, keepdims=True)
            var = jnp.mean(jnp.square(t - mu), axis=-1, keepdims=True)
            return (t - mu) * jax.lax.rsqrt(var + LN_EPS) * gamma + beta
        key = jax.random.key(seed)
        ks = jax.random.split(key, 8)
        x = jax.random.normal(ks[0], (B, S, H), dtype=jnp.float32)
        w1 = jax.random.normal(ks[1], (H, H // 2), dtype=jnp.float32) * 0.02
        b1 = jnp.zeros((H // 2,), dtype=jnp.float32)
        w2 = jax.random.normal(ks[2], (H // 2, E), dtype=jnp.float32) * 0.02
        b2 = jnp.zeros((E,), dtype=jnp.float32)
        a_dn = float(np.sqrt(6.0 / (H + D)))
        a_up = float(np.sqrt(6.0 / (D + H)))
        down_w = jax.random.uniform(ks[3], (E, H, D), dtype=jnp.float32, minval=-a_dn, maxval=a_dn)
        down_b = jnp.zeros((E, D), dtype=jnp.float32)
        up_w = jax.random.uniform(ks[4], (E, D, H), dtype=jnp.float32, minval=-a_up, maxval=a_up)
        gamma = jnp.ones((H,), dtype=jnp.float32)
        beta = jnp.zeros((H,), dtype=jnp.float32)
        return {'x': x, 'w1': w1, 'b1': b1, 'w2': w2, 'b2': b2, 'down_w': down_w, 'down_b': down_b, 'up_w': up_w, 'gamma': gamma, 'beta': beta}
    _L1_ffn_all = _L1_ffn_setup()
    _L1_ffn_in = {k: v for k, v in _L1_ffn_all.items() if k in ('w1', 'b1', 'w2', 'b2', 'down_w', 'down_b', 'up_w', 'gamma', 'beta')}
    del _L1_ffn_all
    return {'x': x, 'src': src, 'dst': dst, 'edge_weight': edge_weight, 'L0_gnn_Wd': _L0_gnn_in['Wd'], 'L0_gnn_bd': _L0_gnn_in['bd'], 'L0_gnn_Wu': _L0_gnn_in['Wu'], 'L0_gnn_bu': _L0_gnn_in['bu'], 'L0_gnn_W1': _L0_gnn_in['W1'], 'L0_gnn_b1': _L0_gnn_in['b1'], 'L0_gnn_W2': _L0_gnn_in['W2'], 'L0_gnn_b2': _L0_gnn_in['b2'], 'L0_ffn_wq': _L0_ffn_in['wq'], 'L0_ffn_bq': _L0_ffn_in['bq'], 'L0_ffn_wk': _L0_ffn_in['wk'], 'L0_ffn_bk': _L0_ffn_in['bk'], 'L0_ffn_wv': _L0_ffn_in['wv'], 'L0_ffn_bv': _L0_ffn_in['bv'], 'L0_ffn_wo': _L0_ffn_in['wo'], 'L0_ffn_bo': _L0_ffn_in['bo'], 'L0_ffn_ln1_g': _L0_ffn_in['ln1_g'], 'L0_ffn_ln1_b': _L0_ffn_in['ln1_b'], 'L0_ffn_ln2_g': _L0_ffn_in['ln2_g'], 'L0_ffn_ln2_b': _L0_ffn_in['ln2_b'], 'L0_ffn_fc1_w': _L0_ffn_in['fc1_w'], 'L0_ffn_fc1_b': _L0_ffn_in['fc1_b'], 'L0_ffn_fc2_w': _L0_ffn_in['fc2_w'], 'L0_ffn_fc2_b': _L0_ffn_in['fc2_b'], 'L0_ffn_r_ln_g': _L0_ffn_in['r_ln_g'], 'L0_ffn_r_ln_b': _L0_ffn_in['r_ln_b'], 'L0_ffn_r_in_w': _L0_ffn_in['r_in_w'], 'L0_ffn_r_in_b': _L0_ffn_in['r_in_b'], 'L0_ffn_r_o1_w': _L0_ffn_in['r_o1_w'], 'L0_ffn_r_o1_b': _L0_ffn_in['r_o1_b'], 'L0_ffn_r_o2_w': _L0_ffn_in['r_o2_w'], 'L0_ffn_r_o2_b': _L0_ffn_in['r_o2_b'], 'L0_ffn_r_o3_w': _L0_ffn_in['r_o3_w'], 'L0_ffn_r_o3_b': _L0_ffn_in['r_o3_b'], 'L0_ffn_lra_down': _L0_ffn_in['lra_down'], 'L0_ffn_lra_up': _L0_ffn_in['lra_up'], 'L1_gnn_W1': _L1_gnn_in['W1'], 'L1_gnn_att_src1': _L1_gnn_in['att_src1'], 'L1_gnn_att_dst1': _L1_gnn_in['att_dst1'], 'L1_gnn_b1': _L1_gnn_in['b1'], 'L1_gnn_W2': _L1_gnn_in['W2'], 'L1_gnn_att_src2': _L1_gnn_in['att_src2'], 'L1_gnn_att_dst2': _L1_gnn_in['att_dst2'], 'L1_gnn_b2': _L1_gnn_in['b2'], 'L1_ffn_w1': _L1_ffn_in['w1'], 'L1_ffn_b1': _L1_ffn_in['b1'], 'L1_ffn_w2': _L1_ffn_in['w2'], 'L1_ffn_b2': _L1_ffn_in['b2'], 'L1_ffn_down_w': _L1_ffn_in['down_w'], 'L1_ffn_down_b': _L1_ffn_in['down_b'], 'L1_ffn_up_w': _L1_ffn_in['up_w'], 'L1_ffn_gamma': _L1_ffn_in['gamma'], 'L1_ffn_beta': _L1_ffn_in['beta']}

def reference(x, src, dst, edge_weight, L0_gnn_Wd, L0_gnn_bd, L0_gnn_Wu, L0_gnn_bu, L0_gnn_W1, L0_gnn_b1, L0_gnn_W2, L0_gnn_b2, L0_ffn_wq, L0_ffn_bq, L0_ffn_wk, L0_ffn_bk, L0_ffn_wv, L0_ffn_bv, L0_ffn_wo, L0_ffn_bo, L0_ffn_ln1_g, L0_ffn_ln1_b, L0_ffn_ln2_g, L0_ffn_ln2_b, L0_ffn_fc1_w, L0_ffn_fc1_b, L0_ffn_fc2_w, L0_ffn_fc2_b, L0_ffn_r_ln_g, L0_ffn_r_ln_b, L0_ffn_r_in_w, L0_ffn_r_in_b, L0_ffn_r_o1_w, L0_ffn_r_o1_b, L0_ffn_r_o2_w, L0_ffn_r_o2_b, L0_ffn_r_o3_w, L0_ffn_r_o3_b, L0_ffn_lra_down, L0_ffn_lra_up, L1_gnn_W1, L1_gnn_att_src1, L1_gnn_att_dst1, L1_gnn_b1, L1_gnn_W2, L1_gnn_att_src2, L1_gnn_att_dst2, L1_gnn_b2, L1_ffn_w1, L1_ffn_b1, L1_ffn_w2, L1_ffn_b2, L1_ffn_down_w, L1_ffn_down_b, L1_ffn_up_w, L1_ffn_gamma, L1_ffn_beta):
    import jax
    import jax.numpy as jnp

    def _L0_gnn_ref(x, edge_index, edge_weight, Wd, bd, Wu, bu, W1, b1, W2, b2):
        import jax, jax.numpy as jnp
        import numpy as np
        N = 6250
        E = 62500
        D = 768
        H = 256
        R = 32

        def _gcn(x, W, b, row, col, ew):
            x = x @ W
            n = x.shape[0]
            deg = jax.ops.segment_sum(ew, col, num_segments=n) + 1.0
            dinv = jax.lax.rsqrt(deg)
            norm = dinv[row] * ew * dinv[col]
            agg = jax.ops.segment_sum(norm[:, None] * x[row], col, num_segments=n)
            return agg + (dinv * dinv)[:, None] * x + b
        h = jax.nn.relu(x @ Wd + bd) @ Wu + bu + x
        row, col = (edge_index[0], edge_index[1])
        h = jax.nn.relu(_gcn(h, W1, b1, row, col, edge_weight))
        h = _gcn(h, W2, b2, row, col, edge_weight)
        return h

    def _L0_ffn_ref(x, wq, bq, wk, bk, wv, bv, wo, bo, ln1_g, ln1_b, ln2_g, ln2_b, fc1_w, fc1_b, fc2_w, fc2_b, r_ln_g, r_ln_b, r_in_w, r_in_b, r_o1_w, r_o1_b, r_o2_w, r_o2_b, r_o3_w, r_o3_b, lra_down, lra_up):
        import jax, jax.numpy as jnp
        import numpy as np
        DIM = 768
        HEADS = 12
        HD = DIM // HEADS
        MLP = 384
        RHD = 512
        RANK = 256
        BS = 2
        RESERVE = 1
        EPS = 1e-05

        def _ln(x, g, b):
            m = jnp.mean(x, axis=-1, keepdims=True)
            v = jnp.var(x, axis=-1, keepdims=True)
            return (x - m) / jnp.sqrt(v + EPS) * g + b

        def _gelu(t):
            return jax.nn.gelu(t, approximate=False)

        def _forward(x, wq, bq, wk, bk, wv, bv, wo, bo, ln1_g, ln1_b, ln2_g, ln2_b, fc1_w, fc1_b, fc2_w, fc2_b, r_ln_g, r_ln_b, r_in_w, r_in_b, r_o1_w, r_o1_b, r_o2_w, r_o2_b, r_o3_w, r_o3_b, lra_down, lra_up):
            B, N, _ = x.shape
            e = _gelu(_ln(x, r_ln_g, r_ln_b) @ r_in_w.T + r_in_b)
            g = jnp.mean(e[:, RESERVE:, :], axis=1, keepdims=True)
            f = jnp.concatenate([e, jnp.broadcast_to(g, e.shape)], axis=-1)
            h1 = _gelu(f @ r_o1_w.T + r_o1_b)
            h2 = _gelu(h1 @ r_o2_w.T + r_o2_b)
            logits = (h2 @ r_o3_w.T + r_o3_b).reshape(B, N, BS, 2)
            hard = jax.nn.one_hot(jnp.argmax(logits, axis=-1), 2, dtype=x.dtype)
            keep = jnp.broadcast_to(jnp.array([0.0, 1.0], dtype=x.dtype), hard[:, :RESERVE].shape)
            hard = hard.at[:, :RESERVE].set(keep)
            hard = jax.lax.stop_gradient(hard)
            bits = hard[..., 1]
            indices = (bits * jnp.array([2.0, 1.0], dtype=x.dtype)).sum(-1).astype(jnp.int32)
            indices = jax.lax.stop_gradient(indices)
            xa = _ln(x, ln1_g, ln1_b)
            q = (xa @ wq.T + bq).reshape(B, N, HEADS, HD).transpose(0, 2, 1, 3)
            k = (xa @ wk.T + bk).reshape(B, N, HEADS, HD).transpose(0, 2, 1, 3)
            v = (xa @ wv.T + bv).reshape(B, N, HEADS, HD).transpose(0, 2, 1, 3)
            s = jax.nn.softmax(jnp.einsum('bhqd,bhkd->bhqk', q, k) / np.float32(np.sqrt(HD)), axis=-1)
            o = jnp.einsum('bhqk,bhkd->bhqd', s, v).transpose(0, 2, 1, 3).reshape(B, N, DIM)
            o = o @ wo.T + bo
            h = x + bits[:, :, 0:1] * o
            xf = _ln(h, ln2_g, ln2_b)
            ff = _gelu(xf @ fc1_w.T + fc1_b) @ fc2_w.T + fc2_b
            out = h + bits[:, :, 1:2] * ff
            down = jnp.einsum('bnd,krd->bknr', out, lra_down)
            up = jnp.einsum('bknr,kdr->bknd', down, lra_up)
            sel = jax.nn.one_hot(indices, 3, dtype=x.dtype)
            out = out + jnp.einsum('bknd,bnk->bnd', up, sel)
            return out
        return _forward(x, wq, bq, wk, bk, wv, bv, wo, bo, ln1_g, ln1_b, ln2_g, ln2_b, fc1_w, fc1_b, fc2_w, fc2_b, r_ln_g, r_ln_b, r_in_w, r_in_b, r_o1_w, r_o1_b, r_o2_w, r_o2_b, r_o3_w, r_o3_b, lra_down, lra_up)

    def _L1_gnn_ref(x, edge_index, W1, att_src1, att_dst1, b1, W2, att_src2, att_dst2, b2):
        import jax, jax.numpy as jnp
        import numpy as np
        N_NODES = 1250
        N_EDGES = 12500
        DIM = 768
        NEG_SLOPE = 0.2

        def gat_conv(x, src, dst, W, att_src, att_dst, bias, num_nodes):
            h = x @ W
            a_s = h @ att_src
            a_d = h @ att_dst
            e = jax.nn.leaky_relu(a_s[src] + a_d[dst], NEG_SLOPE)
            m = jax.ops.segment_max(e, dst, num_segments=num_nodes)
            e = jnp.exp(e - m[dst])
            denom = jax.ops.segment_sum(e, dst, num_segments=num_nodes)
            alpha = e / denom[dst]
            msg = alpha[:, None] * h[src]
            out = jax.ops.segment_sum(msg, dst, num_segments=num_nodes)
            return out + bias
        n = x.shape[0]
        loops = jnp.arange(n, dtype=edge_index.dtype)
        src = jnp.concatenate([edge_index[0], loops])
        dst = jnp.concatenate([edge_index[1], loops])
        h = gat_conv(x, src, dst, W1, att_src1, att_dst1, b1, n)
        h = jax.nn.relu(h)
        out = gat_conv(h, src, dst, W2, att_src2, att_dst2, b2, n)
        return out

    def _L1_ffn_ref(x, w1, b1, w2, b2, down_w, down_b, up_w, gamma, beta):
        import jax, jax.numpy as jnp
        import numpy as np
        B, S, H, D, E = (4, 256, 768, 1024, 8)
        TOP_K = 2
        EPS = 1e-08
        LN_EPS = 1e-05

        def _gelu(t):
            return jax.nn.gelu(t, approximate=False)

        def _layer_norm(t, gamma, beta):
            mu = jnp.mean(t, axis=-1, keepdims=True)
            var = jnp.mean(jnp.square(t - mu), axis=-1, keepdims=True)
            return (t - mu) * jax.lax.rsqrt(var + LN_EPS) * gamma + beta
        logits = _gelu(x @ w1 + b1) @ w2 + b2
        routing = jax.nn.softmax(logits, axis=-1)
        topv, topi = jax.lax.top_k(routing, TOP_K)
        sparse = jnp.sum(jax.nn.one_hot(topi, E, dtype=routing.dtype) * topv[..., None], axis=-2)
        sparse = sparse / (jnp.sum(sparse, axis=-1, keepdims=True) + EPS)
        z = _gelu(jnp.einsum('bsh,ehd->bsed', x, down_w) + down_b)
        expert_out = jnp.einsum('bsed,edh->bseh', z, up_w)
        moe_out = jnp.einsum('bseh,bse->bsh', expert_out, sparse)
        return _layer_norm(x + moe_out, gamma, beta)
    edge_index = jnp.stack([src, dst])
    x = x + _L0_gnn_ref(_layernorm(x, axis=-1), edge_index, edge_weight, L0_gnn_Wd, L0_gnn_bd, L0_gnn_Wu, L0_gnn_bu, L0_gnn_W1, L0_gnn_b1, L0_gnn_W2, L0_gnn_b2)
    x = x + _L0_ffn_ref(_layernorm(x, axis=-1)[None], L0_ffn_wq, L0_ffn_bq, L0_ffn_wk, L0_ffn_bk, L0_ffn_wv, L0_ffn_bv, L0_ffn_wo, L0_ffn_bo, L0_ffn_ln1_g, L0_ffn_ln1_b, L0_ffn_ln2_g, L0_ffn_ln2_b, L0_ffn_fc1_w, L0_ffn_fc1_b, L0_ffn_fc2_w, L0_ffn_fc2_b, L0_ffn_r_ln_g, L0_ffn_r_ln_b, L0_ffn_r_in_w, L0_ffn_r_in_b, L0_ffn_r_o1_w, L0_ffn_r_o1_b, L0_ffn_r_o2_w, L0_ffn_r_o2_b, L0_ffn_r_o3_w, L0_ffn_r_o3_b, L0_ffn_lra_down, L0_ffn_lra_up)[0]
    x = x + _L1_gnn_ref(_layernorm(x, axis=-1), edge_index, L1_gnn_W1, L1_gnn_att_src1, L1_gnn_att_dst1, L1_gnn_b1, L1_gnn_W2, L1_gnn_att_src2, L1_gnn_att_dst2, L1_gnn_b2)
    x = x + _L1_ffn_ref(_layernorm(x, axis=-1)[None], L1_ffn_w1, L1_ffn_b1, L1_ffn_w2, L1_ffn_b2, L1_ffn_down_w, L1_ffn_down_b, L1_ffn_up_w, L1_ffn_gamma, L1_ffn_beta)[0]
    return x

_drawn_inputs = setup_inputs


def setup_inputs(seed=0):
    import zlib

    import numpy as np

    out = dict(_drawn_inputs(seed))
    spreads = {'L0_gnn_bd': (0.0, 0.8),
     'L0_gnn_bu': (0.0, 0.1),
     'L0_gnn_b1': (0.0, 0.1),
     'L0_gnn_b2': (0.0, 0.1),
     'L0_ffn_bq': (0.0, 0.8),
     'L0_ffn_bk': (0.0, 0.8),
     'L0_ffn_bv': (0.0, 0.1),
     'L0_ffn_bo': (0.0, 0.1),
     'L0_ffn_ln1_g': (1.0, 0.6),
     'L0_ffn_ln1_b': (0.0, 0.305),
     'L0_ffn_ln2_g': (1.0, 0.6),
     'L0_ffn_ln2_b': (0.0, 0.633),
     'L0_ffn_fc1_b': (0.0, 0.414),
     'L0_ffn_fc2_b': (0.0, 0.1),
     'L0_ffn_r_ln_g': (1.0, 0.2),
     'L0_ffn_r_ln_b': (0.0, 0.1),
     'L0_ffn_r_in_b': (0.0, 0.1),
     'L0_ffn_r_o1_b': (0.0, 0.1),
     'L0_ffn_r_o2_b': (0.0, 0.1),
     'L1_gnn_b1': (0.0, 0.1),
     'L1_gnn_b2': (0.0, 0.1),
     'L1_ffn_b1': (0.0, 0.1),
     'L1_ffn_b2': (0.0, 0.1),
     'L1_ffn_down_b': (0.0, 0.503),
     'L1_ffn_gamma': (1.0, 0.2),
     'L1_ffn_beta': (0.0, 0.1)}
    factors = {'L0_gnn_Wd': 2.881,
     'L0_ffn_wq': 8.0,
     'L0_ffn_wk': 8.0,
     'L1_gnn_att_dst1': 6.052,
     'L1_gnn_att_src2': 7.06,
     'L1_gnn_att_dst2': 8.0}
    for name, (base, spread) in spreads.items():
        noise = np.random.default_rng([zlib.crc32(name.encode()), seed]).standard_normal(out[name].shape)
        drawn = base * np.exp(spread * noise) if base else spread * noise
        out[name] = jnp.asarray(drawn.astype(out[name].dtype))
    for name, factor in factors.items():
        out[name] = (out[name] * factor).astype(out[name].dtype)
    return out
```

```python
from contextlib import ExitStack, contextmanager

import numpy as np

import concourse.bass as bass
from concourse import mybir

F32 = mybir.dt.float32
BF16 = mybir.dt.bfloat16
F16 = mybir.dt.float16
U16 = mybir.dt.uint16
I32 = mybir.dt.int32
ACT = mybir.ActivationFunctionType
ALU = mybir.AluOpType
AX = mybir.AxisListType

P = 128
N = 1250
TT = 10
TL = N // TT
D = 768
KD = D // P
EDGES = 20000
ET = EDGES // TL
EQ = ET // 2
HEADS, HD = 12, 64
HP = HEADS // 2
BOT = 24
EXPERTS, DE = 8, 1024
KE = DE // P
CH = [(0, 417), (417, 417), (834, 416)]
GROUPS = [(0, 4), (4, 4), (8, 2)]
BIG = 1.0e30
LN_EPS = 1e-5
BUCKETS = [(0, 3), (3, 3), (6, 3), (9, 1)]
BLOCKS = 4

VECTORS = [("bd", 1), ("bu", 6), ("gb1", 2), ("gb2", 6), ("r_g", 6), ("r_b", 6), ("l1_g", 6), ("l1_b", 6),
           ("r_in_b", 4), ("r_o1_b", 4), ("r_o2_b", 2), ("r_o3_b", 1), ("bq", 6), ("bk", 6), ("bv", 6),
           ("bo", 6), ("l2_g", 6), ("l2_b", 6), ("fc1_b", 3), ("fc2_b", 6),
           ("as1", 6), ("ad1", 6), ("gat_b1", 6), ("as2", 6), ("ad2", 6), ("gat_b2", 6),
           ("m_b1", 3), ("m_b2", 1), ("down_b", EXPERTS * KE)]
COL, NCOL = {}, 0
for _name, _n in VECTORS:
    COL[_name] = NCOL
    NCOL += _n

STREAMED = {"w1": (2, 6), "w2": (6, 2), "r_in": (4, 6), "r_o1": (4, 8), "r_o2": (2, 4), "wqkv": (18, 6),
            "wo": (6, 6), "fc1": (3, 6), "fc2": (6, 3), "lra_down": (6, 6), "lra_up": (6, 6),
            "gat_w1": (6, 6), "gat_w2": (6, 6), "m_w1": (3, 6), "down": (EXPERTS * KE, 6), "up": (EXPERTS * 6, KE)}


class Tally:

    passed = {}

    def __init__(self, sem, start=0):
        self.sem, self.count, self.loops = sem, start, []

    def add(self, n=1):
        self.count += n

    def inc(self, instruction, n=1):
        instruction.then_inc(self.sem, n)
        self.count += n

    def value(self, back=0):
        v = self.count - back
        for i, per in self.loops:
            if per:
                v = i * per + v
        return v

    def wait(self, eng, back=0, alone=False):
        if self.count - back > 0:
            value = self.value(back)
            eng.wait_ge(self.sem, value)
            if alone and not isinstance(value, int):
                eng.sem_inc(self.passed[eng.engine], 1)
        else:
            assert not any(per for _, per in self.loops), "a wait below one in a loop"


@contextmanager
def repeat(eng, n, per):
    with eng.Fori(0, n) as i:
        was = [t.count for t, _ in per]
        for t, by in per:
            t.loops.append((i, by))
        yield i
        got = [t.count - w for (t, _), w in zip(per, was)]
        for t, by in per:
            t.loops.pop()
        assert got == [by for _, by in per], (got, [by for _, by in per])
    for t, by in per:
        t.count += by * (n - 1)


PLAN = {"counts": (0, 4), "matrices": (2 * TT, 0), "w_transpose": (0, 3 * TT), "rows": (0, 2 * TT),
        "adapter": (7, 0), "pair": (2, 0), "pair_back": (0, 6), "pairs3": (6, 0), "pairs3_back": (6, 18),
        "r_in": (4, 0), "r_o1": (4, 4), "r_o2": (2, 0), "logits": (1, 0), "masks": (2, 0), "qk": (12, 0),
        "fc1": (3, 0), "att": (2, 1), "alpha": (0, 3 * TT), "agg0": (6, 18), "agg1": (6, 36),
        "m_w1": (3, 0), "gates": (1, 4), "experts": (EXPERTS * 14, 0), "back3": (0, 18)}


class Side:

    def __init__(self, eng, S):
        self.eng = eng
        self.JD = [Tally(S["job_done0"]), Tally(S["job_done1"])]
        self.JO = [Tally(S["job_out0"], 3), Tally(S["job_out1"], 3)]
        self.TD = [Tally(S["unit_done0"]), Tally(S["unit_done1"])]
        self.TO = [Tally(S["unit_out0"], 1), Tally(S["unit_out1"], 1)]
        self.W = [Tally(S["w_full0"]), Tally(S["w_full1"])]
        self.job = self.unit = 0

    @contextmanager
    def loop(self, n, jobs=0, units=0, weights=0, extra=()):
        assert jobs % 2 == 0 and units % 2 == 0 and weights % 2 == 0
        per = [(t, 3 * jobs // 2) for t in self.JD + self.JO] + [(t, units // 2) for t in self.TD + self.TO]
        per += [(t, 16 * weights // 2) for t in self.W] + list(extra)
        with repeat(self.eng, n, per) as i:
            yield i

    def next_job(self):
        self.job += 1
        return (self.job - 1) % 2

    def next_unit(self):
        self.unit += 1
        return (self.unit - 1) % 2

    def wait_chunk(self, s):
        self.JD[s].add(1)
        self.JD[s].wait(self.eng, alone=self.eng.engine == mybir.EngineType.Activation)

    def wait_unit(self, b):
        self.TD[b].add(1)
        self.TD[b].wait(self.eng, alone=self.eng.engine == mybir.EngineType.Activation)

    def slot(self, ahead=0):
        return (self.job + ahead) % 2

    def skip(self, *stages):
        for name in stages:
            if name == "attention":
                for t in self.JD + self.JO:
                    t.add(30 * HP)
                for t in self.TD + self.TO:
                    t.add(40 * HP)
                continue
            jobs, units = PLAN[name]
            for _ in range(jobs):
                s = self.next_job()
                self.JD[s].add(3)
                self.JO[s].add(3)
            for _ in range(units):
                b = self.next_unit()
                self.TD[b].add(1)
                self.TO[b].add(1)

    def skip_in_loop(self, jobs=0, units=0):
        for _ in range(jobs):
            s = self.next_job()
            self.JD[s].add(3)
            self.JO[s].add(3)
        for _ in range(units):
            b = self.next_unit()
            self.TD[b].add(1)
            self.TO[b].add(1)

    def wait_done(self):
        for t in self.JD + self.TD:
            t.wait(self.eng)

    def wait_all_out(self):
        for t in self.JO + self.TO:
            t.wait(self.eng)


def build(nc, A, out):
    ctx = ExitStack()
    with ctx:
        def sb(name, shape, dt=F32):
            return ctx.enter_context(nc.sbuf_tensor(name, shape, dt))

        names = ["job_done0", "job_done1", "job_out0", "job_out1", "unit_done0", "unit_done1", "unit_out0", "unit_out1",
                 "w_full0", "w_full1", "consts_in", "edges_in", "x_in", "small_in", "wu_in", "dve_chain", "tiles_hot",
                 "bounds_ready", "pair_hot0", "pair_hot1", "pair_used0", "pair_used1", "deg_ready", "deg_root", "scaled",
                 "c_ready", "c_saved", "c_back", "x_done", "x_saved", "x_back", "var_ready", "root_ready", "row_ready",
                 "affine_done", "g_ready", "q_staged", "v_staged", "norm_ready", "max_ready", "att_ready", "e_ready", "p_ready",
                 "alpha_ready", "h_staged", "lg_ready", "lg_exp", "gates_ready", "gates_saved", "gate_in", "z_ready",
                 "acc_ready", "rows_in", "out_tile", "out_stored"]
        S = {n: ctx.enter_context(nc.semaphore(n)) for n in names}
        Tally.passed = {e: ctx.enter_context(nc.semaphore(f"passed_{n}")) for e, n in (
            (mybir.EngineType.Activation, "act"), (mybir.EngineType.DVE, "dve"), (mybir.EngineType.PE, "pe"),
            (mybir.EngineType.Pool, "pool"))}

        X = sb("X", [P, TT * D])
        TC = sb("TC", [P, TT * D])
        F0 = sb("F0", [P, KD * N])
        F1 = sb("F1", [P, KD * N])
        R = sb("R", [P, TT * N])
        xt = X[0:TL, :].rearrange("p (t d) -> p t d", t=TT)
        t0 = TC[0:TL, :].rearrange("p (t d) -> p t d", t=TT)
        cnt = TC[:, :].bitcast(U16)[0:TL, 0:TT * N].rearrange("p (t n) -> p t n", t=TT)
        f0 = F0[:, :].rearrange("p (k n) -> p k n", k=KD)
        f1 = F1[:, :].rearrange("p (k n) -> p k n", k=KD)
        r10 = R[0:TL, :].rearrange("p (t n) -> p t n", t=TT)
        rk = R[:, 0:KD * N].rearrange("p (k n) -> p k n", k=KD)
        rz = R[:, 0:KE * N].rearrange("p (k n) -> p k n", k=KE)
        wadj = [f[0:TL, 0:5 * N].rearrange("p (t n) -> p t n", t=5) for f in (F0, F1)]
        c_all = TC[:, :].bitcast(U16)[0:TL, 0:TT * N]
        masks = R[:, KD * N:].bitcast(BF16)[:, 0:5 * N].rearrange("p (k n) -> p k n", k=5)
        free = KD * N + 5 * N // 2
        vst = R[0:TL, free:free + TT * P].rearrange("p (t d) -> p t d", t=TT)
        diag = [R[0:TL, free + TT * P + h * TL:free + TT * P + (h + 1) * TL] for h in range(2)]
        wsl = [sb(f"weights{s}", [P, KE * P]) for s in range(2)]
        ys = [sb(f"ystage{s}", [P, N]) for s in range(2)]
        hs = [sb(f"hstage{s}", [P, TT * P]) for s in range(2)]
        hst = [h[0:TL, :].rearrange("p (t d) -> p t d", t=TT) for h in hs]
        kst = sb("kstage", [P, N])
        cols = sb("cols", [P, NCOL])
        ident = sb("ident", [P, P])
        iota = sb("iota", [P, N], F16)
        wd = sb("wd", [P, KD, BOT])
        w3 = sb("w3", [P, 2, 4])
        wm2 = sb("wm2", [P, 3, 8])
        dif = kst[0:4, 0:2 * P].rearrange("p (k c) -> p k c", k=2)
        small = sb("small", [P, 800])
        used = [0]

        def piece(n):
            used[0] += n
            assert used[0] <= 800
            return small[:, used[0] - n:used[0]]

        stats, mv, var, rs = piece(12 * TT), piece(2 * TT), piece(TT), piece(TT)
        mvt = mv[0:TL, :].rearrange("p (t c) -> p t c", c=2)
        dinv, deg, g4, gbias = piece(TT), piece(TT), piece(4), piece(2)
        mm3, nb, rsum, rinv = piece(8), piece(2), piece(8), piece(2)
        ad, mneg, zs = piece(TT), piece(2), piece(4)
        qs = [[piece(TL) for _ in range(2)] for _ in range(2)]
        lg, pr, t8, oh = qs[0][0][:, 0:80], qs[0][1][:, 0:80], qs[1][0][:, 0:80], qs[1][1][:, 0:80]
        m10 = piece(40)
        ones = piece(16)

        jp = [ctx.enter_context(nc.psum_tensor(f"job_banks{s}", [P, 3, 512], F32)) for s in range(2)]
        up = [ctx.enter_context(nc.psum_tensor(f"unit_bank{b}", [P, 512], F32)) for b in range(2)]

        c_dram = nc.dram_tensor("c_dram", [TL, TT * N], U16, kind="Internal").ap()
        x_dram = nc.dram_tensor("x_dram", [TL, TT * D], F32, kind="Internal").ap()
        g_dram = nc.dram_tensor("g_dram", [EXPERTS, N], F32, kind="Internal").ap()

        def col(name, k=0, n=1, rows=P):
            at = COL[name] + k
            return cols[0:rows, bass.ds(at, n)]

        def tok(t, n=TL):
            return bass.ds(t * TL, n)

        src_i = ys[0][:, :].bitcast(I32)[0:TL, 0:ET]
        dst_i = ys[0][:, :].bitcast(I32)[0:TL, ET:2 * ET]
        ew = ys[0][0:TL, 2 * ET:3 * ET]
        srcf = ys[0][0:TL, 3 * ET:4 * ET]
        dstf = ys[0][0:TL, 4 * ET:5 * ET]
        wpart = [ys[0][0:TL, (5 + k) * ET:(6 + k) * ET] for k in range(2)]
        wthird = ys[1][0:TL, 0:ET]
        wb = ys[1][0:TL, ET:2 * ET].bitcast(BF16)[:, 0:ET]
        in_bucket = R[0:TL, 0:TT * ET]
        ge = ys[1][0:TL, 2 * ET:3 * ET]
        held_all, tmp_all = F1[0:1, 0:3 * ET], F1[0:1, 3 * ET:6 * ET]
        bf = hs[0][0:1, 0:64]
        bounds = hs[0][0:1, 64:128].bitcast(I32)
        hot_src = [hs[s][:, :].bitcast(BF16)[0:TL, 256:256 + N] for s in range(2)]
        hot_dst = [hs[s][:, :].bitcast(BF16)[0:TL, 1600:1600 + 4 * TL].rearrange("p (q d) -> p q d", q=4)
                   for s in range(2)]
        zrow = kst[0:1, 200:900].bitcast(BF16)
        tq = kst[0:1, 1000:1250]

        def view(bank, n, width, rows=TL):
            return bank[0:rows, :].rearrange("p (j c) -> p j c", j=4)[:, 0:n, 0:width]

        block = ctx.enter_context(nc.Block())

        @block.sync
        def _(sp):
            E = Side(sp, S)

            def load(src, kt):
                s = E.next_job()
                E.JD[s].wait(sp)
                E.W[s].inc(sp.dma_start(wsl[s][:, 0:kt * P], src), 16)
                E.JD[s].add(3)
                E.JO[s].add(3)

            def stream(name, first=0, n=None, units=0):
                jobs, kt = STREAMED[name]
                n = n or jobs
                looped = n // 2 * 2 if n >= 4 else 0
                if looped:
                    with E.loop(looped // 2, jobs=2, weights=2) as i:
                        load(A[name][bass.ds(i * 2 + first, 1)].rearrange("o p f -> p (o f)"), kt)
                        load(A[name][bass.ds(i * 2 + (first + 1), 1)].rearrange("o p f -> p (o f)"), kt)
                for j in range(first + looped, first + n):
                    load(A[name][j], kt)

            for dst, name in ((src_i, "src"), (dst_i, "dst"), (ew, "ew"), (iota[:, :], "iota"), (tq[:, 0:ET], "pairno")):
                sp.dma_start(dst, A[name]).then_inc(S["edges_in"], 16)
            sp.dma_start(ident[:, :], A["ident"]).then_inc(S["consts_in"], 16)
            sp.dma_start(cols[:, :], A["cols"]).then_inc(S["consts_in"], 16)
            sp.dma_start(xt, A["x"]).then_inc(S["x_in"], 16)
            for dst, name in ((wd[:, :, :], "wd"), (w3[:, :, :], "w3"), (wm2[:, :, :], "wm2")):
                sp.dma_start(dst, A[name]).then_inc(S["small_in"], 16)
            E.skip("matrices", "adapter")
            stream("w1")
            E.skip("pair", "pair")
            stream("w2")
            if BLOCKS > 1:
                for name in ("r_in", "r_o1", "r_o2"):
                    stream(name)
                E.skip("logits", "masks")
                stream("wqkv")
                E.skip("attention")
                for name in ("wo", "fc1", "fc2", "lra_down", "lra_up"):
                    stream(name)
            if BLOCKS > 2:
                for name in ("gat_w1", "gat_w2"):
                    stream(name)
                    E.skip("att", "agg0")
            if BLOCKS > 3:
                stream("m_w1")
                E.skip("gates")
                with E.loop(EXPERTS, jobs=14, weights=14) as e:
                    with E.loop(KE // 2, jobs=2, weights=2) as i:
                        for h in range(2):
                            load(A["down"][bass.ds(e * KE + i * 2 + h, 1)].rearrange("o p f -> p (o f)"), 6)
                    with E.loop(3, jobs=2, weights=2) as i:
                        for h in range(2):
                            load(A["up"][bass.ds(e * 6 + i * 2 + h, 1)].rearrange("o p f -> p (o f)"), KE)
                with sp.Fori(0, TT) as t:
                    sp.wait_ge(S["out_tile"], t + 1)
                    sp.dma_start(out[:, bass.ds(t, 1), :], xt[:, bass.ds(t, 1), :]).then_inc(S["out_stored"], 16)
                sp.wait_ge(S["out_stored"], 16 * TT)
            else:
                sp.wait_ge(S["x_done"], BLOCKS)
                sp.dma_start(out, xt).then_inc(S["out_stored"], 16)
                sp.wait_ge(S["out_stored"], 16)

        @block.tensor
        def _(pe):
            E = Side(pe, S)

            def job(lhs, kts, rhs, m=P, weights=True):
                s = E.next_job()
                if weights:
                    E.W[s].add(16)
                    E.W[s].wait(pe)
                E.JO[s].wait(pe)
                for c, (at, n) in enumerate(CH):
                    for k in range(kts):
                        mm = nc.tensor.matmul(jp[s][0:m, c, 0:n], lhs(s, k), rhs(k, at, n), start=(k == 0),
                                              stop=(k == kts - 1))
                    E.JD[s].inc(mm)
                E.JO[s].add(3)
                return s

            def unit(blocks):
                b = E.next_unit()
                E.TO[b].wait(pe)
                for o, x in blocks:
                    k = x.shape[0]
                    tr = nc.tensor.transpose(o(up[b]), x, ident[0:k, 0:k])
                E.TD[b].inc(tr)
                E.TO[b].add(1)

            def on(f):
                return lambda k, at, n: f[:, k, bass.ds(at, n)]

            def slot_w(s, k):
                return wsl[s][:, bass.ts(k, P)]

            def back(s):
                for g, n in GROUPS:
                    unit([(lambda bank, j=j: bank[0:TL, bass.ts(j, P)], ys[s][:, tok(g + j)]) for j in range(n)])

            def square(s):
                for g, n in GROUPS:
                    unit([(lambda bank, j=j: bank[0:TL, j * P:j * P + TL], ys[s][0:TL, tok(g + j)]) for j in range(n)])

            rows = Tally(S["row_ready"])

            def rows_to_features():
                with E.loop(TT // 2, units=4, extra=[(rows, 2)]):
                    for s in range(2):
                        rows.add(1)
                        rows.wait(pe)
                        for h in range(2):
                            unit([(lambda bank, j=j: bank[:, j * P:j * P + TL], ys[s][0:TL, bass.ts(3 * h + j, P)])
                                  for j in range(3)])
                E.wait_all_out()

            def jobs(n, kts, f):
                looped = n // 2 * 2 if n >= 4 else 0
                if looped:
                    with E.loop(looped // 2, jobs=2, weights=2):
                        for _ in range(2):
                            job(slot_w, kts, on(f))
                for _ in range(n - looped):
                    job(slot_w, kts, on(f))
                E.wait_all_out()

            def jobs_back(kts, f):
                with E.loop(3, jobs=2, weights=2, units=6):
                    for s in [job(slot_w, kts, on(f)) for _ in range(2)]:
                        E.JO[s].wait(pe)
                        back(s)
                E.wait_all_out()

            def agg():
                return job(lambda s, k: hst[s][:, k, :], TT, lambda k, at, n: r10[:, k, bass.ds(at, n)], weights=False)

            pe.wait_ge(S["consts_in"], 32)
            pe.wait_ge(S["tiles_hot"], 1)
            for g, n in BUCKETS:
                b = E.next_unit()
                E.TO[b].wait(pe)
                E.TD[b].inc(nc.tensor.matmul(up[b][0:1, 0:n * ET], ones[0:TL, 0:1], in_bucket[:, g * ET:(g + n) * ET],
                                             start=True, stop=True))
                E.TO[b].add(1)
            pe.wait_ge(S["bounds_ready"], 1)
            with E.loop(TT, jobs=2) as b:
                first = pe.value_load(bounds[0:1, bass.ds(b + 30, 1)], min_val=1, max_val=TT * EQ)
                end = pe.value_load(bounds[0:1, bass.ds(b + 40, 1)], min_val=2, max_val=TT * EQ + 1)
                for s in range(2):
                    E.JO[s].wait(pe)
                    for c, (at, n) in enumerate(CH):
                        nc.tensor.matmul(jp[s][0:TL, c, 0:n], zrow[:, 0:TL], zrow[:, 0:n], start=True, stop=False,
                                         skip_group_check=True)
                with pe.Fori(first, end) as turn:
                    for s in range(2):
                        pe.wait_ge(S[f"pair_hot{s}"], turn)
                        for k in range(4):
                            for c, (at, n) in enumerate(CH):
                                mm = nc.tensor.matmul(jp[min(k, 1)][0:TL, c, 0:n], hot_dst[s][:, k, :],
                                                      hot_src[s][:, bass.ds(at, n)], start=False, stop=False,
                                                      skip_group_check=True)
                        mm.then_inc(S[f"pair_used{s}"], 1)
                for s in range(2):
                    for c, (at, n) in enumerate(CH):
                        E.JD[s].inc(nc.tensor.matmul(jp[s][0:TL, c, 0:n], zrow[:, 0:TL], zrow[:, 0:n], start=False,
                                                     stop=True, skip_group_check=True))
                    E.JO[s].add(3)
            E.job += 2 * (TT - 1)
            scaled = Tally(S["scaled"])
            with E.loop(TT // 2, units=6, extra=[(scaled, 2)]):
                for s in range(2):
                    scaled.add(1)
                    scaled.wait(pe)
                    square(s)
            rows_to_features()
            pe.wait_ge(S["small_in"], 48)
            job(lambda s, k: wd[:, k, :], KD, on(f0), m=BOT, weights=False)
            E.wait_all_out()
            pe.wait_ge(S["wu_in"], 32)
            for m in range(KD):
                job(lambda s, k: hs[1][0:BOT, bass.ts(m, P)], 1, lambda k, at, n: hs[0][0:BOT, bass.ds(at, n)],
                    weights=False)
            E.wait_all_out()
            for _ in range(2):
                job(slot_w, KD, on(f1))
            for _ in range(2):
                for s in (E.slot(0), E.slot(1)):
                    E.JO[s].wait(pe)
                    back(s)
                E.wait_all_out()
                for _ in range(2):
                    agg()
            E.wait_all_out()
            jobs_back(2, f0)
            if BLOCKS > 1:
                rows_to_features()
                pe.wait_ge(S["affine_done"], 2)
                jobs(4, KD, f0)
                pe.wait_ge(S["g_ready"], 1)
                with E.loop(2, jobs=2, weights=2, units=2):
                    for _ in range(2):
                        s, b = E.slot(), E.next_unit()
                        E.W[s].add(16)
                        E.W[s].wait(pe)
                        E.TO[b].wait(pe)
                        for k in range(4):
                            mm = nc.tensor.matmul(up[b][:, 0:1], slot_w(s, 4 + k), g4[:, k:k + 1], start=(k == 0), stop=(k == 3))
                        E.TD[b].inc(mm)
                        E.TO[b].add(1)
                        job(slot_w, 4, on(rz), weights=False)
                E.wait_all_out()
                jobs(2, 4, f0)
                job(lambda s, k: w3[:, k, :], 2, on(rz), m=4, weights=False)
                E.wait_all_out()
                for k in range(2):
                    job(lambda s, _: dif[:, k, :], 1, lambda _, at, n: hs[0][0:4, bass.ds(at, n)], weights=False)
                with E.loop(6, jobs=2, weights=2):
                    for _ in range(2):
                        job(slot_w, KD, on(f1))
                jobs_back(KD, f1)
                sl = [E.slot(0), E.slot(1)]
                q_in, v_in, norm = Tally(S["q_staged"]), Tally(S["v_staged"]), Tally(S["norm_ready"])

                def scores(h, ts, c, hp):
                    s = sl[h]
                    if c == 0:
                        E.JO[s].wait(pe)
                        E.JO[s].add(3)
                    at, n = CH[c]
                    E.JD[s].inc(nc.tensor.matmul(jp[s][0:TL, c, 0:n], qs[ts][h], rk[:, bass.ds(hp, 1), bass.ds(at, n)],
                                                 start=True, stop=True))

                def two_tiles(hp, pair_ends=False, ends=False):
                    for u in range(4):
                        h, nts = u % 2, (u // 2 + 1) % 2
                        ahead = not (ends and u >= 2)
                        if ahead and h == 0:
                            q_in.add(2)
                            q_in.wait(pe)
                        norm.add(1)
                        norm.wait(pe)
                        for c, (g, n) in enumerate(GROUPS):
                            b = c % 2
                            E.TO[b].wait(pe)
                            for j in range(n):
                                mm = nc.tensor.matmul(up[b][0:TL, j * P:j * P + TL], ys[h][0:TL, tok(g + j)], diag[h],
                                                      start=True, stop=True)
                            E.TD[b].inc(mm)
                            E.TO[b].add(1)
                            if ahead:
                                scores(h, nts, c, hp + 1 if pair_ends and u >= 2 else hp)
                        E.TO[1].wait(pe)
                        E.TO[0].wait(pe)
                        v_in.wait(pe)
                        for k in range(TT):
                            mm = nc.tensor.matmul(up[1][:, 0:TL], vst[:, k, :], hst[h][:, k, 0:TL], start=(k == 0), stop=(k == TT - 1))
                        E.TD[1].inc(mm)
                        E.TO[1].add(1)

                def pair(hp, ends):
                    v_in.add(1)
                    with repeat(pe, 4, list(zip(tallies, [6, 6, 6, 6, 8, 8, 8, 8, 4, 0, 4]))):
                        two_tiles(hp)
                    two_tiles(hp, True, ends)

                tallies = [E.JD[0], E.JD[1], E.JO[0], E.JO[1], E.TD[0], E.TO[0], E.TD[1], E.TO[1], q_in, v_in, norm]
                E.wait_all_out()
                q_in.add(2)
                q_in.wait(pe)
                for h in range(2):
                    for c in range(3):
                        scores(h, 0, c, 0)
                with repeat(pe, HP - 1, list(zip(tallies, [30, 30, 30, 30, 40, 40, 40, 40, 20, 1, 20]))) as hp:
                    pair(hp, False)
                pair(HP - 1, True)
                E.wait_all_out()
                jobs_back(KD, f1)
                rows_to_features()
                pe.wait_ge(S["affine_done"], 3)
                jobs(3, KD, f0)
                jobs_back(3, f1)
                rows_to_features()
                jobs(6, KD, f0)
                jobs_back(KD, f1)
            if BLOCKS > 2:
                rows_to_features()
                staged, alpha = Tally(S["h_staged"]), Tally(S["alpha_ready"])
                for layer in range(2):
                    jobs(6, KD, f0)
                    pe.wait_ge(S["att_ready"], layer + 1)
                    job(lambda s, k: hs[0][:, bass.ts(k, P)], KD, on(f1), weights=False)
                    job(lambda s, k: col(f"ad{layer + 1}", k), KD, on(f1), m=1, weights=False)
                    E.wait_all_out()
                    unit([(lambda bank, t=t: bank[0:TL, t:t + 1], hs[1][0:1, tok(t)]) for t in range(TT)])
                    with E.loop(TT // 2, units=6, extra=[(alpha, 2)]):
                        for s in range(2):
                            alpha.add(1)
                            alpha.wait(pe)
                            square(s)
                    E.wait_all_out()
                    with E.loop(3, jobs=2, units=12 if layer else 6, extra=[(staged, 2)]):
                        for h in range(2):
                            staged.add(1)
                            staged.wait(pe)
                            back(E.slot(h))
                        E.TO[0].wait(pe)
                        E.TO[1].wait(pe)
                        done = [agg() for _ in range(2)]
                        if layer:
                            for s in done:
                                E.JO[s].wait(pe)
                                back(s)
                    E.wait_all_out()
            if BLOCKS > 3:
                rows_to_features()
                jobs(3, KD, f0)
                job(lambda s, k: wm2[:, k, :], 3, on(f1), m=8, weights=False)
                E.wait_all_out()
                unit([(lambda bank, t=t: bank[0:TL, t * 8:t * 8 + 8], ys[0][0:8, tok(t)]) for t in range(TT)])
                pe.wait_ge(S["gates_ready"], 1)
                for g, n in GROUPS:
                    unit([(lambda bank, j=j: bank[0:8, j * P:j * P + TL], pr[0:TL, (g + j) * 8:(g + j) * 8 + 8])
                          for j in range(n)])
                z_in = Tally(S["z_ready"])
                with E.loop(EXPERTS, jobs=14, weights=14, extra=[(z_in, KE)]):
                    with E.loop(KE // 2, jobs=2, weights=2):
                        for _ in range(2):
                            job(slot_w, KD, on(f0))
                    z_in.add(KE)
                    z_in.wait(pe, alone=True)
                    with E.loop(3, jobs=2, weights=2):
                        for _ in range(2):
                            job(slot_w, KE, on(rz))
                with E.loop(3, units=6, extra=[(staged, 2)]):
                    for s in range(2):
                        staged.add(1)
                        staged.wait(pe)
                        back(s)

        @block.scalar
        def _(act):
            E = Side(act, S)

            def take(write):
                s = E.next_job()
                for c, (at, n) in enumerate(CH):
                    E.wait_chunk(s)
                    E.JO[s].inc(write(s, jp[s][:, c, 0:n], at, n))

            def take_unit(write):
                b = E.next_unit()
                E.wait_unit(b)
                E.TO[b].inc(write(up[b]))
                return b

            def move(o, i, func=ACT.Copy, **kw):
                return nc.scalar.activation(o, i, func, **kw)

            def rows_out(f):
                with E.loop(TT // 2, units=4) as i:
                    for s in range(2):
                        for h in range(2):
                            take_unit(lambda bank: move(f[:, 3 * h:3 * h + 3, bass.ds(i * (2 * TL) + s * TL, TL)],
                                                        view(bank, 3, TL, P)))

            def squares_out():
                for s in range(2):
                    for g, n in GROUPS:
                        take_unit(lambda bank: move(r10[:, g:g + n, bass.ds(squares_out.i * (2 * TL) + s * TL, TL)],
                                                    view(bank, n, TL)))

            def root(k):
                act.wait_ge(S["var_ready"], k)
                nc.scalar.activation(var[0:TL, :], var[0:TL, :], ACT.Sqrt).then_inc(S["root_ready"], 1)

            def row(f, m, at, n):
                return f[:, m, bass.ds(at, n)] if isinstance(m, int) else f[:, bass.ds(m, 1), bass.ds(at, n)]

            def to_rows(f, n, func, name=None):
                def one(m):
                    kw = {"bias": col(name, m)} if name else {}
                    take(lambda s, bank, at, w: move(row(f, m, at, w), bank, func, **kw))
                looped = n // 2 * 2 if n >= 4 else 0
                if looped:
                    with E.loop(looped // 2, jobs=2) as i:
                        one(i * 2)
                        one(i * 2 + 1)
                for m in range(looped, n):
                    one(m)

            def staged(func, name, m):
                kw = {"bias": col(name, m)} if name else {}
                take(lambda s, bank, at, w: move(ys[s][:, bass.ds(at, w)], bank, func, **kw))

            def staged_pairs(name):
                with E.loop(3, jobs=2, units=6) as i:
                    for h in range(2):
                        staged(ACT.Identity if name else ACT.Copy, name, i * 2 + h)
                    E.skip_in_loop(units=6)

            act.wait_ge(S["consts_in"], 32)
            E.skip("counts")
            for half in range(2):
                w5 = wadj[half]
                with E.loop(5, jobs=2) as b:
                    take(lambda s, bank, at, n: move(cnt[:, bass.ds(b + 5 * half, 1), bass.ds(at, n)], bank[0:TL, :]))
                    take(lambda s, bank, at, n: move(w5[:, bass.ds(b, 1), bass.ds(at, n)], bank[0:TL, :]))
            act.wait_ge(S["deg_ready"], 1)
            nc.scalar.activation(dinv[0:TL, :], deg[0:TL, :], ACT.Sqrt).then_inc(S["deg_root"], 1)
            with E.loop(TT // 2, units=6) as i:
                squares_out.i = i
                squares_out()
            root(1)
            act.wait_ge(S["scaled"], TT)
            rows_out(f0)
            take(lambda s, bank, at, n: move(hs[0][0:BOT, bass.ds(at, n)], bank[0:BOT, :], ACT.Relu, bias=col("bd", rows=BOT)))
            E.skip_in_loop(jobs=6)
            for m in range(2):
                staged(ACT.Copy, None, m)
            E.skip("pair_back")
            for m in range(2):
                staged(ACT.Relu, "gb1", m)
            E.skip("pair_back")
            to_rows(f0, 2, ACT.Copy)
            staged_pairs("gb2")
            if BLOCKS > 1:
                root(2)
                root(3)
                rows_out(f0)
                act.wait_ge(S["affine_done"], 1)
                for k in range(KD):
                    a = move(f0[:, k, :], f0[:, k, :], ACT.Identity, bias=col("r_b", k), scale=col("r_g", k))
                a.then_inc(S["affine_done"], 1)
                to_rows(rz, 4, ACT.Gelu, "r_in_b")
                with E.loop(2, jobs=2, units=2) as i:
                    for h in range(2):
                        b = take_unit(lambda bank: move(gbias[:, h:h + 1], bank[:, 0:1], ACT.Identity, bias=col("r_o1_b", i * 2 + h)))
                        E.TO[b].wait(act)
                        take(lambda s, bank, at, n: move(f0[:, bass.ds(i * 2 + h, 1), bass.ds(at, n)], bank, ACT.Gelu,
                                                         bias=gbias[:, h:h + 1]))
                to_rows(rz, 2, ACT.Gelu, "r_o2_b")
                take(lambda s, bank, at, n: move(hs[0][0:4, bass.ds(at, n)], bank[0:4, :], ACT.Identity, bias=col("r_o3_b", rows=4)))
                E.skip("masks")
                to_rows(f0, 6, ACT.Identity, "bq")
                to_rows(rk, 6, ACT.Identity, "bk")
                staged_pairs("bv")
                sl = [E.slot(0), E.slot(1)]
                peak = Tally(S["max_ready"])

                def exps(h):
                    s = sl[h]
                    peak.add(1)
                    peak.wait(act)
                    E.JD[s].add(3)
                    E.JO[s].inc(nc.scalar.activation(
                        ys[h][0:TL, 0:2 * CH[0][1]].rearrange("p (c n) -> p c n", c=2), jp[s][0:TL, 0:2, 0:CH[0][1]], ACT.Exp,
                        bias=nb[0:TL, h:h + 1], scale=HD ** -0.5, accum_out=rsum[0:TL, 2 * h:2 * h + 1]))
                    at, n = CH[2]
                    E.JO[s].inc(nc.scalar.activation(
                        ys[h][0:TL, at:at + n], jp[s][0:TL, 2, 0:n], ACT.Exp,
                        bias=nb[0:TL, h:h + 1], scale=HD ** -0.5, accum_out=rsum[0:TL, 2 * h + 1:2 * h + 2]), 2)

                def two_tiles(ends=False):
                    g, n = GROUPS[1]
                    for u in range(4):
                        E.TD[1].add(1)
                        E.TD[1].wait(act, alone=True)
                        E.TO[1].inc(move(hst[u % 2][:, g:g + n, 0:TL], view(up[1], n, TL)))
                        E.TD[1].add(1)
                        E.TO[1].add(1)
                        if not (ends and u >= 2):
                            exps(u % 2)

                def pair(ends):
                    with repeat(act, 4, list(zip(tallies, [6, 6, 6, 6, 8, 8, 4]))):
                        two_tiles()
                    two_tiles(ends)

                tallies = [E.JD[0], E.JD[1], E.JO[0], E.JO[1], E.TD[1], E.TO[1], peak]
                exps(0)
                exps(1)
                with repeat(act, HP - 1, list(zip(tallies, [30, 30, 30, 30, 40, 40, 20]))):
                    pair(False)
                pair(True)
                E.TD[0].add(40 * HP)
                E.TO[0].add(40 * HP)
                E.skip("pairs3_back")
                root(4)
                rows_out(f0)
                to_rows(f1, 3, ACT.Gelu, "fc1_b")
                E.skip("pairs3_back")
                rows_out(f0)
                E.skip("pairs3")
                staged_pairs(None)
            if BLOCKS > 2:
                root(5)
                rows_out(f0)
                e_in, p_out = Tally(S["e_ready"]), Tally(S["p_ready"])
                for layer in range(2):
                    to_rows(f1, 6, ACT.Copy)
                    take(lambda s, bank, at, n: move(kst[:, bass.ds(at, n)], bank))
                    take(lambda s, bank, at, n: move(hs[1][0:1, bass.ds(at, n)], bank[0:1, :]))
                    E.skip_in_loop(units=1)
                    with E.loop(TT // 2, units=6, extra=[(e_in, 2), (p_out, 2)]) as i:
                        for s in range(2):
                            e_in.add(1)
                            e_in.wait(act)
                            p_out.inc(nc.scalar.activation(hs[s][0:TL, 0:N], hs[s][0:TL, 0:N], ACT.Exp, bias=mneg[0:TL, s:s + 1]))
                        squares_out.i = i
                        squares_out()
                    with E.loop(3, jobs=2, units=12 if layer else 6) as i:
                        E.skip_in_loop(units=6)
                        for h in range(2):
                            if layer:
                                staged(ACT.Identity, "gat_b2", i * 2 + h)
                            else:
                                take(lambda s, bank, at, n: move(f0[:, bass.ds(i * 2 + h, 1), bass.ds(at, n)], bank, ACT.Relu,
                                                                 bias=col("gat_b1", i * 2 + h)))
                        if layer:
                            E.skip_in_loop(units=6)
            if BLOCKS > 3:
                root(6)
                rows_out(f0)
                to_rows(f1, 3, ACT.Gelu, "m_b1")
                take(lambda s, bank, at, n: move(ys[0][0:8, bass.ds(at, n)], bank[0:8, :], ACT.Identity, bias=col("m_b2", rows=8)))
                E.skip_in_loop(units=1)
                act.wait_ge(S["lg_ready"], 1)
                nc.scalar.activation(lg[0:TL, :], lg[0:TL, :], ACT.Exp).then_inc(S["lg_exp"], 1)
                for g, n in GROUPS:
                    take_unit(lambda bank: move(ys[1][0:8, tok(g, n * TL)].rearrange("p (j c) -> p j c", j=n), view(bank, n, TL, 8)))
                with E.loop(EXPERTS, jobs=14) as e:
                    with E.loop(KE // 2, jobs=2) as i:
                        for h in range(2):
                            take(lambda s, bank, at, n: move(rz[:, bass.ds(i * 2 + h, 1), bass.ds(at, n)], bank, ACT.Gelu,
                                                             bias=col("down_b", e * KE + i * 2 + h)))
                    E.skip_in_loop(jobs=6)
                E.skip("back3")
                root(7)

        @block.vector
        def _(dve):
            E = Side(dve, S)
            V = nc.vector
            chain = Tally(S["dve_chain"])

            def then(instruction):
                chain.inc(instruction)
                chain.wait(dve)

            def take(write):
                s = E.next_job()
                for c, (at, n) in enumerate(CH):
                    E.wait_chunk(s)
                    E.JO[s].inc(write(s, jp[s][:, c, 0:n], at, n))
                return s

            def take_unit(write):
                b = E.next_unit()
                E.wait_unit(b)
                E.TO[b].inc(write(up[b]))
                return b

            rows = Tally(S["row_ready"])

            def stats_of(src, k):
                E.wait_all_out()
                st = stats[0:TL, :].rearrange("p (t h c) -> p t h c", t=TT, h=2)
                for t in range(TT):
                    for h in range(2):
                        i = V.bn_stats(st[:, t, h, :], src[:, t, h * 384:(h + 1) * 384])
                then(i)
                for t in range(TT):
                    i = V.bn_aggr(mvt[:, t, :], stats[0:TL, 12 * t:12 * t + 12])
                then(i)
                V.tensor_scalar(var[0:TL, :], mvt[:, :, 1], LN_EPS, None, ALU.add).then_inc(S["var_ready"], 1)
                dve.wait_ge(S["root_ready"], k)
                then(V.reciprocal(rs[0:TL, :], var[0:TL, :]))

            def normal(o, src, t):
                return V.tensor_scalar(o, src, mvt[:, t, 0:1], rs[0:TL, t:t + 1], ALU.subtract, ALU.mult)

            def stage_rows(src, norm=True, keep=None):
                E.wait_done()
                with E.loop(TT // 2, units=4, extra=[(rows, 2)]) as i:
                    for s in range(2):
                        t = i * 2 + s
                        E.TD[0].wait(dve, 1)
                        E.TD[1].wait(dve, 1)
                        x = src[:, bass.ds(t, 1), :]
                        o = ys[s][0:TL, 0:D]
                        if norm:
                            m, r = mvt[:, bass.ds(t, 1), 0], rs[0:TL, bass.ds(t, 1)]
                            if keep is not None:
                                V.tensor_scalar(keep[:, bass.ds(t, 1), :], x, m, r, ALU.subtract, ALU.mult)
                            rows.inc(V.tensor_scalar(o, x, m, r, ALU.subtract, ALU.mult))
                        else:
                            rows.inc(V.tensor_copy(o, x))
                        E.skip_in_loop(units=2)

            def add_back(x, pairs=3):
                with E.loop(pairs, jobs=2, units=6) as i:
                    E.skip_in_loop(jobs=2)
                    add_pair(x, i)

            def add_pair(x, i):
                for h in range(2):
                    for g, n in GROUPS:
                        xs = x[:, g:g + n, bass.ds(i * (2 * P) + h * P, P)]
                        take_unit(lambda bank: V.tensor_tensor(xs, xs, view(bank, n, P), ALU.add))

            for b in range(2):
                V.memset(gbias[:, b:b + 1], 0.0).then_inc(S[f"job_out{b}"], 3)
                V.memset(mneg[:, b:b + 1], 0.0).then_inc(S[f"unit_out{b}"], 1)
                V.memset(nb[:, b:b + 1], 0.0).then_inc(S[f"pair_used{b}"], 1)
            V.memset(zrow, 0.0)
            for ts in range(2):
                for h in range(2):
                    V.memset(qs[ts][h], 0.0)
            then(V.memset(ones[:, :], 1.0))
            dve.wait_ge(S["edges_in"], 80)
            V.tensor_copy(srcf, src_i)
            then(V.tensor_copy(dstf, dst_i))
            for b in range(TT):
                then(V.tensor_scalar(ge, dstf, float(b * TL), None, ALU.is_ge))
                i = V.scalar_tensor_tensor(in_bucket[:, b * ET:(b + 1) * ET], dstf, float((b + 1) * TL), ge, ALU.is_lt, ALU.mult)
                if b < TT - 1:
                    then(i)
            i.then_inc(S["tiles_hot"], 1)
            then(V.tensor_copy(wb, ew))
            then(V.tensor_copy(wpart[0], wb))
            then(V.tensor_tensor(wthird, ew, wpart[0], ALU.subtract))
            then(V.tensor_copy(wb, wthird))
            then(V.tensor_copy(wpart[1], wb))
            then(V.tensor_tensor(wthird, wthird, wpart[1], ALU.subtract))
            for g, n in BUCKETS:
                held = held_all[:, 0:n * ET].rearrange("p (b t) -> p b t", b=n)
                no = tq[:, 0:ET].rearrange("p (o t) -> p o t", o=1).to_broadcast([1, n, ET])
                b = take_unit(lambda bank: V.tensor_scalar(held_all[:, 0:n * ET], bank[0:1, 0:n * ET], 0.0, None, ALU.is_gt))
                E.TO[b].wait(dve)
                tmp = tmp_all[:, 0:n * ET].rearrange("p (b t) -> p b t", b=n)
                then(V.scalar_tensor_tensor(tmp, no, 1.0, held, ALU.add, ALU.mult))
                then(V.tensor_reduce(bf[:, 10 + g:10 + g + n], tmp, AX.X, ALU.max))
                then(V.scalar_tensor_tensor(tmp, no, -1000.0, held, ALU.add, ALU.mult))
                then(V.tensor_reduce(bf[:, g:g + n], tmp, AX.X, ALU.min))
            lo_f, hi_f, n_f, cum = bf[:, 0:10], bf[:, 10:20], bf[:, 30:40], bf[:, 40:50]
            then(V.tensor_scalar(lo_f, lo_f, 1000.0, float(EQ - 1), ALU.add, ALU.min))
            then(V.scalar_tensor_tensor(hi_f, lo_f, 1.0, hi_f, ALU.add, ALU.max))
            then(V.tensor_tensor(n_f, hi_f, lo_f, ALU.subtract))
            then(V.tensor_tensor_scan(cum, ones[0:1, 0:10], n_f, 0.0, ALU.mult, ALU.add))
            then(V.tensor_tensor(cum, cum, n_f, ALU.subtract))
            then(V.tensor_scalar(cum, cum, 1.0, None, ALU.add))
            then(V.scalar_tensor_tensor(bf[:, 20:30], lo_f, float(TT * EQ), cum, ALU.add, ALU.subtract))
            then(V.tensor_tensor(bf[:, 50:60], cum, n_f, ALU.add))
            then(V.tensor_copy(bounds[:, 20:30], bf[:, 20:30]))
            then(V.tensor_copy(bounds[:, 30:50], bf[:, 40:60]))
            V.memset(zs[:, 0:1], 0.0).then_inc(S["bounds_ready"], 1)
            with repeat(dve, TT, []) as b:
                first = dve.value_load(bounds[0:1, bass.ds(b + 30, 1)], min_val=1, max_val=TT * EQ)
                end = dve.value_load(bounds[0:1, bass.ds(b + 40, 1)], min_val=2, max_val=TT * EQ + 1)
                shift = dve.value_load(bounds[0:1, bass.ds(b + 20, 1)], min_val=0, max_val=TT * EQ + EQ)
                with dve.Fori(first, end) as turn:
                    pair = nc.s_assert_within(turn + shift - TT * EQ, 0, EQ - 1, skip_runtime_bounds_check_because=
                                              "a bucket's turns run over its range of pairs, within 0 to EQ - 1")
                    for s in range(2):
                        e = bass.ds(pair * 2 + s, 1)
                        dve.wait_ge(S[f"pair_used{s}"], turn)
                        V.tensor_scalar(hot_src[s], iota[0:TL, :], srcf[:, e], None, ALU.is_equal)
                        here = iota[0:TL, bass.ds(b * TL, TL)]
                        V.tensor_scalar(hot_dst[s][:, 0, :], here, dstf[:, e], None, ALU.is_equal)
                        for k, w in enumerate((wpart[0], wpart[1], wthird)):
                            i = V.tensor_scalar(hot_dst[s][:, 1 + k, :], here, dstf[:, e], w[:, e], ALU.is_equal, ALU.mult)
                        i.then_inc(S[f"pair_hot{s}"], 1)
            E.skip("matrices")
            E.wait_all_out()
            id_t = ident[0:TL, 0:TL]
            for t in range(TT):
                dg = cnt[:, t, tok(t)]
                i = V.tensor_tensor(dg, dg, id_t, ALU.add)
            i.then_inc(S["c_ready"], 1)
            for t in range(TT):
                dg = wadj[t // 5][:, t % 5, tok(t)]
                i = V.tensor_tensor(dg, dg, id_t, ALU.add)
            then(i)
            for half in range(2):
                i = V.tensor_reduce(deg[0:TL, 5 * half:5 * half + 5], wadj[half], AX.X, ALU.add)
            i.then_inc(S["deg_ready"], 1)
            dve.wait_ge(S["deg_root"], 1)
            then(V.reciprocal(dinv[0:TL, :], dinv[0:TL, :]))
            scaled = Tally(S["scaled"])
            E.wait_done()
            for t in range(TT):
                s = t % 2
                if t >= 2:
                    for b in range(2):
                        E.TD[b].wait(dve)
                scaled.inc(V.tensor_scalar(ys[s][0:TL, :], wadj[t // 5][:, t % 5, :], dinv[0:TL, t:t + 1], None, ALU.mult))
                if t >= 1:
                    E.skip_in_loop(units=3)
            E.skip_in_loop(units=3)
            dve.wait_ge(S["x_in"], 16)
            stats_of(xt, 1)
            stage_rows(xt)
            E.skip_in_loop(jobs=1)
            for m in range(KD):
                take(lambda s, bank, at, n: V.scalar_tensor_tensor(f1[:, m, bass.ds(at, n)], bank, col("bu", m),
                                                                   f0[:, m, bass.ds(at, n)], ALU.add, ALU.add))

            def features_staged(s, scale=None):
                for g, n in GROUPS:
                    if scale is None:
                        take_unit(lambda bank: V.tensor_copy(hst[s][:, g:g + n, :], view(bank, n, P)))
                    else:
                        sc = scale[0:TL, g:g + n].rearrange("p (t o) -> p t o", o=1).to_broadcast([TL, n, P])
                        take_unit(lambda bank: V.tensor_tensor(hst[s][:, g:g + n, :], view(bank, n, P), sc, ALU.mult))

            E.skip("pair")
            for _ in range(2):
                for s in (E.slot(0), E.slot(1)):
                    features_staged(s, dinv)
                E.skip("pair")
            add_back(xt)
            E.wait_all_out()
            V.memset(zs[:, 0:1], 0.0).then_inc(S["x_done"], 1)
            if BLOCKS > 1:
                stats_of(xt, 2)
                dve.wait_ge(S["c_saved"], 16)
                for t in range(TT):
                    i = normal(t0[:, t, :], xt[:, t, :], t)
                then(i)
                stats_of(t0, 3)
                stage_rows(t0)
                E.wait_all_out()
                for k in range(KD):
                    i = V.tensor_scalar(f1[:, k, :], f0[:, k, :], col("l1_g", k), col("l1_b", k), ALU.mult, ALU.add)
                i.then_inc(S["affine_done"], 1)
                E.skip("r_in")
                E.wait_all_out()
                then(V.tensor_reduce(g4, rz[:, 0:4, 1:N], AX.X, ALU.add))
                V.tensor_scalar(g4, g4, 1.0 / (N - 1), None, ALU.mult).then_inc(S["g_ready"], 1)
                E.skip("r_o1", "r_o2", "logits")
                for k in range(2):
                    take(lambda s, bank, at, n: V.tensor_scalar(masks[:, k, bass.ds(at, n)], bank, 0.0, None, ALU.is_gt))
                E.wait_all_out()
                then(V.memset(masks[:, 0:2, 0:1], 1.0))
                then(V.tensor_scalar(masks[:, 2, :], masks[:, 0, :], -1.0, 1.0, ALU.mult, ALU.add))
                V.tensor_scalar(masks[:, 4, :], masks[:, 1, :], -1.0, 1.0, ALU.mult, ALU.add)
                then(V.tensor_tensor(masks[:, 3, :], masks[:, 2, :], masks[:, 1, :], ALU.mult))
                then(V.tensor_tensor(masks[:, 2, :], masks[:, 2, :], masks[:, 4, :], ALU.mult))
                then(V.tensor_tensor(masks[:, 4, :], masks[:, 4, :], masks[:, 0, :], ALU.mult))
                E.skip("qk")
                dve.wait_ge(S["x_saved"], 16)
                with E.loop(3, jobs=2, units=6) as i:
                    E.skip_in_loop(jobs=2)
                    for h in range(2):
                        for g, n in GROUPS:
                            take_unit(lambda bank: V.tensor_copy(xt[:, g:g + n, bass.ds(i * (2 * P) + h * P, P)], view(bank, n, P)))
                sl = [E.slot(0), E.slot(1)]
                peak, norm, v_out = Tally(S["max_ready"]), Tally(S["norm_ready"]), Tally(S["v_staged"])
                n0 = CH[0][1]

                def maximum(h):
                    s = sl[h]
                    E.JD[s].add(2)
                    E.JD[s].wait(dve)
                    V.tensor_reduce(mm3[0:TL, 2 * h:2 * h + 1], jp[s][0:TL, 0:2, 0:n0], AX.XY, ALU.max)
                    E.JD[s].add(1)
                    E.JD[s].wait(dve)
                    then(V.tensor_reduce(mm3[0:TL, 2 * h + 1:2 * h + 2], jp[s][0:TL, 2, 0:CH[2][1]], AX.X, ALU.max))
                    peak.inc(V.tensor_scalar(nb[0:TL, h:h + 1], mm3[0:TL, 2 * h:2 * h + 1], mm3[0:TL, 2 * h + 1:2 * h + 2],
                                             -(HD ** -0.5), ALU.max, ALU.mult))
                    E.JO[s].add(3)

                def scale(h):
                    E.JO[sl[h]].wait(dve)
                    then(V.tensor_tensor(rinv[0:TL, h:h + 1], rsum[0:TL, 2 * h:2 * h + 1], rsum[0:TL, 2 * h + 1:2 * h + 2], ALU.add))
                    then(V.reciprocal(rinv[0:TL, h:h + 1], rinv[0:TL, h:h + 1]))
                    norm.inc(V.tensor_scalar(diag[h], ident[0:TL, 0:TL], rinv[0:TL, h:h + 1], None, ALU.mult))

                def two_tiles(hp, i, ends=False):
                    for u in range(4):
                        ts, h = u // 2, u % 2
                        for c, (g, n) in enumerate(GROUPS):
                            E.TD[c % 2].add(1)
                            if c == 1:
                                E.TO[1].add(1)
                                continue
                            E.TD[0].wait(dve)
                            E.TO[0].inc(V.tensor_copy(hst[h][:, g:g + n, 0:TL], view(up[0], n, TL)))
                        if not (ends and u == 3):
                            scale((u + 1) % 2)
                        if not (ends and u >= 2):
                            maximum(h)
                        E.TD[1].add(1)
                        E.TD[1].wait(dve)
                        mine = slice(h * HD, h * HD + HD)
                        E.TO[1].inc(V.tensor_copy(f1[mine, bass.ds(hp, 1), bass.ds(i * (2 * TL) + ts * TL, TL)], up[1][mine, 0:TL]))

                def pair(hp, ends):
                    v_out.inc(V.tensor_copy(vst, xt[:, :, bass.ds(hp * P, P)]))
                    with repeat(dve, 4, list(zip(tallies, [6, 6, 6, 6, 8, 8, 8, 8, 4, 4, 0, 12]))) as i:
                        two_tiles(hp, i)
                    two_tiles(hp, 4, ends)

                tallies = [E.JD[0], E.JD[1], E.JO[0], E.JO[1], E.TD[0], E.TO[0], E.TD[1], E.TO[1], peak, norm, v_out, chain]
                for t in E.TO:
                    t.wait(dve)
                maximum(0)
                maximum(1)
                scale(0)
                with repeat(dve, HP - 1, list(zip(tallies, [30, 30, 30, 30, 40, 40, 40, 40, 20, 20, 1, 60]))) as hp:
                    pair(hp, False)
                pair(HP - 1, True)

                def masked_back(name, mask):
                    with E.loop(3, jobs=2, units=6) as i:
                        for h in range(2):
                            take(lambda s, bank, at, n: V.scalar_tensor_tensor(
                                ys[s][:, bass.ds(at, n)], bank, col(name, i * 2 + h), masks[:, mask, bass.ds(at, n)],
                                ALU.add, ALU.mult))
                        add_pair(t0, i)

                masked_back("bo", 0)
                stats_of(t0, 4)
                stage_rows(t0)
                E.wait_all_out()
                for k in range(KD):
                    i = V.tensor_scalar(f0[:, k, :], f0[:, k, :], col("l2_g", k), col("l2_b", k), ALU.mult, ALU.add)
                i.then_inc(S["affine_done"], 1)
                E.skip("fc1")
                masked_back("fc2_b", 1)
                E.wait_all_out()
                stage_rows(t0, norm=False)
                with E.loop(3, jobs=2) as i:
                    for h in range(2):
                        take(lambda s, bank, at, n: V.tensor_tensor(f1[:, bass.ds(i * 2 + h, 1), bass.ds(at, n)], bank,
                                                                    masks[:, bass.ds(i + 2, 1), bass.ds(at, n)], ALU.mult))
                add_back(t0)
                E.wait_all_out()
                dve.wait_ge(S["x_back"], 16)
                V.tensor_tensor(X[0:TL, :], X[0:TL, :], TC[0:TL, :], ALU.add).then_inc(S["x_done"], 1)
                dve.wait_ge(S["x_done"], 2)
            if BLOCKS > 2:
                stats_of(xt, 5)
                stage_rows(xt)
                e_out, p_in, alpha = Tally(S["e_ready"]), Tally(S["p_ready"]), Tally(S["alpha_ready"])
                for layer in range(2):
                    E.wait_done()
                    V.tensor_copy(hs[0][:, 0:D].rearrange("p (k c) -> p k c", k=KD),
                                  col(f"as{layer + 1}", 0, KD).rearrange("p (k o) -> p k o", o=1).to_broadcast([P, KD, P])
                                  ).then_inc(S["att_ready"], 1)
                    E.skip("pairs3")
                    E.skip_in_loop(jobs=2)
                    b = take_unit(lambda bank: V.tensor_copy(ad[0:TL, :], bank[0:TL, 0:TT]))
                    E.wait_all_out()
                    E.wait_done()
                    if layer == 0:
                        dve.wait_ge(S["c_back"], 16)
                    with E.loop(TT // 2, units=6, extra=[(e_out, 2), (p_in, 2), (alpha, 2), (chain, 14)]) as i:
                        for s in range(2):
                            t = i * 2 + s
                            h, c = hs[s][0:TL, 0:N], cnt[:, bass.ds(t, 1), :]
                            then(V.tensor_scalar(h, c, 0.0, -BIG, ALU.is_equal, ALU.mult))
                            then(V.tensor_tensor(h, h, kst[0:TL, :], ALU.add))
                            then(V.tensor_scalar(h, h, ad[0:TL, bass.ds(t, 1)], None, ALU.add, ALU.max, accum_out=zs[0:TL, s:s + 1]))
                            then(V.scalar_tensor_tensor(h, h, 0.2, h, ALU.mult, ALU.max))
                            then(V.scalar_tensor_tensor(zs[0:TL, 2 + s:3 + s], zs[0:TL, s:s + 1], 0.2, zs[0:TL, s:s + 1], ALU.mult, ALU.max))
                            e_out.inc(V.tensor_scalar(mneg[0:TL, s:s + 1], zs[0:TL, 2 + s:3 + s], -1.0, None, ALU.mult))
                        for s in range(2):
                            t = i * 2 + s
                            p_in.add(1)
                            p_in.wait(dve, alone=True)
                            if s == 0:
                                E.TD[0].wait(dve, alone=True)
                                E.TD[1].wait(dve, alone=True)
                            then(V.scalar_tensor_tensor(ys[s][0:TL, :], hs[s][0:TL, 0:N], 1.0, cnt[:, bass.ds(t, 1), :],
                                                        ALU.mult, ALU.mult, accum_out=rinv[0:TL, s:s + 1]))
                            then(V.reciprocal(zs[0:TL, s:s + 1], rinv[0:TL, s:s + 1]))
                            alpha.inc(V.tensor_scalar(ys[s][0:TL, :], ys[s][0:TL, :], zs[0:TL, s:s + 1], None, ALU.mult))
                        E.skip_in_loop(units=6)
                    E.wait_all_out()
                    with E.loop(3, jobs=2, units=12 if layer else 6) as i:
                        for h in range(2):
                            features_staged(E.slot(h))
                        E.skip_in_loop(jobs=2)
                        if layer:
                            add_pair(xt, i)
                E.wait_all_out()
                V.memset(zs[:, 0:1], 0.0).then_inc(S["x_done"], 1)
            if BLOCKS > 3:
                stats_of(xt, 6)
                stage_rows(xt, keep=t0)
                E.skip("m_w1")
                E.skip_in_loop(jobs=1)
                b = take_unit(lambda bank: V.tensor_copy(lg[0:TL, :], bank[0:TL, 0:8 * TT]))
                E.TO[b].wait(dve)
                lg3, pr3, t3, oh3 = [x[0:TL, :].rearrange("p (t e) -> p t e", t=TT) for x in (lg, pr, t8, oh)]
                top = m10[0:TL, 0:TT]

                def wide(x):
                    return x.rearrange("p (t o) -> p t o", o=1).to_broadcast([TL, TT, EXPERTS])

                number = iota[0:TL, 0:EXPERTS].rearrange("p (o e) -> p o e", o=1).to_broadcast([TL, TT, EXPERTS])
                then(V.tensor_reduce(top, lg3, AX.X, ALU.max))
                V.tensor_tensor(lg3, lg3, wide(top), ALU.subtract).then_inc(S["lg_ready"], 1)
                dve.wait_ge(S["lg_exp"], 1)
                then(V.tensor_reduce(top, lg3, AX.X, ALU.add))
                then(V.reciprocal(m10[0:TL, 10:20], top))
                then(V.tensor_tensor(lg3, lg3, wide(m10[0:TL, 10:20]), ALU.mult))
                then(V.tensor_copy(pr3, lg3))
                for turn in range(2):
                    then(V.tensor_reduce(top, pr3, AX.X, ALU.max))
                    then(V.tensor_tensor(t3, pr3, wide(top), ALU.not_equal))
                    then(V.scalar_tensor_tensor(t3, t3, 100.0, number, ALU.mult, ALU.add))
                    then(V.tensor_reduce(m10[0:TL, 20:30], t3, AX.X, ALU.min))
                    then(V.tensor_tensor(t3, number, wide(m10[0:TL, 20:30]), ALU.is_equal))
                    if turn == 0:
                        then(V.tensor_copy(oh3, t3))
                        then(V.scalar_tensor_tensor(pr3, t3, -4.0, pr3, ALU.mult, ALU.add))
                    else:
                        then(V.tensor_tensor(oh3, oh3, t3, ALU.add))
                then(V.tensor_tensor(pr3, lg3, oh3, ALU.mult))
                then(V.tensor_reduce(top, pr3, AX.X, ALU.add))
                then(V.tensor_scalar(top, top, 1e-8, None, ALU.add))
                then(V.reciprocal(m10[0:TL, 10:20], top))
                V.tensor_tensor(pr3, pr3, wide(m10[0:TL, 10:20]), ALU.mult).then_inc(S["gates_ready"], 1)
                for t in E.JD:
                    t.wait(dve)
                then(V.memset(F1[:, :], 0.0))
                E.skip_in_loop(units=3)
                gate, z_out = Tally(S["gate_in"]), Tally(S["z_ready"])
                with E.loop(EXPERTS, jobs=14, extra=[(gate, 16), (z_out, KE)]):
                    gate.add(16)
                    gate.wait(dve, alone=True)
                    with E.loop(KE // 2, jobs=2, extra=[(z_out, 2)]) as i:
                        for h in range(2):
                            s = E.next_job()
                            E.JD[s].add(3)
                            E.JO[s].add(3)
                            E.JO[s].wait(dve)
                            zr = rz[:, bass.ds(i * 2 + h, 1), :]
                            z_out.inc(V.tensor_tensor(zr, zr, kst[:, :], ALU.mult))
                    with E.loop(3, jobs=2) as i:
                        for h in range(2):
                            def add(s, bank, at, n):
                                fr = f1[:, bass.ds(i * 2 + h, 1), bass.ds(at, n)]
                                return V.tensor_tensor(fr, fr, bank, ALU.add)
                            take(add)
                    for t in E.JO:
                        t.wait(dve, alone=True)
                V.memset(zs[:, 0:1], 0.0).then_inc(S["acc_ready"], 1)
                with E.loop(3, units=6) as i:
                    add_pair(t0, i)
                stats_of(t0, 7)
                dve.wait_ge(S["rows_in"], 32)
                for t in range(TT):
                    then(normal(t0[:, t, :], t0[:, t, :], t))
                    then(V.tensor_tensor(t0[:, t, :], t0[:, t, :], hs[0][0:TL, 0:D], ALU.mult))
                    then(V.tensor_tensor(xt[:, t, :], xt[:, t, :], t0[:, t, :], ALU.add))
                    V.tensor_tensor(xt[:, t, :], xt[:, t, :], hs[1][0:TL, 0:D], ALU.add).then_inc(S["out_tile"], 1)

        @block.gpsimd
        def _(pool):
            E = Side(pool, S)
            E.skip("counts", "matrices")
            for t in E.JD:
                t.wait(pool)
            pool.dma_start(hs[1][0:BOT, 0:D], A["wu"]).then_inc(S["wu_in"], 16)
            pool.dma_start(dif, A["dif"]).then_inc(S["wu_in"], 16)
            pool.wait_ge(S["c_ready"], 1)
            pool.dma_start(c_dram, c_all).then_inc(S["c_saved"], 16)
            E.skip("w_transpose", "rows", "adapter", "pair", "pair_back", "pair", "pair_back", "pair", "pairs3_back")
            if BLOCKS > 1:
                pool.wait_ge(S["x_done"], 1)
                pool.dma_start(x_dram, X[0:TL, :]).then_inc(S["x_saved"], 16)
                E.skip("rows", "r_in", "r_o1", "r_o2", "logits", "masks", "qk", "pairs3_back")
                E.wait_all_out()
                q_out = Tally(S["q_staged"])
                done = [Tally(S["job_done0"], E.JD[0].count - 3), Tally(S["job_done1"], E.JD[1].count - 3)]
                with repeat(pool, HP, [(q_out, 20), (done[0], 30), (done[1], 30)]) as hp:
                    with repeat(pool, TT // 2, [(q_out, 4), (done[0], 6), (done[1], 6)]) as i:
                        for ts in range(2):
                            for d in done:
                                d.wait(pool)
                                d.add(3)
                            for h in range(2):
                                mine = slice(h * HD, h * HD + HD)
                                q_out.inc(nc.gpsimd.tensor_copy(
                                    qs[ts][h][mine, :], f0[mine, bass.ds(hp, 1), bass.ds(i * (2 * TL) + ts * TL, TL)]))
                                q_out.wait(pool, alone=True)
                E.skip("attention")
                for t in E.TD:
                    t.wait(pool)
                pool.dma_start(X[0:TL, :], x_dram).then_inc(S["x_back"], 16)
                E.skip("pairs3_back", "rows", "fc1", "pairs3_back", "rows", "pairs3", "pairs3_back")
                pool.wait_ge(S["x_done"], 2)
                pool.wait_ge(S["c_saved"], 16)
                pool.dma_start(c_all, c_dram).then_inc(S["c_back"], 16)
            if BLOCKS > 2:
                staged = Tally(S["h_staged"])
                E.skip("rows")
                for layer in range(2):
                    E.skip("pairs3", "att", "alpha")
                    E.wait_all_out()
                    E.wait_done()
                    with E.loop(3, jobs=2, units=12 if layer else 6, extra=[(staged, 2)]) as i:
                        E.wait_done()
                        for h in range(2):
                            staged.inc(nc.gpsimd.tensor_copy(ys[E.slot(h)][:, :], f1[:, bass.ds(i * 2 + h, 1), :]))
                        E.skip_in_loop(jobs=2, units=12 if layer else 6)
            if BLOCKS > 3:
                E.wait_done()
                pool.dma_start(hs[0][0:TL, 0:D], A["gamma"].to_broadcast([TL, D])).then_inc(S["rows_in"], 16)
                pool.dma_start(hs[1][0:TL, 0:D], A["beta"].to_broadcast([TL, D])).then_inc(S["rows_in"], 16)
                E.skip("rows", "m_w1", "gates")
                for t in E.TO:
                    t.wait(pool)
                pool.dma_start(g_dram, ys[1][0:EXPERTS, :]).then_inc(S["gates_saved"], 16)
                pool.wait_ge(S["gates_saved"], 16)
                z_in = Tally(S["z_ready"])
                pool.dma_start(kst[:, :], g_dram[0:1, :].to_broadcast([P, N])).then_inc(S["gate_in"], 16)
                with repeat(pool, EXPERTS - 1, [(z_in, KE)]) as e:
                    z_in.add(KE)
                    z_in.wait(pool)
                    pool.dma_start(kst[:, :], g_dram[bass.ds(e + 1, 1), :].to_broadcast([P, N])).then_inc(S["gate_in"], 16)
                pool.wait_ge(S["acc_ready"], 1)
                E.skip("experts")
                done = [Tally(S["unit_done0"], E.TD[0].count), Tally(S["unit_done1"], E.TD[1].count)]
                with repeat(pool, 3, [(staged, 2), (done[0], 3), (done[1], 3)]) as i:
                    for d in done:
                        d.wait(pool)
                    for s in range(2):
                        staged.inc(nc.gpsimd.tensor_copy(ys[s][:, :], f1[:, bass.ds(i * 2 + s, 1), :]))
                    for d in done:
                        d.add(3)


def kernel(**inputs):
    import concourse.bacc as bacc
    from concourse.bass_utils import run_bass_kernel_spmd

    a = {k: np.ascontiguousarray(v) for k, v in inputs.items()}

    def tiles(w):
        k, m = w.shape
        return np.ascontiguousarray(w.reshape(k // P, P, m // P, P).transpose(2, 1, 0, 3).reshape(m // P, P, k))

    def narrow(w):
        return np.ascontiguousarray(w.reshape(-1, P, w.shape[1]).transpose(1, 0, 2))

    def edges(e):
        return np.ascontiguousarray(e.reshape(ET, TL).T)

    f, g, m = "L0_ffn_", "L0_gnn_", "L1_ffn_"
    vec = {"bd": a[g + "bd"], "bu": a[g + "bu"], "gb1": a[g + "b1"], "gb2": a[g + "b2"], "r_g": a[f + "r_ln_g"],
           "r_b": a[f + "r_ln_b"], "l1_g": a[f + "ln1_g"], "l1_b": a[f + "ln1_b"], "r_in_b": a[f + "r_in_b"],
           "r_o1_b": a[f + "r_o1_b"], "r_o2_b": a[f + "r_o2_b"], "r_o3_b": a[f + "r_o3_b"], "bq": a[f + "bq"],
           "bk": a[f + "bk"], "bv": a[f + "bv"], "bo": a[f + "bo"], "l2_g": a[f + "ln2_g"], "l2_b": a[f + "ln2_b"],
           "fc1_b": a[f + "fc1_b"], "fc2_b": a[f + "fc2_b"], "as1": a["L1_gnn_att_src1"], "ad1": a["L1_gnn_att_dst1"],
           "gat_b1": a["L1_gnn_b1"], "as2": a["L1_gnn_att_src2"], "ad2": a["L1_gnn_att_dst2"], "gat_b2": a["L1_gnn_b2"],
           "m_b1": a[m + "b1"], "m_b2": a[m + "b2"], "down_b": a[m + "down_b"].reshape(-1)}
    cols = np.zeros((P, NCOL), np.float32)
    for name, n in VECTORS:
        v = vec[name]
        if v.size < P:
            cols[:v.size, COL[name]] = v
        else:
            cols[:, COL[name]:COL[name] + n] = v.reshape(n, P).T
    dif = np.zeros((4, 2, P), np.float32)
    for k in range(2):
        dif[2 * k, k], dif[2 * k + 1, k] = -1.0, 1.0
    arrays = {
        "src": edges(a["src"]), "dst": edges(a["dst"]), "ew": edges(a["edge_weight"]),
        "iota": np.ascontiguousarray(np.broadcast_to(np.arange(N, dtype=np.float16), (P, N))),
        "pairno": (np.arange(ET) // 2).astype(np.float32).reshape(1, ET),
        "ident": np.eye(P, dtype=np.float32), "cols": cols, "dif": dif,
        "x": np.ascontiguousarray(a["x"].reshape(TT, TL, D).transpose(1, 0, 2)),
        "wd": narrow(a[g + "Wd"]), "w3": narrow(a[f + "r_o3_w"].T), "wm2": narrow(a[m + "w2"]), "wu": a[g + "Wu"],
        "w1": tiles(a[g + "W1"]), "w2": tiles(a[g + "W2"]), "r_in": tiles(a[f + "r_in_w"].T),
        "r_o1": tiles(a[f + "r_o1_w"].T), "r_o2": tiles(a[f + "r_o2_w"].T),
        "wqkv": np.concatenate([tiles(a[f + w].T) for w in ("wq", "wk", "wv")]), "wo": tiles(a[f + "wo"].T),
        "fc1": tiles(a[f + "fc1_w"].T), "fc2": tiles(a[f + "fc2_w"].T),
        "lra_down": tiles(a[f + "lra_down"].reshape(D, D).T),
        "lra_up": tiles(a[f + "lra_up"].transpose(0, 2, 1).reshape(D, D)),
        "gat_w1": tiles(a["L1_gnn_W1"]), "gat_w2": tiles(a["L1_gnn_W2"]), "m_w1": tiles(a[m + "w1"]),
        "down": np.concatenate([tiles(w) for w in a[m + "down_w"]]), "up": np.concatenate([tiles(w) for w in a[m + "up_w"]]),
        "gamma": a[m + "gamma"].reshape(1, D), "beta": a[m + "beta"].reshape(1, D),
    }
    nc = bacc.Bacc("TRN2", target_bir_lowering=False, num_devices=1)
    A = {k: nc.dram_tensor(f"in_{k}", v.shape, mybir.dt.from_np(v.dtype), kind="ExternalInput").ap() for k, v in arrays.items()}
    out = nc.dram_tensor("result", (TL, TT, D), F32, kind="ExternalOutput").ap()
    build(nc, A, out)
    r = run_bass_kernel_spmd(nc, [{f"in_{k}": v for k, v in arrays.items()}], core_ids=[0])
    return r.results[0]["result"].transpose(1, 0, 2).reshape(N, D)
```

```python
from contextlib import ExitStack, contextmanager

import numpy as np

import concourse.bass as bass
from concourse import mybir

F32 = mybir.dt.float32
BF16 = mybir.dt.bfloat16
F16 = mybir.dt.float16
U16 = mybir.dt.uint16
I32 = mybir.dt.int32
ACT = mybir.ActivationFunctionType
ALU = mybir.AluOpType
AX = mybir.AxisListType

P = 128
N = 1250
TT = 10
TL = N // TT
D = 768
KD = D // P
EDGES = 20000
ET = EDGES // TL
EQ = ET // 2
HEADS, HD = 12, 64
HP = HEADS // 2
BOT = 24
EXPERTS, DE = 8, 1024
KE = DE // P
CHOICES = 2
SLOTS = (CHOICES * N + EXPERTS * (P - 1)) // P + 1
CH = [(0, 417), (417, 417), (834, 416)]
GROUPS = [(0, 4), (4, 4), (8, 2)]
BIG = 1.0e30
LN_EPS = 1e-5
BUCKETS = [(0, 3), (3, 3), (6, 3), (9, 1)]
BLOCKS = 4

VECTORS = [("bd", 1), ("bu", 6), ("gb1", 2), ("gb2", 6), ("r_g", 6), ("r_b", 6), ("l1_g", 6), ("l1_b", 6),
           ("r_in_b", 4), ("r_o1_b", 4), ("r_o2_b", 2), ("r_o3_b", 1), ("bq", 6), ("bk", 6), ("bv", 6),
           ("bo", 6), ("l2_g", 6), ("l2_b", 6), ("fc1_b", 3), ("fc2_b", 6),
           ("as1", 6), ("ad1", 6), ("gat_b1", 6), ("as2", 6), ("ad2", 6), ("gat_b2", 6),
           ("m_b1", 3), ("m_b2", 1), ("down_b", EXPERTS * KE)]
COL, NCOL = {}, 0
for _name, _n in VECTORS:
    COL[_name] = NCOL
    NCOL += _n

STREAMED = {"w1": (2, 6), "w2": (6, 2), "r_in": (4, 6), "r_o1": (4, 8), "r_o2": (2, 4), "wqkv": (18, 6),
            "wo": (6, 6), "fc1": (3, 6), "fc2": (6, 3), "lra_down": (6, 6), "lra_up": (6, 6),
            "gat_w1": (6, 6), "gat_w2": (6, 6), "m_w1": (3, 6)}


class Tally:

    passed = {}

    def __init__(self, sem, start=0):
        self.sem, self.count, self.loops = sem, start, []

    def add(self, n=1):
        self.count += n

    def inc(self, instruction, n=1):
        instruction.then_inc(self.sem, n)
        self.count += n

    def value(self, back=0):
        v = self.count - back
        for i, per in self.loops:
            if per:
                v = i * per + v
        return v

    def wait(self, eng, back=0, alone=False):
        if self.count - back > 0:
            value = self.value(back)
            eng.wait_ge(self.sem, value)
            if alone and not isinstance(value, int):
                eng.sem_inc(self.passed[eng.engine], 1)
        else:
            assert not any(per for _, per in self.loops), "a wait below one in a loop"


@contextmanager
def repeat(eng, n, per):
    with eng.Fori(0, n) as i:
        was = [t.count for t, _ in per]
        for t, by in per:
            t.loops.append((i, by))
        yield i
        got = [t.count - w for (t, _), w in zip(per, was)]
        for t, by in per:
            t.loops.pop()
        assert got == [by for _, by in per], (got, [by for _, by in per])
    for t, by in per:
        t.count += by * (n - 1)


PLAN = {"counts": (0, 4), "matrices": (2 * TT, 0), "w_transpose": (0, 3 * TT), "rows": (0, 2 * TT),
        "adapter": (7, 0), "pair": (2, 0), "pair_back": (0, 6), "pairs3": (6, 0), "pairs3_back": (6, 18),
        "r_in": (4, 0), "r_o1": (4, 4), "r_o2": (2, 0), "logits": (1, 0), "masks": (2, 0), "qk": (12, 0),
        "fc1": (3, 0), "vectors": (0, 2), "att": (2, 1), "alpha": (0, 3 * TT), "agg0": (6, 18), "agg1": (6, 36),
        "m_w1": (3, 0), "gates": (1, 1)}


class Side:

    def __init__(self, eng, S):
        self.eng = eng
        self.JD = [Tally(S["job_done0"]), Tally(S["job_done1"])]
        self.JO = [Tally(S["job_out0"], 3), Tally(S["job_out1"], 3)]
        self.TD = [Tally(S["unit_done0"]), Tally(S["unit_done1"])]
        self.TO = [Tally(S["unit_out0"], 1), Tally(S["unit_out1"], 1)]
        self.W = [Tally(S["w_full0"]), Tally(S["w_full1"])]
        self.job = self.unit = 0

    @contextmanager
    def loop(self, n, jobs=0, units=0, weights=0, extra=()):
        assert jobs % 2 == 0 and units % 2 == 0 and weights % 2 == 0
        per = [(t, 3 * jobs // 2) for t in self.JD + self.JO] + [(t, units // 2) for t in self.TD + self.TO]
        per += [(t, 16 * weights // 2) for t in self.W] + list(extra)
        with repeat(self.eng, n, per) as i:
            yield i

    def next_job(self):
        self.job += 1
        return (self.job - 1) % 2

    def next_unit(self):
        self.unit += 1
        return (self.unit - 1) % 2

    def wait_chunk(self, s):
        self.JD[s].add(1)
        self.JD[s].wait(self.eng, alone=self.eng.engine == mybir.EngineType.Activation)

    def wait_unit(self, b):
        self.TD[b].add(1)
        self.TD[b].wait(self.eng, alone=self.eng.engine == mybir.EngineType.Activation)

    def slot(self, ahead=0):
        return (self.job + ahead) % 2

    def skip(self, *stages):
        for name in stages:
            if name == "attention":
                for t in self.JD + self.JO:
                    t.add(30 * HP)
                for t in self.TD + self.TO:
                    t.add(40 * HP)
                continue
            jobs, units = PLAN[name]
            for _ in range(jobs):
                s = self.next_job()
                self.JD[s].add(3)
                self.JO[s].add(3)
            for _ in range(units):
                b = self.next_unit()
                self.TD[b].add(1)
                self.TO[b].add(1)

    def skip_in_loop(self, jobs=0, units=0):
        for _ in range(jobs):
            s = self.next_job()
            self.JD[s].add(3)
            self.JO[s].add(3)
        for _ in range(units):
            b = self.next_unit()
            self.TD[b].add(1)
            self.TO[b].add(1)

    def wait_done(self):
        for t in self.JD + self.TD:
            t.wait(self.eng)

    def wait_all_out(self):
        for t in self.JO + self.TO:
            t.wait(self.eng)


def build(nc, A, out):
    ctx = ExitStack()
    with ctx:
        def sb(name, shape, dt=F32):
            return ctx.enter_context(nc.sbuf_tensor(name, shape, dt))

        names = ["job_done0", "job_done1", "job_out0", "job_out1", "unit_done0", "unit_done1", "unit_out0", "unit_out1",
                 "w_full0", "w_full1", "consts_in", "edges_in", "x_in", "small_in", "wu_in", "dve_chain", "tiles_hot",
                 "bounds_ready", "pair_hot0", "pair_hot1", "pair_used0", "pair_used1", "deg_ready", "deg_root", "scaled",
                 "c_ready", "c_saved", "c_back", "x_done", "x_saved", "x_back", "var_ready", "root_ready", "row_ready",
                 "affine_done", "g_ready", "wt_in", "q_staged", "v_staged", "norm_ready", "max_ready", "att_ready", "e_ready", "p_ready",
                 "alpha_ready", "h_staged", "lg_ready", "lg_exp", "chosen", "one_hot", "route_ready",
                 "stream_ready", "stream_saved", "expert_w0", "expert_w1", "expert_done", "x_gathered", "x_turned", "member_ready",
                 "xt_ready", "down_done0", "down_done1", "z_ready", "up_done0", "up_done1", "y_ready", "y_saved", "y_free", "y_filled", "y_gathered0", "y_gathered1", "y_gathered2", "y_gathered3",
                 "y_gathered4", "rows_in", "out_tile", "out_stored"]
        S = {n: ctx.enter_context(nc.semaphore(n)) for n in names}
        Tally.passed = {e: ctx.enter_context(nc.semaphore(f"passed_{n}")) for e, n in (
            (mybir.EngineType.Activation, "act"), (mybir.EngineType.DVE, "dve"), (mybir.EngineType.PE, "pe"),
            (mybir.EngineType.Pool, "pool"))}

        X = sb("X", [P, TT * D])
        TC = sb("TC", [P, TT * D])
        F0 = sb("F0", [P, KD * N])
        F1 = sb("F1", [P, KD * N])
        R = sb("R", [P, TT * N])
        xt = X[0:TL, :].rearrange("p (t d) -> p t d", t=TT)
        t0 = TC[0:TL, :].rearrange("p (t d) -> p t d", t=TT)
        cnt = TC[:, :].bitcast(U16)[0:TL, 0:TT * N].rearrange("p (t n) -> p t n", t=TT)
        f0 = F0[:, :].rearrange("p (k n) -> p k n", k=KD)
        f1 = F1[:, :].rearrange("p (k n) -> p k n", k=KD)
        r10 = R[0:TL, :].rearrange("p (t n) -> p t n", t=TT)
        rk = R[:, 0:KD * N].rearrange("p (k n) -> p k n", k=KD)
        rz = R[:, 0:KE * N].rearrange("p (k n) -> p k n", k=KE)
        wadj = [f[0:TL, 0:5 * N].rearrange("p (t n) -> p t n", t=5) for f in (F0, F1)]
        c_all = TC[:, :].bitcast(U16)[0:TL, 0:TT * N]
        wt = R[:, 0:2 * KD * D]
        masks = R[:, KD * N:].bitcast(BF16)[:, 0:5 * N].rearrange("p (k n) -> p k n", k=5)
        free = KD * N + 5 * N // 2
        vst = R[0:TL, free:free + TT * P].rearrange("p (t d) -> p t d", t=TT)
        diag = [R[0:TL, free + TT * P + h * TL:free + TT * P + (h + 1) * TL] for h in range(2)]
        wsl = [sb(f"weights{s}", [P, KE * P]) for s in range(2)]
        ys = [sb(f"ystage{s}", [P, N]) for s in range(2)]
        hs = [sb(f"hstage{s}", [P, TT * P]) for s in range(2)]
        hst = [h[0:TL, :].rearrange("p (t d) -> p t d", t=TT) for h in hs]
        kst = sb("kstage", [P, N])
        cols = sb("cols", [P, NCOL])
        ident = sb("ident", [P, P])
        iota = sb("iota", [P, N], F16)
        wd = sb("wd", [P, KD, BOT])
        w3 = sb("w3", [P, 2, 4])
        wm2 = sb("wm2", [P, 3, 8])
        dif = kst[0:4, 0:2 * P].rearrange("p (k c) -> p k c", k=2)
        small = sb("small", [P, 800])
        used = [0]

        def piece(n):
            used[0] += n
            assert used[0] <= 800
            return small[:, used[0] - n:used[0]]

        stats, mv, var, rs = piece(12 * TT), piece(2 * TT), piece(TT), piece(TT)
        mvt = mv[0:TL, :].rearrange("p (t c) -> p t c", c=2)
        dinv, deg, g4, gbias = piece(TT), piece(TT), piece(4), piece(2)
        mm3, nb, rsum, rinv = piece(8), piece(2), piece(8), piece(2)
        ad, mneg, zs = piece(TT), piece(2), piece(4)
        qs = [[piece(TL) for _ in range(2)] for _ in range(2)]
        lg, pr, t8, oh = qs[0][0][:, 0:80], qs[0][1][:, 0:80], qs[1][0][:, 0:80], qs[1][1][:, 0:80]
        att_v = qs[1][1][:, 80:80 + 4 * KD]
        m10 = piece(40)
        ones = piece(16)

        jp = [ctx.enter_context(nc.psum_tensor(f"job_banks{s}", [P, 3, 512], F32)) for s in range(2)]
        up = [ctx.enter_context(nc.psum_tensor(f"unit_bank{b}", [P, 512], F32)) for b in range(2)]

        c_dram = nc.dram_tensor("c_dram", [TL, TT * N], U16, kind="Internal").ap()
        x_dram = nc.dram_tensor("x_dram", [TL, TT * D], F32, kind="Internal").ap()
        stream_dram = nc.dram_tensor("stream_dram", [N, D], F32, kind="Internal").ap()
        y_dram = nc.dram_tensor("y_dram", [SLOTS * P, D], F32, kind="Internal").ap()

        w_down = [R[:, 0:KE * D], F0[:, 0:KE * D]]
        w_up = [R[:, KE * D:2 * KE * D], F1[:, 0:KE * D]]
        x_rows = wsl[1][:, 0:D]
        x_feat = kst[:, 0:KD * P]
        z_feat = wsl[0][:, 0:KE * P]
        y_rows = ys[0][:, 0:D]
        before = hs[0][0:TL, D:D + 2 * TL]
        token_no = hs[1][0:TL, D:D + TT]
        places = hs[1][0:TL, D + 16:D + 16 + CHOICES * TT].bitcast(I32)
        first_slot = hs[1][0:1, D + 40:D + 40 + EXPERTS + 2].bitcast(I32)
        members = hs[1][:, D + 64:D + 64 + SLOTS + 2].bitcast(I32)
        member = hs[1][:, D + 100:D + 101].bitcast(I32)
        hot_row = [f[0:TL, KE * D:KE * D + TT * P].rearrange("p (t c) -> p t c", t=TT) for f in (F0, F1)]
        hot_slot = ys[1][0:TL, 0:CHOICES * TT * (SLOTS + 2)].rearrange("p (i s) -> p i s", i=CHOICES * TT)
        y_got = [(R if i < 16 else F0)[0:TL, i % 16 * D:i % 16 * D + D] for i in range(CHOICES * TT)]

        def col(name, k=0, n=1, rows=P):
            at = COL[name] + k
            return cols[0:rows, bass.ds(at, n)]

        def att_pair(layer, k):
            at = COL[f"as{layer + 1}"] + k
            return cols[:, at:at + KD + 1:KD]

        def tok(t, n=TL):
            return bass.ds(t * TL, n)

        src_i = ys[0][:, :].bitcast(I32)[0:TL, 0:ET]
        dst_i = ys[0][:, :].bitcast(I32)[0:TL, ET:2 * ET]
        ew = ys[0][0:TL, 2 * ET:3 * ET]
        srcf = ys[0][0:TL, 3 * ET:4 * ET]
        dstf = ys[0][0:TL, 4 * ET:5 * ET]
        wpart = [ys[0][0:TL, (5 + k) * ET:(6 + k) * ET] for k in range(2)]
        wthird = ys[1][0:TL, 0:ET]
        wb = ys[1][0:TL, ET:2 * ET].bitcast(BF16)[:, 0:ET]
        in_bucket = R[0:TL, 0:TT * ET]
        ge = ys[1][0:TL, 2 * ET:3 * ET]
        held_all, tmp_all = F1[0:1, 0:3 * ET], F1[0:1, 3 * ET:6 * ET]
        bf = hs[0][0:1, 0:64]
        bounds = hs[0][0:1, 64:128].bitcast(I32)
        hot_src = [hs[s][:, :].bitcast(BF16)[0:TL, 256:256 + N] for s in range(2)]
        hot_dst = [hs[s][:, :].bitcast(BF16)[0:TL, 1600:1600 + 4 * TL].rearrange("p (q d) -> p q d", q=4)
                   for s in range(2)]
        zrow = kst[0:1, 200:900].bitcast(BF16)
        tq = kst[0:1, 1000:1250]

        def view(bank, n, width, rows=TL):
            return bank[0:rows, :].rearrange("p (j c) -> p j c", j=4)[:, 0:n, 0:width]

        block = ctx.enter_context(nc.Block())

        @block.sync
        def _(sp):
            E = Side(sp, S)

            weighted = [0, 0]

            def load(src, kt, back=None):
                s = E.next_job()
                if back is None:
                    E.JD[s].wait(sp)
                else:
                    E.JD[s].wait(sp, back=back[s])
                E.W[s].inc(sp.dma_start(wsl[s][:, 0:kt * P], src), 16)
                E.JD[s].add(3)
                E.JO[s].add(3)

            def stream(name, first=0, n=None):
                jobs, kt = STREAMED[name]
                n = n or jobs
                looped = (n - 2) // 2 * 2 if n >= 6 else 0
                back = [t.count - w for t, w in zip(E.JD, weighted)]
                for j in range(first, first + min(2, n)):
                    load(A[name][j], kt, back)
                if looped:
                    with E.loop(looped // 2, jobs=2, weights=2) as i:
                        load(A[name][bass.ds(i * 2 + (first + 2), 1)].rearrange("o p f -> p (o f)"), kt)
                        load(A[name][bass.ds(i * 2 + (first + 3), 1)].rearrange("o p f -> p (o f)"), kt)
                for j in range(first + 2 + looped, first + n):
                    load(A[name][j], kt)
                weighted[:] = [t.count for t in E.JD]

            for dst, name in ((src_i, "src"), (dst_i, "dst"), (ew, "ew"), (iota[:, :], "iota"), (tq[:, 0:ET], "pairno")):
                sp.dma_start(dst, A[name]).then_inc(S["edges_in"], 16)
            sp.dma_start(ident[:, :], A["ident"]).then_inc(S["consts_in"], 16)
            sp.dma_start(cols[:, :], A["cols"]).then_inc(S["consts_in"], 16)
            sp.dma_start(xt, A["x"]).then_inc(S["x_in"], 16)
            for dst, name in ((wd[:, :, :], "wd"), (w3[:, :, :], "w3"), (wm2[:, :, :], "wm2")):
                sp.dma_start(dst, A[name]).then_inc(S["small_in"], 16)
            E.skip("matrices", "adapter")
            stream("w1")
            E.skip("pair", "pair")
            stream("w2")
            if BLOCKS > 1:
                for name in ("r_in", "r_o1", "r_o2"):
                    stream(name)
                E.skip("logits", "masks")
                stream("wqkv")
                E.skip("attention")
                for name in ("wo", "fc1", "fc2", "lra_down", "lra_up"):
                    stream(name)
            if BLOCKS > 2:
                for name in ("gat_w1", "gat_w2"):
                    E.skip("att")
                    stream(name)
                    E.skip("agg0")
            if BLOCKS > 3:
                def expert_weights(h, dst_src):
                    for dst, src in dst_src:
                        sp.dma_start(dst, src).then_inc(S[f"expert_w{h}"], 16)

                def down(e):
                    return A["down"][bass.ds(e, 1)].rearrange("o p f -> p (o f)")

                def up_of(e):
                    return A["up"][bass.ds(e, 1)].rearrange("o p f -> p (o f)")

                stream("m_w1", 0, 2)
                for t in (Tally(S["job_done0"], E.JD[0].count - 3), Tally(S["job_done1"], E.JD[1].count - 3)):
                    t.wait(sp)
                expert_weights(0, [(w_down[0], A["down"][0]), (w_up[0], A["up"][0])])
                stream("m_w1", 2, 1)
                E.skip("gates")
                sp.wait_ge(S["route_ready"], 1)
                expert_weights(1, [(w_down[1], A["down"][1]), (w_up[1], A["up"][1])])
                sp.wait_ge(S["stream_saved"], 16)
                empty = sp.value_load(first_slot[0:1, EXPERTS + 1:EXPERTS + 2], min_val=1, max_val=SLOTS - 1)
                with sp.Fori(1, empty + 1) as k:
                    sp.dma_start(y_dram[bass.ds(SLOTS * P - k * P, P), :], stream_dram[0:P, :]).then_inc(S["y_filled"], 16)
                with sp.Fori(1, EXPERTS // 2) as i:
                    for h in range(2):
                        sp.wait_ge(S["expert_done"], i * 2 + (h - 1))
                        expert_weights(h, [(w_down[h], down(i * 2 + h)), (w_up[h], up_of(i * 2 + h))])
                with sp.Fori(0, TT) as t:
                    sp.wait_ge(S["out_tile"], t + 1)
                    sp.dma_start(out[:, bass.ds(t, 1), :], xt[:, bass.ds(t, 1), :]).then_inc(S["out_stored"], 16)
                sp.wait_ge(S["out_stored"], 16 * TT)
            else:
                sp.wait_ge(S["x_done"], BLOCKS)
                sp.dma_start(out, xt).then_inc(S["out_stored"], 16)
                sp.wait_ge(S["out_stored"], 16)

        @block.tensor
        def _(pe):
            E = Side(pe, S)

            def job(lhs, kts, rhs, m=P, weights=True):
                s = E.next_job()
                if weights:
                    E.W[s].add(16)
                    E.W[s].wait(pe)
                E.JO[s].wait(pe)
                for c, (at, n) in enumerate(CH):
                    for k in range(kts):
                        mm = nc.tensor.matmul(jp[s][0:m, c, 0:n], lhs(s, k), rhs(k, at, n), start=(k == 0),
                                              stop=(k == kts - 1))
                    E.JD[s].inc(mm)
                E.JO[s].add(3)
                return s

            def unit(blocks):
                b = E.next_unit()
                E.TO[b].wait(pe)
                for o, x in blocks:
                    k = x.shape[0]
                    tr = nc.tensor.transpose(o(up[b]), x, ident[0:k, 0:k])
                E.TD[b].inc(tr)
                E.TO[b].add(1)

            def on(f):
                return lambda k, at, n: f[:, k, bass.ds(at, n)]

            def slot_w(s, k):
                return wsl[s][:, bass.ts(k, P)]

            def back(s):
                for g, n in GROUPS:
                    unit([(lambda bank, j=j: bank[0:TL, bass.ts(j, P)], ys[s][:, tok(g + j)]) for j in range(n)])

            def square(s):
                for g, n in GROUPS:
                    unit([(lambda bank, j=j: bank[0:TL, j * P:j * P + TL], ys[s][0:TL, tok(g + j)]) for j in range(n)])

            rows = Tally(S["row_ready"])

            def rows_to_features():
                with E.loop(TT // 2, units=4, extra=[(rows, 2)]):
                    for s in range(2):
                        rows.add(1)
                        rows.wait(pe)
                        for h in range(2):
                            unit([(lambda bank, j=j: bank[:, j * P:j * P + TL], ys[s][0:TL, bass.ts(3 * h + j, P)])
                                  for j in range(3)])
                E.wait_all_out()

            def jobs(n, kts, f):
                looped = n // 2 * 2 if n >= 4 else 0
                if looped:
                    with E.loop(looped // 2, jobs=2, weights=2):
                        for _ in range(2):
                            job(slot_w, kts, on(f))
                for _ in range(n - looped):
                    job(slot_w, kts, on(f))
                E.wait_all_out()

            def jobs_back(kts, f):
                with E.loop(3, jobs=2, weights=2, units=6):
                    for s in [job(slot_w, kts, on(f)) for _ in range(2)]:
                        E.JO[s].wait(pe)
                        back(s)
                E.wait_all_out()

            def agg():
                return job(lambda s, k: hst[s][:, k, :], TT, lambda k, at, n: r10[:, k, bass.ds(at, n)], weights=False)

            pe.wait_ge(S["consts_in"], 32)
            pe.wait_ge(S["tiles_hot"], 1)
            for g, n in BUCKETS:
                b = E.next_unit()
                E.TO[b].wait(pe)
                E.TD[b].inc(nc.tensor.matmul(up[b][0:1, 0:n * ET], ones[0:TL, 0:1], in_bucket[:, g * ET:(g + n) * ET],
                                             start=True, stop=True))
                E.TO[b].add(1)
            pe.wait_ge(S["bounds_ready"], 1)
            with E.loop(TT, jobs=2) as b:
                first = pe.value_load(bounds[0:1, bass.ds(b + 30, 1)], min_val=1, max_val=TT * EQ)
                end = pe.value_load(bounds[0:1, bass.ds(b + 40, 1)], min_val=2, max_val=TT * EQ + 1)
                for s in range(2):
                    E.JO[s].wait(pe)
                    for c, (at, n) in enumerate(CH):
                        nc.tensor.matmul(jp[s][0:TL, c, 0:n], zrow[:, 0:TL], zrow[:, 0:n], start=True, stop=False,
                                         skip_group_check=True)
                with pe.Fori(first, end) as turn:
                    for s in range(2):
                        pe.wait_ge(S[f"pair_hot{s}"], turn)
                        for k in range(4):
                            for c, (at, n) in enumerate(CH):
                                mm = nc.tensor.matmul(jp[min(k, 1)][0:TL, c, 0:n], hot_dst[s][:, k, :],
                                                      hot_src[s][:, bass.ds(at, n)], start=False, stop=False,
                                                      skip_group_check=True)
                        mm.then_inc(S[f"pair_used{s}"], 1)
                for s in range(2):
                    for c, (at, n) in enumerate(CH):
                        E.JD[s].inc(nc.tensor.matmul(jp[s][0:TL, c, 0:n], zrow[:, 0:TL], zrow[:, 0:n], start=False,
                                                     stop=True, skip_group_check=True))
                    E.JO[s].add(3)
            E.job += 2 * (TT - 1)
            scaled = Tally(S["scaled"])
            with E.loop(TT // 2, units=6, extra=[(scaled, 2)]):
                for s in range(2):
                    scaled.add(1)
                    scaled.wait(pe)
                    square(s)
            rows_to_features()
            pe.wait_ge(S["small_in"], 48)
            job(lambda s, k: wd[:, k, :], KD, on(f0), m=BOT, weights=False)
            E.wait_all_out()
            pe.wait_ge(S["wu_in"], 32)
            for m in range(KD):
                job(lambda s, k: hs[1][0:BOT, bass.ts(m, P)], 1, lambda k, at, n: hs[0][0:BOT, bass.ds(at, n)],
                    weights=False)
            E.wait_all_out()
            for _ in range(2):
                job(slot_w, KD, on(f1))
            for _ in range(2):
                for s in (E.slot(0), E.slot(1)):
                    E.JO[s].wait(pe)
                    back(s)
                E.wait_all_out()
                for _ in range(2):
                    agg()
            E.wait_all_out()
            jobs_back(2, f0)
            if BLOCKS > 1:
                rows_to_features()
                pe.wait_ge(S["affine_done"], 2)
                jobs(4, KD, f0)
                pe.wait_ge(S["g_ready"], 1)
                with E.loop(2, jobs=2, weights=2, units=2):
                    for _ in range(2):
                        s, b = E.slot(), E.next_unit()
                        E.W[s].add(16)
                        E.W[s].wait(pe)
                        E.TO[b].wait(pe)
                        for k in range(4):
                            mm = nc.tensor.matmul(up[b][:, 0:1], slot_w(s, 4 + k), g4[:, k:k + 1], start=(k == 0), stop=(k == 3))
                        E.TD[b].inc(mm)
                        E.TO[b].add(1)
                        job(slot_w, 4, on(rz), weights=False)
                E.wait_all_out()
                jobs(2, 4, f0)
                job(lambda s, k: w3[:, k, :], 2, on(rz), m=4, weights=False)
                E.wait_all_out()
                for k in range(2):
                    job(lambda s, _: dif[:, k, :], 1, lambda _, at, n: hs[0][0:4, bass.ds(at, n)], weights=False)
                with E.loop(6, jobs=2, weights=2):
                    for _ in range(2):
                        job(slot_w, KD, on(f1))
                jobs_back(KD, f1)
                sl = [E.slot(0), E.slot(1)]
                q_in, v_in, norm = Tally(S["q_staged"]), Tally(S["v_staged"]), Tally(S["norm_ready"])

                def scores(h, ts, c, hp):
                    s = sl[h]
                    if c == 0:
                        E.JO[s].wait(pe)
                        E.JO[s].add(3)
                    at, n = CH[c]
                    E.JD[s].inc(nc.tensor.matmul(jp[s][0:TL, c, 0:n], qs[ts][h], rk[:, bass.ds(hp, 1), bass.ds(at, n)],
                                                 start=True, stop=True))

                def two_tiles(hp, pair_ends=False, ends=False):
                    for u in range(4):
                        h, nts = u % 2, (u // 2 + 1) % 2
                        ahead = not (ends and u >= 2)
                        if ahead and h == 0:
                            q_in.add(2)
                            q_in.wait(pe)
                        norm.add(1)
                        norm.wait(pe)
                        for c, (g, n) in enumerate(GROUPS):
                            b = c % 2
                            E.TO[b].wait(pe)
                            for j in range(n):
                                mm = nc.tensor.matmul(up[b][0:TL, j * P:j * P + TL], ys[h][0:TL, tok(g + j)], diag[h],
                                                      start=True, stop=True)
                            E.TD[b].inc(mm)
                            E.TO[b].add(1)
                            if ahead:
                                scores(h, nts, c, hp + 1 if pair_ends and u >= 2 else hp)
                        E.TO[1].wait(pe)
                        E.TO[0].wait(pe)
                        v_in.wait(pe)
                        for k in range(TT):
                            mm = nc.tensor.matmul(up[1][:, 0:TL], vst[:, k, :], hst[h][:, k, 0:TL], start=(k == 0), stop=(k == TT - 1))
                        E.TD[1].inc(mm)
                        E.TO[1].add(1)

                def pair(hp, ends):
                    v_in.add(1)
                    with repeat(pe, 4, list(zip(tallies, [6, 6, 6, 6, 8, 8, 8, 8, 4, 0, 4]))):
                        two_tiles(hp)
                    two_tiles(hp, True, ends)

                tallies = [E.JD[0], E.JD[1], E.JO[0], E.JO[1], E.TD[0], E.TO[0], E.TD[1], E.TO[1], q_in, v_in, norm]
                E.wait_all_out()
                q_in.add(2)
                q_in.wait(pe)
                for h in range(2):
                    for c in range(3):
                        scores(h, 0, c, 0)
                with repeat(pe, HP - 1, list(zip(tallies, [30, 30, 30, 30, 40, 40, 40, 40, 20, 1, 20]))) as hp:
                    pair(hp, False)
                pair(HP - 1, True)
                E.wait_all_out()
                jobs_back(KD, f1)
                rows_to_features()
                pe.wait_ge(S["affine_done"], 3)
                jobs(3, KD, f0)
                jobs_back(3, f1)
                rows_to_features()
                jobs(6, KD, f0)
                jobs_back(KD, f1)
            if BLOCKS > 2:
                pe.wait_ge(S["wt_in"], 16)
                for layer in range(2):
                    b = E.next_unit()
                    E.TO[b].wait(pe)
                    for m in range(KD):
                        for k in range(KD):
                            mm = nc.tensor.matmul(up[b][:, 2 * m:2 * m + 2], wt[:, (layer * KD + k) * D + m * P:(layer * KD + k) * D + (m + 1) * P],
                                                  att_pair(layer, k), start=(k == 0), stop=(k == KD - 1))
                    E.TD[b].inc(mm)
                    E.TO[b].add(1)
                rows_to_features()
                staged, alpha = Tally(S["h_staged"]), Tally(S["alpha_ready"])
                for layer in range(2):
                    pe.wait_ge(S["att_ready"], layer + 1)
                    job(lambda s, k: hs[0][:, bass.ts(k, P)], KD, on(f0), weights=False)
                    job(lambda s, k: att_v[:, 2 * (layer * KD + k) + 1:2 * (layer * KD + k) + 2], KD, on(f0), m=1, weights=False)
                    E.wait_all_out()
                    unit([(lambda bank, t=t: bank[0:TL, t:t + 1], hs[1][0:1, tok(t)]) for t in range(TT)])

                    def job_and_tiles():
                        job(slot_w, KD, on(f0))
                        for s in range(2):
                            alpha.add(1)
                            alpha.wait(pe)
                            square(s)

                    with E.loop(2, jobs=2, weights=2, units=12, extra=[(alpha, 4)]):
                        job_and_tiles()
                        job_and_tiles()
                    job_and_tiles()
                    job(slot_w, KD, on(f0))
                    E.wait_all_out()
                    with E.loop(3, jobs=2, units=12 if layer else 6, extra=[(staged, 2)]):
                        for h in range(2):
                            staged.add(1)
                            staged.wait(pe)
                            back(E.slot(h))
                        E.TO[0].wait(pe)
                        E.TO[1].wait(pe)
                        done = [agg() for _ in range(2)]
                        if layer:
                            for s in done:
                                E.JO[s].wait(pe)
                                back(s)
                    E.wait_all_out()
            if BLOCKS > 3:
                rows_to_features()
                jobs(3, KD, f0)
                job(lambda s, k: wm2[:, k, :], 3, on(f1), m=8, weights=False)
                E.wait_all_out()
                unit([(lambda bank, t=t: bank[0:TL, t * 8:t * 8 + 8], ys[0][0:8, tok(t)]) for t in range(TT)])
                pe.wait_ge(S["chosen"], 1)
                pe.wait_ge(S["rows_in"], 64)
                E.TO[0].wait(pe)
                E.TO[1].wait(pe)
                nc.tensor.matmul(up[1][0:TL, 0:80], before[:, 0:TL], oh[0:TL, :], start=True, stop=True)
                nc.tensor.matmul(up[1][0:TL, 80:160], before[:, TL:2 * TL], oh[0:TL, :], start=True, stop=True).then_inc(
                    S["chosen"], 1)
                pe.wait_ge(S["one_hot"], 1)
                for i in range(CHOICES * TT):
                    mm = nc.tensor.matmul(up[0][:, 0:SLOTS + 2], hot_row[i // TT][:, i % TT, :], hot_slot[:, i, :],
                                          start=(i == 0), stop=(i == CHOICES * TT - 1))
                mm.then_inc(S["one_hot"], 1)

                def turn_rows():
                    for k in range(KD):
                        o = jp[0][:, 2, k * P:(k + 1) * P] if k < 4 else jp[1][:, 2, (k - 4) * P:(k - 3) * P]
                        tr = nc.tensor.transpose(o, x_rows[:, bass.ts(k, P)], ident[:, :])
                    tr.then_inc(S["x_turned"], 1)

                pe.wait_ge(S["x_gathered"], 16)
                turn_rows()
                pe.wait_ge(S["route_ready"], 1)
                with pe.Fori(0, EXPERTS // 2) as i:
                    for h in range(2):
                        first = pe.value_load(first_slot[0:1, bass.ds(i * 2 + h, 1)], min_val=1, max_val=SLOTS - 1)
                        end = pe.value_load(first_slot[0:1, bass.ds(i * 2 + h + 1, 1)], min_val=2, max_val=SLOTS)
                        pe.wait_ge(S[f"expert_w{h}"], i * 32 + 32)
                        pe.sem_inc(Tally.passed[pe.engine], 1)
                        with pe.Fori(first, end) as s:
                            pe.wait_ge(S["xt_ready"], s)
                            for j in range(KE):
                                for k in range(KD):
                                    mm = nc.tensor.matmul(jp[0][:, j // 4, j % 4 * P:(j % 4 + 1) * P],
                                                          w_down[h][:, bass.ts(j * KD + k, P)], x_feat[:, bass.ts(k, P)],
                                                          start=(k == 0), stop=(k == KD - 1))
                                if j % 4 == 3:
                                    mm.then_inc(S[f"down_done{j // 4}"], 1)
                            pe.wait_ge(S["x_gathered"], s * 16 + 16)
                            turn_rows()
                            pe.wait_ge(S["z_ready"], s)
                            pe.wait_ge(S["y_ready"], s)
                            for c in range(2):
                                for k in range(KE):
                                    mm = nc.tensor.matmul(jp[1][:, c, 0:D // 2], z_feat[:, bass.ts(k, P)],
                                                          w_up[h][:, bass.ds(k * D + c * (D // 2), D // 2)],
                                                          start=(k == 0), stop=(k == KE - 1))
                                mm.then_inc(S[f"up_done{c}"], 1)
                        pe.wait_ge(S["up_done1"], end)
                        pe.sem_inc(S["expert_done"], 1)

        @block.scalar
        def _(act):
            E = Side(act, S)

            def take(write):
                s = E.next_job()
                for c, (at, n) in enumerate(CH):
                    E.wait_chunk(s)
                    E.JO[s].inc(write(s, jp[s][:, c, 0:n], at, n))

            def take_unit(write):
                b = E.next_unit()
                E.wait_unit(b)
                E.TO[b].inc(write(up[b]))
                return b

            def move(o, i, func=ACT.Copy, **kw):
                return nc.scalar.activation(o, i, func, **kw)

            def rows_out(f):
                with E.loop(TT // 2, units=4) as i:
                    for s in range(2):
                        for h in range(2):
                            take_unit(lambda bank: move(f[:, 3 * h:3 * h + 3, bass.ds(i * (2 * TL) + s * TL, TL)],
                                                        view(bank, 3, TL, P)))

            def squares_out():
                for s in range(2):
                    for g, n in GROUPS:
                        take_unit(lambda bank: move(r10[:, g:g + n, bass.ds(squares_out.i * (2 * TL) + s * TL, TL)],
                                                    view(bank, n, TL)))

            def root(k):
                act.wait_ge(S["var_ready"], k)
                nc.scalar.activation(var[0:TL, :], var[0:TL, :], ACT.Sqrt).then_inc(S["root_ready"], 1)

            def row(f, m, at, n):
                return f[:, m, bass.ds(at, n)] if isinstance(m, int) else f[:, bass.ds(m, 1), bass.ds(at, n)]

            def to_rows(f, n, func, name=None):
                def one(m):
                    kw = {"bias": col(name, m)} if name else {}
                    take(lambda s, bank, at, w: move(row(f, m, at, w), bank, func, **kw))
                looped = n // 2 * 2 if n >= 4 else 0
                if looped:
                    with E.loop(looped // 2, jobs=2) as i:
                        one(i * 2)
                        one(i * 2 + 1)
                for m in range(looped, n):
                    one(m)

            def staged(func, name, m):
                kw = {"bias": col(name, m)} if name else {}
                take(lambda s, bank, at, w: move(ys[s][:, bass.ds(at, w)], bank, func, **kw))

            def staged_pairs(name):
                with E.loop(3, jobs=2, units=6) as i:
                    for h in range(2):
                        staged(ACT.Identity if name else ACT.Copy, name, i * 2 + h)
                    E.skip_in_loop(units=6)

            act.wait_ge(S["consts_in"], 32)
            E.skip("counts")
            for half in range(2):
                w5 = wadj[half]
                with E.loop(5, jobs=2) as b:
                    take(lambda s, bank, at, n: move(cnt[:, bass.ds(b + 5 * half, 1), bass.ds(at, n)], bank[0:TL, :]))
                    take(lambda s, bank, at, n: move(w5[:, bass.ds(b, 1), bass.ds(at, n)], bank[0:TL, :]))
            act.wait_ge(S["deg_ready"], 1)
            nc.scalar.activation(dinv[0:TL, :], deg[0:TL, :], ACT.Sqrt).then_inc(S["deg_root"], 1)
            with E.loop(TT // 2, units=6) as i:
                squares_out.i = i
                squares_out()
            root(1)
            act.wait_ge(S["scaled"], TT)
            rows_out(f0)
            take(lambda s, bank, at, n: move(hs[0][0:BOT, bass.ds(at, n)], bank[0:BOT, :], ACT.Relu, bias=col("bd", rows=BOT)))
            E.skip_in_loop(jobs=6)
            for m in range(2):
                staged(ACT.Copy, None, m)
            E.skip("pair_back")
            for m in range(2):
                staged(ACT.Relu, "gb1", m)
            E.skip("pair_back")
            to_rows(f0, 2, ACT.Copy)
            staged_pairs("gb2")
            if BLOCKS > 1:
                root(2)
                root(3)
                rows_out(f0)
                act.wait_ge(S["affine_done"], 1)
                for k in range(KD):
                    a = move(f0[:, k, :], f0[:, k, :], ACT.Identity, bias=col("r_b", k), scale=col("r_g", k))
                a.then_inc(S["affine_done"], 1)
                to_rows(rz, 4, ACT.Gelu, "r_in_b")
                with E.loop(2, jobs=2, units=2) as i:
                    for h in range(2):
                        b = take_unit(lambda bank: move(gbias[:, h:h + 1], bank[:, 0:1], ACT.Identity, bias=col("r_o1_b", i * 2 + h)))
                        E.TO[b].wait(act)
                        take(lambda s, bank, at, n: move(f0[:, bass.ds(i * 2 + h, 1), bass.ds(at, n)], bank, ACT.Gelu,
                                                         bias=gbias[:, h:h + 1]))
                to_rows(rz, 2, ACT.Gelu, "r_o2_b")
                take(lambda s, bank, at, n: move(hs[0][0:4, bass.ds(at, n)], bank[0:4, :], ACT.Identity, bias=col("r_o3_b", rows=4)))
                E.skip("masks")
                to_rows(f0, 6, ACT.Identity, "bq")
                to_rows(rk, 6, ACT.Identity, "bk")
                staged_pairs("bv")
                sl = [E.slot(0), E.slot(1)]
                peak = Tally(S["max_ready"])

                def exps(h):
                    s = sl[h]
                    peak.add(1)
                    peak.wait(act)
                    E.JD[s].add(3)
                    E.JO[s].inc(nc.scalar.activation(
                        ys[h][0:TL, 0:2 * CH[0][1]].rearrange("p (c n) -> p c n", c=2), jp[s][0:TL, 0:2, 0:CH[0][1]], ACT.Exp,
                        bias=nb[0:TL, h:h + 1], scale=HD ** -0.5, accum_out=rsum[0:TL, 2 * h:2 * h + 1]))
                    at, n = CH[2]
                    E.JO[s].inc(nc.scalar.activation(
                        ys[h][0:TL, at:at + n], jp[s][0:TL, 2, 0:n], ACT.Exp,
                        bias=nb[0:TL, h:h + 1], scale=HD ** -0.5, accum_out=rsum[0:TL, 2 * h + 1:2 * h + 2]), 2)

                def two_tiles(ends=False):
                    g, n = GROUPS[1]
                    for u in range(4):
                        E.TD[1].add(1)
                        E.TD[1].wait(act, alone=True)
                        E.TO[1].inc(move(hst[u % 2][:, g:g + n, 0:TL], view(up[1], n, TL)))
                        E.TD[1].add(1)
                        E.TO[1].add(1)
                        if not (ends and u >= 2):
                            exps(u % 2)

                def pair(ends):
                    with repeat(act, 4, list(zip(tallies, [6, 6, 6, 6, 8, 8, 4]))):
                        two_tiles()
                    two_tiles(ends)

                tallies = [E.JD[0], E.JD[1], E.JO[0], E.JO[1], E.TD[1], E.TO[1], peak]
                exps(0)
                exps(1)
                with repeat(act, HP - 1, list(zip(tallies, [30, 30, 30, 30, 40, 40, 20]))):
                    pair(False)
                pair(True)
                E.TD[0].add(40 * HP)
                E.TO[0].add(40 * HP)
                E.skip("pairs3_back")
                root(4)
                rows_out(f0)
                to_rows(f1, 3, ACT.Gelu, "fc1_b")
                E.skip("pairs3_back")
                rows_out(f0)
                E.skip("pairs3")
                staged_pairs(None)
            if BLOCKS > 2:
                root(5)
                E.skip("vectors")
                rows_out(f0)
                e_in, p_out = Tally(S["e_ready"]), Tally(S["p_ready"])
                for layer in range(2):
                    take(lambda s, bank, at, n: move(kst[:, bass.ds(at, n)], bank))
                    take(lambda s, bank, at, n: move(hs[1][0:1, bass.ds(at, n)], bank[0:1, :]))
                    E.skip_in_loop(units=1)

                    def job_and_tiles(i):
                        for s in range(2):
                            e_in.add(1)
                            e_in.wait(act)
                            p_out.inc(nc.scalar.activation(hs[s][0:TL, 0:N], hs[s][0:TL, 0:N], ACT.Exp, bias=mneg[0:TL, s:s + 1]))
                        take(lambda s, bank, at, n: move(row(f1, i, at, n), bank))
                        squares_out.i = i
                        squares_out()

                    with E.loop(2, jobs=2, units=12, extra=[(e_in, 4), (p_out, 4)]) as i:
                        job_and_tiles(i * 2)
                        job_and_tiles(i * 2 + 1)
                    job_and_tiles(4)
                    take(lambda s, bank, at, n: move(row(f1, 5, at, n), bank))
                    with E.loop(3, jobs=2, units=12 if layer else 6) as i:
                        E.skip_in_loop(units=6)
                        for h in range(2):
                            if layer:
                                staged(ACT.Identity, "gat_b2", i * 2 + h)
                            else:
                                take(lambda s, bank, at, n: move(f0[:, bass.ds(i * 2 + h, 1), bass.ds(at, n)], bank, ACT.Relu,
                                                                 bias=col("gat_b1", i * 2 + h)))
                        if layer:
                            E.skip_in_loop(units=6)
            if BLOCKS > 3:
                root(6)
                rows_out(f0)
                to_rows(f1, 3, ACT.Gelu, "m_b1")
                take(lambda s, bank, at, n: move(ys[0][0:8, bass.ds(at, n)], bank[0:8, :], ACT.Identity, bias=col("m_b2", rows=8)))
                E.skip_in_loop(units=1)
                act.wait_ge(S["lg_ready"], 1)
                nc.scalar.activation(lg[0:TL, :], lg[0:TL, :], ACT.Exp).then_inc(S["lg_exp"], 1)
                act.wait_ge(S["route_ready"], 1)
                with act.Fori(0, EXPERTS // 2) as i:
                    for h in range(2):
                        first = act.value_load(first_slot[0:1, bass.ds(i * 2 + h, 1)], min_val=1, max_val=SLOTS - 1)
                        end = act.value_load(first_slot[0:1, bass.ds(i * 2 + h + 1, 1)], min_val=2, max_val=SLOTS)
                        with act.Fori(first, end) as s:
                            for c in range(2):
                                act.wait_ge(S[f"down_done{c}"], s)
                                act.sem_inc(Tally.passed[act.engine], 1)
                                for j in range(4 * c, 4 * c + 4):
                                    g = move(z_feat[:, bass.ts(j, P)], jp[0][:, c, j % 4 * P:(j % 4 + 1) * P], ACT.Gelu,
                                             bias=col("down_b", i * (2 * KE) + h * KE + j))
                            g.then_inc(S["z_ready"], 1)
                root(7)

        @block.vector
        def _(dve):
            E = Side(dve, S)
            V = nc.vector
            chain = Tally(S["dve_chain"])

            def then(instruction):
                chain.inc(instruction)
                chain.wait(dve)

            def take(write):
                s = E.next_job()
                for c, (at, n) in enumerate(CH):
                    E.wait_chunk(s)
                    E.JO[s].inc(write(s, jp[s][:, c, 0:n], at, n))
                return s

            def take_unit(write):
                b = E.next_unit()
                E.wait_unit(b)
                E.TO[b].inc(write(up[b]))
                return b

            rows = Tally(S["row_ready"])

            def stats_of(src, k):
                E.wait_all_out()
                st = stats[0:TL, :].rearrange("p (t h c) -> p t h c", t=TT, h=2)
                for t in range(TT):
                    for h in range(2):
                        i = V.bn_stats(st[:, t, h, :], src[:, t, h * 384:(h + 1) * 384])
                then(i)
                for t in range(TT):
                    i = V.bn_aggr(mvt[:, t, :], stats[0:TL, 12 * t:12 * t + 12])
                then(i)
                V.tensor_scalar(var[0:TL, :], mvt[:, :, 1], LN_EPS, None, ALU.add).then_inc(S["var_ready"], 1)
                dve.wait_ge(S["root_ready"], k)
                then(V.reciprocal(rs[0:TL, :], var[0:TL, :]))

            def normal(o, src, t):
                return V.tensor_scalar(o, src, mvt[:, t, 0:1], rs[0:TL, t:t + 1], ALU.subtract, ALU.mult)

            def stage_rows(src, norm=True, keep=None):
                E.wait_done()
                with E.loop(TT // 2, units=4, extra=[(rows, 2)]) as i:
                    for s in range(2):
                        t = i * 2 + s
                        E.TD[0].wait(dve, 1)
                        E.TD[1].wait(dve, 1)
                        x = src[:, bass.ds(t, 1), :]
                        o = ys[s][0:TL, 0:D]
                        if norm:
                            m, r = mvt[:, bass.ds(t, 1), 0], rs[0:TL, bass.ds(t, 1)]
                            if keep is not None:
                                V.tensor_scalar(keep[:, bass.ds(t, 1), :], x, m, r, ALU.subtract, ALU.mult)
                            rows.inc(V.tensor_scalar(o, x, m, r, ALU.subtract, ALU.mult))
                        else:
                            rows.inc(V.tensor_copy(o, x))
                        E.skip_in_loop(units=2)

            def add_back(x, pairs=3):
                with E.loop(pairs, jobs=2, units=6) as i:
                    E.skip_in_loop(jobs=2)
                    add_pair(x, i)

            def add_pair(x, i):
                for h in range(2):
                    for g, n in GROUPS:
                        xs = x[:, g:g + n, bass.ds(i * (2 * P) + h * P, P)]
                        take_unit(lambda bank: V.tensor_tensor(xs, xs, view(bank, n, P), ALU.add))

            for b in range(2):
                V.memset(gbias[:, b:b + 1], 0.0).then_inc(S[f"job_out{b}"], 3)
                V.memset(mneg[:, b:b + 1], 0.0).then_inc(S[f"unit_out{b}"], 1)
                V.memset(nb[:, b:b + 1], 0.0).then_inc(S[f"pair_used{b}"], 1)
            V.memset(zrow, 0.0)
            for ts in range(2):
                for h in range(2):
                    V.memset(qs[ts][h], 0.0)
            then(V.memset(ones[:, :], 1.0))
            dve.wait_ge(S["edges_in"], 80)
            V.tensor_copy(srcf, src_i)
            then(V.tensor_copy(dstf, dst_i))
            for b in range(TT):
                then(V.tensor_scalar(ge, dstf, float(b * TL), None, ALU.is_ge))
                i = V.scalar_tensor_tensor(in_bucket[:, b * ET:(b + 1) * ET], dstf, float((b + 1) * TL), ge, ALU.is_lt, ALU.mult)
                if b < TT - 1:
                    then(i)
            i.then_inc(S["tiles_hot"], 1)
            then(V.tensor_copy(wb, ew))
            then(V.tensor_copy(wpart[0], wb))
            then(V.tensor_tensor(wthird, ew, wpart[0], ALU.subtract))
            then(V.tensor_copy(wb, wthird))
            then(V.tensor_copy(wpart[1], wb))
            then(V.tensor_tensor(wthird, wthird, wpart[1], ALU.subtract))
            for g, n in BUCKETS:
                held = held_all[:, 0:n * ET].rearrange("p (b t) -> p b t", b=n)
                no = tq[:, 0:ET].rearrange("p (o t) -> p o t", o=1).to_broadcast([1, n, ET])
                b = take_unit(lambda bank: V.tensor_scalar(held_all[:, 0:n * ET], bank[0:1, 0:n * ET], 0.0, None, ALU.is_gt))
                E.TO[b].wait(dve)
                tmp = tmp_all[:, 0:n * ET].rearrange("p (b t) -> p b t", b=n)
                then(V.scalar_tensor_tensor(tmp, no, 1.0, held, ALU.add, ALU.mult))
                then(V.tensor_reduce(bf[:, 10 + g:10 + g + n], tmp, AX.X, ALU.max))
                then(V.scalar_tensor_tensor(tmp, no, -1000.0, held, ALU.add, ALU.mult))
                then(V.tensor_reduce(bf[:, g:g + n], tmp, AX.X, ALU.min))
            lo_f, hi_f, n_f, cum = bf[:, 0:10], bf[:, 10:20], bf[:, 30:40], bf[:, 40:50]
            then(V.tensor_scalar(lo_f, lo_f, 1000.0, float(EQ - 1), ALU.add, ALU.min))
            then(V.scalar_tensor_tensor(hi_f, lo_f, 1.0, hi_f, ALU.add, ALU.max))
            then(V.tensor_tensor(n_f, hi_f, lo_f, ALU.subtract))
            then(V.tensor_tensor_scan(cum, ones[0:1, 0:10], n_f, 0.0, ALU.mult, ALU.add))
            then(V.tensor_tensor(cum, cum, n_f, ALU.subtract))
            then(V.tensor_scalar(cum, cum, 1.0, None, ALU.add))
            then(V.scalar_tensor_tensor(bf[:, 20:30], lo_f, float(TT * EQ), cum, ALU.add, ALU.subtract))
            then(V.tensor_tensor(bf[:, 50:60], cum, n_f, ALU.add))
            then(V.tensor_copy(bounds[:, 20:30], bf[:, 20:30]))
            then(V.tensor_copy(bounds[:, 30:50], bf[:, 40:60]))
            V.memset(zs[:, 0:1], 0.0).then_inc(S["bounds_ready"], 1)
            with repeat(dve, TT, []) as b:
                first = dve.value_load(bounds[0:1, bass.ds(b + 30, 1)], min_val=1, max_val=TT * EQ)
                end = dve.value_load(bounds[0:1, bass.ds(b + 40, 1)], min_val=2, max_val=TT * EQ + 1)
                shift = dve.value_load(bounds[0:1, bass.ds(b + 20, 1)], min_val=0, max_val=TT * EQ + EQ)
                with dve.Fori(first, end) as turn:
                    pair = nc.s_assert_within(turn + shift - TT * EQ, 0, EQ - 1, skip_runtime_bounds_check_because=
                                              "a bucket's turns run over its range of pairs, within 0 to EQ - 1")
                    for s in range(2):
                        e = bass.ds(pair * 2 + s, 1)
                        dve.wait_ge(S[f"pair_used{s}"], turn)
                        V.tensor_scalar(hot_src[s], iota[0:TL, :], srcf[:, e], None, ALU.is_equal)
                        here = iota[0:TL, bass.ds(b * TL, TL)]
                        V.tensor_scalar(hot_dst[s][:, 0, :], here, dstf[:, e], None, ALU.is_equal)
                        for k, w in enumerate((wpart[0], wpart[1], wthird)):
                            i = V.tensor_scalar(hot_dst[s][:, 1 + k, :], here, dstf[:, e], w[:, e], ALU.is_equal, ALU.mult)
                        i.then_inc(S[f"pair_hot{s}"], 1)
            E.skip("matrices")
            E.wait_all_out()
            id_t = ident[0:TL, 0:TL]
            for t in range(TT):
                dg = cnt[:, t, tok(t)]
                i = V.tensor_tensor(dg, dg, id_t, ALU.add)
            i.then_inc(S["c_ready"], 1)
            for t in range(TT):
                dg = wadj[t // 5][:, t % 5, tok(t)]
                i = V.tensor_tensor(dg, dg, id_t, ALU.add)
            then(i)
            for half in range(2):
                i = V.tensor_reduce(deg[0:TL, 5 * half:5 * half + 5], wadj[half], AX.X, ALU.add)
            i.then_inc(S["deg_ready"], 1)
            dve.wait_ge(S["deg_root"], 1)
            then(V.reciprocal(dinv[0:TL, :], dinv[0:TL, :]))
            scaled = Tally(S["scaled"])
            E.wait_done()
            for t in range(TT):
                s = t % 2
                if t >= 2:
                    for b in range(2):
                        E.TD[b].wait(dve)
                scaled.inc(V.tensor_scalar(ys[s][0:TL, :], wadj[t // 5][:, t % 5, :], dinv[0:TL, t:t + 1], None, ALU.mult))
                if t >= 1:
                    E.skip_in_loop(units=3)
            E.skip_in_loop(units=3)
            dve.wait_ge(S["x_in"], 16)
            stats_of(xt, 1)
            stage_rows(xt)
            E.skip_in_loop(jobs=1)
            for m in range(KD):
                take(lambda s, bank, at, n: V.scalar_tensor_tensor(f1[:, m, bass.ds(at, n)], bank, col("bu", m),
                                                                   f0[:, m, bass.ds(at, n)], ALU.add, ALU.add))

            def features_staged(s, scale=None):
                for g, n in GROUPS:
                    if scale is None:
                        take_unit(lambda bank: V.tensor_copy(hst[s][:, g:g + n, :], view(bank, n, P)))
                    else:
                        sc = scale[0:TL, g:g + n].rearrange("p (t o) -> p t o", o=1).to_broadcast([TL, n, P])
                        take_unit(lambda bank: V.tensor_tensor(hst[s][:, g:g + n, :], view(bank, n, P), sc, ALU.mult))

            E.skip("pair")
            for _ in range(2):
                for s in (E.slot(0), E.slot(1)):
                    features_staged(s, dinv)
                E.skip("pair")
            add_back(xt)
            E.wait_all_out()
            V.memset(zs[:, 0:1], 0.0).then_inc(S["x_done"], 1)
            if BLOCKS > 1:
                stats_of(xt, 2)
                dve.wait_ge(S["c_saved"], 16)
                for t in range(TT):
                    i = normal(t0[:, t, :], xt[:, t, :], t)
                then(i)
                stats_of(t0, 3)
                stage_rows(t0)
                E.wait_all_out()
                for k in range(KD):
                    i = V.tensor_scalar(f1[:, k, :], f0[:, k, :], col("l1_g", k), col("l1_b", k), ALU.mult, ALU.add)
                i.then_inc(S["affine_done"], 1)
                E.skip("r_in")
                E.wait_all_out()
                then(V.tensor_reduce(g4, rz[:, 0:4, 1:N], AX.X, ALU.add))
                V.tensor_scalar(g4, g4, 1.0 / (N - 1), None, ALU.mult).then_inc(S["g_ready"], 1)
                E.skip("r_o1", "r_o2", "logits")
                for k in range(2):
                    take(lambda s, bank, at, n: V.tensor_scalar(masks[:, k, bass.ds(at, n)], bank, 0.0, None, ALU.is_gt))
                E.wait_all_out()
                then(V.memset(masks[:, 0:2, 0:1], 1.0))
                then(V.tensor_scalar(masks[:, 2, :], masks[:, 0, :], -1.0, 1.0, ALU.mult, ALU.add))
                V.tensor_scalar(masks[:, 4, :], masks[:, 1, :], -1.0, 1.0, ALU.mult, ALU.add)
                then(V.tensor_tensor(masks[:, 3, :], masks[:, 2, :], masks[:, 1, :], ALU.mult))
                then(V.tensor_tensor(masks[:, 2, :], masks[:, 2, :], masks[:, 4, :], ALU.mult))
                then(V.tensor_tensor(masks[:, 4, :], masks[:, 4, :], masks[:, 0, :], ALU.mult))
                E.skip("qk")
                dve.wait_ge(S["x_saved"], 16)
                with E.loop(3, jobs=2, units=6) as i:
                    E.skip_in_loop(jobs=2)
                    for h in range(2):
                        for g, n in GROUPS:
                            take_unit(lambda bank: V.tensor_copy(xt[:, g:g + n, bass.ds(i * (2 * P) + h * P, P)], view(bank, n, P)))
                sl = [E.slot(0), E.slot(1)]
                peak, norm, v_out = Tally(S["max_ready"]), Tally(S["norm_ready"]), Tally(S["v_staged"])
                n0 = CH[0][1]

                def maximum(h):
                    s = sl[h]
                    E.JD[s].add(2)
                    E.JD[s].wait(dve)
                    V.tensor_reduce(mm3[0:TL, 2 * h:2 * h + 1], jp[s][0:TL, 0:2, 0:n0], AX.XY, ALU.max)
                    E.JD[s].add(1)
                    E.JD[s].wait(dve)
                    then(V.tensor_reduce(mm3[0:TL, 2 * h + 1:2 * h + 2], jp[s][0:TL, 2, 0:CH[2][1]], AX.X, ALU.max))
                    peak.inc(V.tensor_scalar(nb[0:TL, h:h + 1], mm3[0:TL, 2 * h:2 * h + 1], mm3[0:TL, 2 * h + 1:2 * h + 2],
                                             -(HD ** -0.5), ALU.max, ALU.mult))
                    E.JO[s].add(3)

                def scale(h):
                    E.JO[sl[h]].wait(dve)
                    then(V.tensor_tensor(rinv[0:TL, h:h + 1], rsum[0:TL, 2 * h:2 * h + 1], rsum[0:TL, 2 * h + 1:2 * h + 2], ALU.add))
                    then(V.reciprocal(rinv[0:TL, h:h + 1], rinv[0:TL, h:h + 1]))
                    norm.inc(V.tensor_scalar(diag[h], ident[0:TL, 0:TL], rinv[0:TL, h:h + 1], None, ALU.mult))

                def two_tiles(hp, i, ends=False):
                    for u in range(4):
                        ts, h = u // 2, u % 2
                        for c, (g, n) in enumerate(GROUPS):
                            E.TD[c % 2].add(1)
                            if c == 1:
                                E.TO[1].add(1)
                                continue
                            E.TD[0].wait(dve)
                            E.TO[0].inc(V.tensor_copy(hst[h][:, g:g + n, 0:TL], view(up[0], n, TL)))
                        if not (ends and u == 3):
                            scale((u + 1) % 2)
                        if not (ends and u >= 2):
                            maximum(h)
                        E.TD[1].add(1)
                        E.TD[1].wait(dve)
                        mine = slice(h * HD, h * HD + HD)
                        E.TO[1].inc(V.tensor_copy(f1[mine, bass.ds(hp, 1), bass.ds(i * (2 * TL) + ts * TL, TL)], up[1][mine, 0:TL]))

                def pair(hp, ends):
                    v_out.inc(V.tensor_copy(vst, xt[:, :, bass.ds(hp * P, P)]))
                    with repeat(dve, 4, list(zip(tallies, [6, 6, 6, 6, 8, 8, 8, 8, 4, 4, 0, 12]))) as i:
                        two_tiles(hp, i)
                    two_tiles(hp, 4, ends)

                tallies = [E.JD[0], E.JD[1], E.JO[0], E.JO[1], E.TD[0], E.TO[0], E.TD[1], E.TO[1], peak, norm, v_out, chain]
                for t in E.TO:
                    t.wait(dve)
                maximum(0)
                maximum(1)
                scale(0)
                with repeat(dve, HP - 1, list(zip(tallies, [30, 30, 30, 30, 40, 40, 40, 40, 20, 20, 1, 60]))) as hp:
                    pair(hp, False)
                pair(HP - 1, True)

                def masked_back(name, mask):
                    with E.loop(3, jobs=2, units=6) as i:
                        for h in range(2):
                            take(lambda s, bank, at, n: V.scalar_tensor_tensor(
                                ys[s][:, bass.ds(at, n)], bank, col(name, i * 2 + h), masks[:, mask, bass.ds(at, n)],
                                ALU.add, ALU.mult))
                        add_pair(t0, i)

                masked_back("bo", 0)
                stats_of(t0, 4)
                stage_rows(t0)
                E.wait_all_out()
                for k in range(KD):
                    i = V.tensor_scalar(f0[:, k, :], f0[:, k, :], col("l2_g", k), col("l2_b", k), ALU.mult, ALU.add)
                i.then_inc(S["affine_done"], 1)
                E.skip("fc1")
                masked_back("fc2_b", 1)
                E.wait_all_out()
                stage_rows(t0, norm=False)
                with E.loop(3, jobs=2) as i:
                    for h in range(2):
                        take(lambda s, bank, at, n: V.tensor_tensor(f1[:, bass.ds(i * 2 + h, 1), bass.ds(at, n)], bank,
                                                                    masks[:, bass.ds(i + 2, 1), bass.ds(at, n)], ALU.mult))
                add_back(t0)
                E.wait_all_out()
                dve.wait_ge(S["x_back"], 16)
                V.tensor_tensor(X[0:TL, :], X[0:TL, :], TC[0:TL, :], ALU.add).then_inc(S["x_done"], 1)
                dve.wait_ge(S["x_done"], 2)
            if BLOCKS > 2:
                stats_of(xt, 5)
                for layer in range(2):
                    b = take_unit(lambda bank: V.tensor_copy(att_v[:, layer * 2 * KD:(layer + 1) * 2 * KD], bank[:, 0:2 * KD]))
                stage_rows(xt)
                e_out, p_in, alpha = Tally(S["e_ready"]), Tally(S["p_ready"]), Tally(S["alpha_ready"])
                for layer in range(2):
                    E.wait_done()
                    for t in E.TO:
                        t.wait(dve)
                    V.tensor_copy(hs[0][:, 0:D].rearrange("p (k c) -> p k c", k=KD),
                                  att_v[:, layer * 2 * KD:(layer + 1) * 2 * KD:2].rearrange("p (k o) -> p k o", o=1)
                                  .to_broadcast([P, KD, P])).then_inc(S["att_ready"], 1)
                    E.skip_in_loop(jobs=2)
                    b = take_unit(lambda bank: V.tensor_copy(ad[0:TL, :], bank[0:TL, 0:TT]))
                    E.wait_all_out()
                    E.wait_done()
                    if layer == 0:
                        dve.wait_ge(S["c_back"], 16)
                    with E.loop(TT // 2, units=6, extra=[(e_out, 2), (p_in, 2), (alpha, 2), (chain, 14)]) as i:
                        for s in range(2):
                            t = i * 2 + s
                            h, c = hs[s][0:TL, 0:N], cnt[:, bass.ds(t, 1), :]
                            then(V.tensor_scalar(h, c, 0.0, -BIG, ALU.is_equal, ALU.mult))
                            then(V.tensor_tensor(h, h, kst[0:TL, :], ALU.add))
                            then(V.tensor_scalar(h, h, ad[0:TL, bass.ds(t, 1)], None, ALU.add, ALU.max, accum_out=zs[0:TL, s:s + 1]))
                            then(V.scalar_tensor_tensor(h, h, 0.2, h, ALU.mult, ALU.max))
                            then(V.scalar_tensor_tensor(zs[0:TL, 2 + s:3 + s], zs[0:TL, s:s + 1], 0.2, zs[0:TL, s:s + 1], ALU.mult, ALU.max))
                            e_out.inc(V.tensor_scalar(mneg[0:TL, s:s + 1], zs[0:TL, 2 + s:3 + s], -1.0, None, ALU.mult))
                        for s in range(2):
                            t = i * 2 + s
                            p_in.add(1)
                            p_in.wait(dve, alone=True)
                            if s == 0:
                                E.TD[0].wait(dve, alone=True)
                                E.TD[1].wait(dve, alone=True)
                            then(V.scalar_tensor_tensor(ys[s][0:TL, :], hs[s][0:TL, 0:N], 1.0, cnt[:, bass.ds(t, 1), :],
                                                        ALU.mult, ALU.mult, accum_out=rinv[0:TL, s:s + 1]))
                            then(V.reciprocal(zs[0:TL, s:s + 1], rinv[0:TL, s:s + 1]))
                            alpha.inc(V.tensor_scalar(ys[s][0:TL, :], ys[s][0:TL, :], zs[0:TL, s:s + 1], None, ALU.mult))
                        E.skip_in_loop(units=6)
                    E.skip("pairs3")
                    E.wait_all_out()
                    with E.loop(3, jobs=2, units=12 if layer else 6) as i:
                        for h in range(2):
                            features_staged(E.slot(h))
                        E.skip_in_loop(jobs=2)
                        if layer:
                            add_pair(xt, i)
                E.wait_all_out()
                V.memset(zs[:, 0:1], 0.0).then_inc(S["x_done"], 1)
            if BLOCKS > 3:
                stats_of(xt, 6)
                stage_rows(xt, keep=t0)
                V.memset(zs[:, 1:2], 0.0).then_inc(S["stream_ready"], 1)
                E.skip("m_w1")
                E.skip_in_loop(jobs=1)
                b = take_unit(lambda bank: V.tensor_copy(lg[0:TL, :], bank[0:TL, 0:8 * TT]))
                E.TO[b].wait(dve)
                lg3, pr3, t3, oh3 = [x[0:TL, :].rearrange("p (t e) -> p t e", t=TT) for x in (lg, pr, t8, oh)]
                top = m10[0:TL, 0:TT]

                def wide(x):
                    return x.rearrange("p (t o) -> p t o", o=1).to_broadcast([TL, TT, EXPERTS])

                number = iota[0:TL, 0:EXPERTS].rearrange("p (o e) -> p o e", o=1).to_broadcast([TL, TT, EXPERTS])
                then(V.tensor_reduce(top, lg3, AX.X, ALU.max))
                V.tensor_tensor(lg3, lg3, wide(top), ALU.subtract).then_inc(S["lg_ready"], 1)
                dve.wait_ge(S["lg_exp"], 1)
                then(V.tensor_reduce(top, lg3, AX.X, ALU.add))
                then(V.reciprocal(m10[0:TL, 10:20], top))
                then(V.tensor_tensor(lg3, lg3, wide(m10[0:TL, 10:20]), ALU.mult))
                then(V.tensor_copy(pr3, lg3))
                hot = [lg3, t3]
                gates = m10[0:TL, 0:CHOICES * TT]
                for c in range(CHOICES):
                    top = gates[:, c * TT:(c + 1) * TT]
                    then(V.tensor_reduce(top, pr3, AX.X, ALU.max))
                    then(V.tensor_tensor(t3, pr3, wide(top), ALU.not_equal))
                    then(V.scalar_tensor_tensor(t3, t3, 100.0, number, ALU.mult, ALU.add))
                    then(V.tensor_reduce(m10[0:TL, 20:30], t3, AX.X, ALU.min))
                    then(V.tensor_tensor(hot[c], number, wide(m10[0:TL, 20:30]), ALU.is_equal))
                    if c == 0:
                        then(V.scalar_tensor_tensor(pr3, hot[0], -4.0, pr3, ALU.mult, ALU.add))
                V.tensor_tensor(oh3, hot[0], hot[1], ALU.add).then_inc(S["chosen"], 1)
                g2 = gates.rearrange("p (c t) -> p c t", c=CHOICES)
                total = m10[0:TL, 20:30]
                then(V.tensor_tensor(total, gates[:, 0:TT], gates[:, TT:2 * TT], ALU.add))
                then(V.tensor_scalar(total, total, 1e-8, None, ALU.add))
                then(V.reciprocal(total, total))
                V.tensor_tensor(g2, g2, total.rearrange("p (c t) -> p c t", c=1).to_broadcast([TL, CHOICES, TT]), ALU.mult)
                room = [ys[1][0:TL, 700 + k * 80:780 + k * 80] for k in range(3)]
                rank, upto, scratch = [x.rearrange("p (t e) -> p t e", t=TT) for x in room]
                fine = hs[1][0:TL, D + 110:D + 310]
                dve.wait_ge(S["chosen"], 2)
                V.tensor_copy(rank, up[1][0:TL, 0:80].rearrange("p (t e) -> p t e", t=TT))
                then(V.tensor_copy(scratch, up[1][0:TL, 80:160].rearrange("p (t e) -> p t e", t=TT)))
                then(V.memset(upto[:, 0, :], 0.0))
                for t in range(1, TT):
                    then(V.tensor_tensor(upto[:, t, :], upto[:, t - 1, :], scratch[:, t - 1, :], ALU.add))
                small8 = fine[:, 160:200]
                load, slots, cum, begin = [small8[:, k * 8:k * 8 + 8] for k in range(4)]
                V.tensor_tensor(rank, rank, upto, ALU.add)
                then(V.tensor_tensor(load, upto[:, TT - 1, :], scratch[:, TT - 1, :], ALU.add))
                steps = iota[0:TL, 0:(TT - 1) * P + 1:P]
                cmp = fine[:, 0:80].rearrange("p (e k) -> p e k", e=EXPERTS)
                then(V.tensor_tensor(cmp, load.rearrange("p (e k) -> p e k", k=1).to_broadcast([TL, EXPERTS, TT]),
                                     steps.rearrange("p (e k) -> p e k", e=1).to_broadcast([TL, EXPERTS, TT]), ALU.is_gt))
                then(V.tensor_reduce(slots, cmp, AX.X, ALU.add))
                then(V.tensor_scalar(slots, slots, 1.0, None, ALU.max))
                then(V.tensor_tensor_scan(cum, ones[0:TL, 0:EXPERTS], slots, 0.0, ALU.mult, ALU.add))
                then(V.tensor_tensor(begin, cum, slots, ALU.subtract))
                then(V.tensor_scalar(begin, begin, 1.0, None, ALU.add))
                V.tensor_copy(first_slot[:, 0:EXPERTS], begin[0:1, :])
                then(V.tensor_scalar(cum, cum, 1.0, None, ALU.add))
                then(V.tensor_copy(first_slot[:, EXPERTS:EXPERTS + 1], cum[0:1, EXPERTS - 1:EXPERTS]))
                then(V.tensor_scalar(cum, cum, -1.0, float(SLOTS + 1), ALU.mult, ALU.add))
                V.tensor_copy(first_slot[:, EXPERTS + 1:EXPERTS + 2], cum[0:1, EXPERTS - 1:EXPERTS])
                base, order, count, row, place = [ys[1][0:TL, 940 + k * 20:960 + k * 20] for k in range(5)]
                starts = begin.rearrange("p (t e) -> p t e", t=1).to_broadcast([TL, TT, EXPERTS])
                for c in range(CHOICES):
                    mine = slice(c * TT, (c + 1) * TT)
                    then(V.tensor_tensor(scratch, hot[c], starts, ALU.mult))
                    then(V.tensor_reduce(base[:, mine], scratch, AX.X, ALU.add))
                    then(V.tensor_tensor(scratch, hot[c], rank, ALU.mult))
                    then(V.tensor_reduce(order[:, mine], scratch, AX.X, ALU.add))
                cmp = ys[1][0:TL, 1040:1240].rearrange("p (i k) -> p i k", k=TT)
                then(V.tensor_tensor(cmp, order.rearrange("p (i k) -> p i k", k=1).to_broadcast([TL, CHOICES * TT, TT]),
                                     steps.rearrange("p (i k) -> p i k", i=1).to_broadcast([TL, CHOICES * TT, TT]), ALU.is_ge))
                then(V.tensor_reduce(count, cmp, AX.X, ALU.add))
                then(V.tensor_scalar(count, count, -1.0, None, ALU.add))
                then(V.scalar_tensor_tensor(row, count, -float(P), order, ALU.mult, ALU.add))
                then(V.tensor_tensor(base, base, count, ALU.add))
                then(V.tensor_scalar(place, base, -1.0, float(P), ALU.add, ALU.mult))
                then(V.tensor_tensor(place, place, row, ALU.add))
                V.tensor_copy(places, place)
                wide_slot = [TL, CHOICES * TT, SLOTS + 2]
                V.tensor_tensor(hot_slot, base.rearrange("p (i k) -> p i k", k=1).to_broadcast(wide_slot),
                                iota[0:TL, 1:SLOTS + 3].rearrange("p (i k) -> p i k", i=1).to_broadcast(wide_slot), ALU.is_equal)
                dve.wait_ge(S["rows_in"], 64)
                for i in range(CHOICES * TT):
                    hr = V.tensor_scalar(hot_row[i // TT][:, i % TT, :], iota[0:TL, 0:P], row[:, i:i + 1],
                                         token_no[:, i % TT:i % TT + 1], ALU.is_equal, ALU.mult)
                hr.then_inc(S["one_hot"], 1)
                dve.wait_ge(S["one_hot"], 2)
                V.tensor_copy(members, up[0][:, 0:SLOTS + 2]).then_inc(S["route_ready"], 1)
                dve.wait_ge(S["route_ready"], 1)

                def features():
                    V.tensor_copy(x_feat[:, 0:4 * P], jp[0][:, 2, :])
                    V.tensor_copy(x_feat[:, 4 * P:KD * P], jp[1][:, 2, 0:2 * P]).then_inc(S["xt_ready"], 1)

                V.memset(zs[:, 0:1], 0.0).then_inc(S["y_ready"], 1)
                V.memset(zs[:, 2:3], 0.0).then_inc(S["y_free"], 1)
                V.memset(zs[:, 3:4], 0.0).then_inc(S["up_done1"], 1)
                dve.wait_ge(S["x_turned"], 1)
                features()
                end = dve.value_load(first_slot[0:1, EXPERTS:EXPERTS + 1], min_val=2, max_val=SLOTS)
                with dve.Fori(1, end) as s:
                    dve.wait_ge(S["x_turned"], s + 1)
                    features()
                    dve.wait_ge(S["y_free"], s)
                    for c in range(2):
                        dve.wait_ge(S[f"up_done{c}"], s + c)
                        o = V.tensor_copy(y_rows[:, c * (D // 2):(c + 1) * (D // 2)], jp[1][:, c, 0:D // 2])
                    o.then_inc(S["y_ready"], 1)
                for i in range(CHOICES * TT):
                    c, t = i % 2, i // 2
                    if i % 4 == 0:
                        dve.wait_ge(S[f"y_gathered{i // 4}"], 64)
                    k = c * TT + t
                    then(V.scalar_tensor_tensor(t0[:, t, :], y_got[k], gates[:, k:k + 1], t0[:, t, :], ALU.mult, ALU.add))
                stats_of(t0, 7)
                for t in range(TT):
                    then(normal(t0[:, t, :], t0[:, t, :], t))
                    then(V.tensor_tensor(t0[:, t, :], t0[:, t, :], hs[0][0:TL, 0:D], ALU.mult))
                    then(V.tensor_tensor(xt[:, t, :], xt[:, t, :], t0[:, t, :], ALU.add))
                    V.tensor_tensor(xt[:, t, :], xt[:, t, :], hs[1][0:TL, 0:D], ALU.add).then_inc(S["out_tile"], 1)

        @block.gpsimd
        def _(pool):
            E = Side(pool, S)
            E.skip("counts", "matrices")
            for t in E.JD:
                t.wait(pool)
            pool.dma_start(hs[1][0:BOT, 0:D], A["wu"]).then_inc(S["wu_in"], 16)
            pool.dma_start(dif, A["dif"]).then_inc(S["wu_in"], 16)
            pool.wait_ge(S["c_ready"], 1)
            pool.dma_start(c_dram, c_all).then_inc(S["c_saved"], 16)
            E.skip("w_transpose", "rows", "adapter", "pair", "pair_back", "pair", "pair_back", "pair", "pairs3_back")
            if BLOCKS > 1:
                pool.wait_ge(S["x_done"], 1)
                pool.dma_start(x_dram, X[0:TL, :]).then_inc(S["x_saved"], 16)
                E.skip("rows", "r_in", "r_o1", "r_o2", "logits", "masks", "qk", "pairs3_back")
                E.wait_all_out()
                q_out = Tally(S["q_staged"])
                done = [Tally(S["job_done0"], E.JD[0].count - 3), Tally(S["job_done1"], E.JD[1].count - 3)]
                with repeat(pool, HP, [(q_out, 20), (done[0], 30), (done[1], 30)]) as hp:
                    with repeat(pool, TT // 2, [(q_out, 4), (done[0], 6), (done[1], 6)]) as i:
                        for ts in range(2):
                            for d in done:
                                d.wait(pool)
                                d.add(3)
                            for h in range(2):
                                mine = slice(h * HD, h * HD + HD)
                                q_out.inc(nc.gpsimd.tensor_copy(
                                    qs[ts][h][mine, :], f0[mine, bass.ds(hp, 1), bass.ds(i * (2 * TL) + ts * TL, TL)]))
                                q_out.wait(pool, alone=True)
                E.skip("attention")
                for t in E.TD:
                    t.wait(pool)
                pool.dma_start(X[0:TL, :], x_dram).then_inc(S["x_back"], 16)
                E.skip("pairs3_back", "rows", "fc1", "pairs3_back", "rows", "pairs3")
                for t in E.JO:
                    t.wait(pool)
                if BLOCKS > 2:
                    pool.dma_start(wt.rearrange("p (l f) -> p l f", l=2), A["gat_wt"]).then_inc(S["wt_in"], 16)
                E.skip("pairs3_back")
                pool.wait_ge(S["x_done"], 2)
                pool.wait_ge(S["c_saved"], 16)
                pool.dma_start(c_all, c_dram).then_inc(S["c_back"], 16)
            if BLOCKS > 2:
                staged = Tally(S["h_staged"])
                E.skip("vectors", "rows")
                for layer in range(2):
                    E.skip("att", "alpha", "pairs3")
                    E.wait_all_out()
                    E.wait_done()
                    with E.loop(3, jobs=2, units=12 if layer else 6, extra=[(staged, 2)]) as i:
                        E.wait_done()
                        for h in range(2):
                            staged.inc(nc.gpsimd.tensor_copy(ys[E.slot(h)][:, :], f1[:, bass.ds(i * 2 + h, 1), :]))
                        E.skip_in_loop(jobs=2, units=12 if layer else 6)
            if BLOCKS > 3:
                E.wait_done()
                pool.dma_start(hs[0][0:TL, 0:D], A["gamma"].to_broadcast([TL, D])).then_inc(S["rows_in"], 16)
                pool.dma_start(hs[1][0:TL, 0:D], A["beta"].to_broadcast([TL, D])).then_inc(S["rows_in"], 16)
                pool.dma_start(before, A["before"]).then_inc(S["rows_in"], 16)
                pool.dma_start(token_no, A["token_no"]).then_inc(S["rows_in"], 16)
                pool.wait_ge(S["stream_ready"], 1)
                pool.dma_start(stream_dram.rearrange("(t p) d -> p t d", p=TL), t0).then_inc(S["stream_saved"], 16)
                pool.wait_ge(S["route_ready"], 1)
                pool.wait_ge(S["stream_saved"], 16)

                def gather(slot, s):
                    nc.gpsimd.tensor_copy(member, members[:, bass.ds(slot, 1)]).then_inc(S["member_ready"], 1)
                    pool.wait_ge(S["member_ready"], s)
                    pool.sem_inc(Tally.passed[pool.engine], 1)
                    nc.gpsimd.indirect_dma_start(x_rows, None, stream_dram, bass.IndirectOffsetOnAxis(ap=member, axis=0)).then_inc(
                        S["x_gathered"], 16)

                gather(0, 1)
                pool.wait_ge(S["x_turned"], 1)
                gather(1, 2)
                end = pool.value_load(first_slot[0:1, EXPERTS:EXPERTS + 1], min_val=2, max_val=SLOTS)
                empty = pool.value_load(first_slot[0:1, EXPERTS + 1:EXPERTS + 2], min_val=1, max_val=SLOTS - 1)
                with pool.Fori(1, end) as s:
                    pool.wait_ge(S["x_turned"], s + 1)
                    gather(s + 1, s + 2)
                    pool.wait_ge(S["y_ready"], s + 1)
                    pool.dma_start(y_dram[bass.ds(s * P - P, P), :], y_rows).then_inc(S["y_saved"], 16)
                    pool.wait_ge(S["y_saved"], s * 16)
                    pool.sem_inc(S["y_free"], 1)
                pool.wait_ge(S["y_free"], end)
                pool.wait_ge(S["y_filled"], empty * 16)
                pool.wait_ge(S["x_gathered"], end * 16 + 16)
                pool.sem_inc(Tally.passed[pool.engine], 1)
                for i in range(CHOICES * TT):
                    k = i % 2 * TT + i // 2
                    nc.gpsimd.indirect_dma_start(y_got[k], None, y_dram, bass.IndirectOffsetOnAxis(ap=places[:, k:k + 1], axis=0)).then_inc(
                        S[f"y_gathered{i // 4}"], 16)


def kernel(**inputs):
    import concourse.bacc as bacc
    from concourse.bass_utils import run_bass_kernel_spmd

    a = {k: np.ascontiguousarray(v) for k, v in inputs.items()}

    def tiles(w):
        k, m = w.shape
        return np.ascontiguousarray(w.reshape(k // P, P, m // P, P).transpose(2, 1, 0, 3).reshape(m // P, P, k))

    def narrow(w):
        return np.ascontiguousarray(w.reshape(-1, P, w.shape[1]).transpose(1, 0, 2))

    def edges(e):
        return np.ascontiguousarray(e.reshape(ET, TL).T)

    f, g, m = "L0_ffn_", "L0_gnn_", "L1_ffn_"
    vec = {"bd": a[g + "bd"], "bu": a[g + "bu"], "gb1": a[g + "b1"], "gb2": a[g + "b2"], "r_g": a[f + "r_ln_g"],
           "r_b": a[f + "r_ln_b"], "l1_g": a[f + "ln1_g"], "l1_b": a[f + "ln1_b"], "r_in_b": a[f + "r_in_b"],
           "r_o1_b": a[f + "r_o1_b"], "r_o2_b": a[f + "r_o2_b"], "r_o3_b": a[f + "r_o3_b"], "bq": a[f + "bq"],
           "bk": a[f + "bk"], "bv": a[f + "bv"], "bo": a[f + "bo"], "l2_g": a[f + "ln2_g"], "l2_b": a[f + "ln2_b"],
           "fc1_b": a[f + "fc1_b"], "fc2_b": a[f + "fc2_b"], "as1": a["L1_gnn_att_src1"], "ad1": a["L1_gnn_att_dst1"],
           "gat_b1": a["L1_gnn_b1"], "as2": a["L1_gnn_att_src2"], "ad2": a["L1_gnn_att_dst2"], "gat_b2": a["L1_gnn_b2"],
           "m_b1": a[m + "b1"], "m_b2": a[m + "b2"], "down_b": a[m + "down_b"].reshape(-1)}
    cols = np.zeros((P, NCOL), np.float32)
    for name, n in VECTORS:
        v = vec[name]
        if v.size < P:
            cols[:v.size, COL[name]] = v
        else:
            cols[:, COL[name]:COL[name] + n] = v.reshape(n, P).T
    dif = np.zeros((4, 2, P), np.float32)
    for k in range(2):
        dif[2 * k, k], dif[2 * k + 1, k] = -1.0, 1.0
    arrays = {
        "src": edges(a["src"]), "dst": edges(a["dst"]), "ew": edges(a["edge_weight"]),
        "iota": np.ascontiguousarray(np.broadcast_to(np.arange(N, dtype=np.float16), (P, N))),
        "pairno": (np.arange(ET) // 2).astype(np.float32).reshape(1, ET),
        "ident": np.eye(P, dtype=np.float32), "cols": cols, "dif": dif,
        "x": np.ascontiguousarray(a["x"].reshape(TT, TL, D).transpose(1, 0, 2)),
        "wd": narrow(a[g + "Wd"]), "w3": narrow(a[f + "r_o3_w"].T), "wm2": narrow(a[m + "w2"]), "wu": a[g + "Wu"],
        "w1": tiles(a[g + "W1"]), "w2": tiles(a[g + "W2"]), "r_in": tiles(a[f + "r_in_w"].T),
        "r_o1": tiles(a[f + "r_o1_w"].T), "r_o2": tiles(a[f + "r_o2_w"].T),
        "wqkv": np.concatenate([tiles(a[f + w].T) for w in ("wq", "wk", "wv")]), "wo": tiles(a[f + "wo"].T),
        "fc1": tiles(a[f + "fc1_w"].T), "fc2": tiles(a[f + "fc2_w"].T),
        "lra_down": tiles(a[f + "lra_down"].reshape(D, D).T),
        "lra_up": tiles(a[f + "lra_up"].transpose(0, 2, 1).reshape(D, D)),
        "gat_wt": np.stack([narrow(a[f"L1_gnn_W{k}"].T).reshape(P, KD * D) for k in (1, 2)], 1),
        "gat_w1": tiles(a["L1_gnn_W1"]), "gat_w2": tiles(a["L1_gnn_W2"]), "m_w1": tiles(a[m + "w1"]),
        "down": tiles(a[m + "down_w"].transpose(1, 0, 2).reshape(D, EXPERTS * DE)).reshape(EXPERTS, KE, P, D)
        .transpose(0, 2, 1, 3).reshape(EXPERTS, P, KE * D),
        "up": a[m + "up_w"].reshape(EXPERTS, KE, P, D).transpose(0, 2, 1, 3).reshape(EXPERTS, P, KE * D),
        "before": np.concatenate([np.triu(np.ones((TL, TL), np.float32), 1), np.ones((TL, TL), np.float32)], 1),
        "token_no": np.ascontiguousarray(np.arange(N, dtype=np.float32).reshape(TT, TL).T),
        "gamma": a[m + "gamma"].reshape(1, D), "beta": a[m + "beta"].reshape(1, D),
    }
    nc = bacc.Bacc("TRN2", target_bir_lowering=False, num_devices=1)
    A = {k: nc.dram_tensor(f"in_{k}", v.shape, mybir.dt.from_np(v.dtype), kind="ExternalInput").ap() for k, v in arrays.items()}
    out = nc.dram_tensor("result", (TL, TT, D), F32, kind="ExternalOutput").ap()
    build(nc, A, out)
    r = run_bass_kernel_spmd(nc, [{f"in_{k}": v for k, v in arrays.items()}], core_ids=[0])
    return r.results[0]["result"].transpose(1, 0, 2).reshape(N, D)
```

```python
from contextlib import ExitStack, contextmanager

import numpy as np

import concourse.bass as bass
from concourse import mybir

F32 = mybir.dt.float32
BF16 = mybir.dt.bfloat16
F16 = mybir.dt.float16
U16 = mybir.dt.uint16
I32 = mybir.dt.int32
ACT = mybir.ActivationFunctionType
ALU = mybir.AluOpType
AX = mybir.AxisListType

P = 128
N = 1250
TT = 10
TL = N // TT
D = 768
KD = D // P
EDGES = 20000
ET = EDGES // TL
EQ = ET // 2
HEADS, HD = 12, 64
HP = HEADS // 2
BOT = 24
EXPERTS, DE = 8, 1024
KE = DE // P
CHOICES = 2
SLOTS = (CHOICES * N + EXPERTS * (P - 1)) // P + 1
CH = [(0, 417), (417, 417), (834, 416)]
GROUPS = [(0, 4), (4, 4), (8, 2)]
BIG = 1.0e30
LN_EPS = 1e-5
BUCKETS = [(0, 3), (3, 3), (6, 3), (9, 1)]
BLOCKS = 4

VECTORS = [("bd", 1), ("bu", 6), ("gb1", 2), ("gb2", 6), ("r_g", 6), ("r_b", 6), ("l1_g", 6), ("l1_b", 6),
           ("r_in_b", 4), ("r_o1_b", 4), ("r_o2_b", 2), ("r_o3_b", 1), ("bq", 6), ("bk", 6), ("bv", 6),
           ("bo", 6), ("l2_g", 6), ("l2_b", 6), ("fc1_b", 3), ("fc2_b", 6),
           ("as1", 6), ("ad1", 6), ("gat_b1", 6), ("as2", 6), ("ad2", 6), ("gat_b2", 6),
           ("m_b1", 3), ("m_b2", 1), ("down_b", EXPERTS * KE)]
COL, NCOL = {}, 0
for _name, _n in VECTORS:
    COL[_name] = NCOL
    NCOL += _n

STREAMED = {"w1": (2, 6), "w2": (6, 2), "r_in": (4, 6), "r_o1": (4, 8), "r_o2": (2, 4), "wqkv": (18, 6),
            "wo": (6, 6), "fc1": (3, 6), "fc2": (6, 3), "lra_down": (6, 6), "lra_up": (6, 6),
            "gat_w1": (6, 6), "gat_w2": (6, 6), "m_w1": (3, 6)}


class Tally:

    passed = {}

    def __init__(self, sem, start=0):
        self.sem, self.count, self.loops = sem, start, []

    def add(self, n=1):
        self.count += n

    def inc(self, instruction, n=1):
        instruction.then_inc(self.sem, n)
        self.count += n

    def value(self, back=0):
        v = self.count - back
        for i, per in self.loops:
            if per:
                v = i * per + v
        return v

    def wait(self, eng, back=0, alone=False):
        if self.count - back > 0:
            value = self.value(back)
            eng.wait_ge(self.sem, value)
            if alone and not isinstance(value, int):
                eng.sem_inc(self.passed[eng.engine], 1)
        else:
            assert not any(per for _, per in self.loops), "a wait below one in a loop"


@contextmanager
def repeat(eng, n, per):
    with eng.Fori(0, n) as i:
        was = [t.count for t, _ in per]
        for t, by in per:
            t.loops.append((i, by))
        yield i
        got = [t.count - w for (t, _), w in zip(per, was)]
        for t, by in per:
            t.loops.pop()
        assert got == [by for _, by in per], (got, [by for _, by in per])
    for t, by in per:
        t.count += by * (n - 1)


PLAN = {"counts": (0, 4), "matrices": (2 * TT, 0), "w_transpose": (TT, 0), "rows": (TT, 0),
        "adapter": (7, 0), "pair": (2, 0), "pair_back": (0, 6), "pairs3": (6, 0), "pairs3_back": (6, 18),
        "r_in": (4, 0), "r_o1": (4, 4), "r_o2": (2, 0), "logits": (1, 0), "masks": (2, 0), "qk": (12, 0),
        "fc1": (3, 0), "vectors": (0, 2), "att": (2, 1), "alpha": (0, 3 * TT), "agg0": (6, 18), "agg1": (6, 36),
        "m_w1": (3, 0), "gates": (1, 1)}


class Side:

    def __init__(self, eng, S):
        self.eng = eng
        self.JD = [Tally(S["job_done0"]), Tally(S["job_done1"])]
        self.JO = [Tally(S["job_out0"], 3), Tally(S["job_out1"], 3)]
        self.TD = [Tally(S["unit_done0"]), Tally(S["unit_done1"])]
        self.TO = [Tally(S["unit_out0"], 1), Tally(S["unit_out1"], 1)]
        self.W = [Tally(S["w_full0"]), Tally(S["w_full1"])]
        self.job = self.unit = 0

    @contextmanager
    def loop(self, n, jobs=0, units=0, weights=0, extra=()):
        assert jobs % 2 == 0 and units % 2 == 0 and weights % 2 == 0
        per = [(t, 3 * jobs // 2) for t in self.JD + self.JO] + [(t, units // 2) for t in self.TD + self.TO]
        per += [(t, 16 * weights // 2) for t in self.W] + list(extra)
        with repeat(self.eng, n, per) as i:
            yield i

    def next_job(self):
        self.job += 1
        return (self.job - 1) % 2

    def next_unit(self):
        self.unit += 1
        return (self.unit - 1) % 2

    def wait_chunk(self, s):
        self.JD[s].add(1)
        self.JD[s].wait(self.eng, alone=self.eng.engine == mybir.EngineType.Activation)

    def wait_unit(self, b):
        self.TD[b].add(1)
        self.TD[b].wait(self.eng, alone=self.eng.engine == mybir.EngineType.Activation)

    def slot(self, ahead=0):
        return (self.job + ahead) % 2

    def skip(self, *stages):
        for name in stages:
            if name == "attention":
                for t in self.JD + self.JO:
                    t.add(30 * HP)
                for t in self.TD + self.TO:
                    t.add(40 * HP)
                continue
            jobs, units = PLAN[name]
            for _ in range(jobs):
                s = self.next_job()
                self.JD[s].add(3)
                self.JO[s].add(3)
            for _ in range(units):
                b = self.next_unit()
                self.TD[b].add(1)
                self.TO[b].add(1)

    def skip_in_loop(self, jobs=0, units=0):
        for _ in range(jobs):
            s = self.next_job()
            self.JD[s].add(3)
            self.JO[s].add(3)
        for _ in range(units):
            b = self.next_unit()
            self.TD[b].add(1)
            self.TO[b].add(1)

    def wait_done(self):
        for t in self.JD + self.TD:
            t.wait(self.eng)

    def wait_all_out(self):
        for t in self.JO + self.TO:
            t.wait(self.eng)


def build(nc, A, out):
    ctx = ExitStack()
    with ctx:
        def sb(name, shape, dt=F32):
            return ctx.enter_context(nc.sbuf_tensor(name, shape, dt))

        names = ["job_done0", "job_done1", "job_out0", "job_out1", "unit_done0", "unit_done1", "unit_out0", "unit_out1",
                 "w_full0", "w_full1", "consts_in", "edges_in", "x_in", "small_in", "wu_in", "dve_chain", "tiles_hot",
                 "bounds_ready", "pair_hot0", "pair_hot1", "pair_used0", "pair_used1", "deg_ready", "deg_root", "scaled",
                 "c_ready", "c_saved", "c_back", "x_done", "x_saved", "x_back", "var_ready", "root_ready", "row_ready",
                 "affine_act", "affine_dve", "g_ready", "wt_in", "q_staged", "v_staged", "norm_ready", "max_ready", "att_ready", "e_ready", "p_ready",
                 "alpha_ready", "h_staged", "lg_ready", "lg_exp", "chosen", "one_hot", "route_ready",
                 "stream_ready", "stream_saved", "expert_w0", "expert_w1", "expert_done", "x_gathered", "x_turned", "member_ready",
                 "xt_ready", "down_done0", "down_done1", "z_ready", "up_done0", "up_done1", "y_ready", "y_saved", "y_free", "y_filled", "y_gathered0", "y_gathered1", "y_gathered2", "y_gathered3",
                 "y_gathered4", "rows_in", "shift_ready", "normal_ready", "out_tile", "out_stored"]
        S = {n: ctx.enter_context(nc.semaphore(n)) for n in names}
        Tally.passed = {e: ctx.enter_context(nc.semaphore(f"passed_{n}")) for e, n in (
            (mybir.EngineType.Activation, "act"), (mybir.EngineType.DVE, "dve"), (mybir.EngineType.PE, "pe"),
            (mybir.EngineType.Pool, "pool"))}

        X = sb("X", [P, TT * D])
        TC = sb("TC", [P, TT * D])
        F0 = sb("F0", [P, KD * N])
        F1 = sb("F1", [P, KD * N])
        R = sb("R", [P, TT * N])
        xt = X[0:TL, :].rearrange("p (t d) -> p t d", t=TT)
        t0 = TC[0:TL, :].rearrange("p (t d) -> p t d", t=TT)
        cnt = TC[:, :].bitcast(U16)[0:TL, 0:TT * N].rearrange("p (t n) -> p t n", t=TT)
        f0 = F0[:, :].rearrange("p (k n) -> p k n", k=KD)
        f1 = F1[:, :].rearrange("p (k n) -> p k n", k=KD)
        r10 = R[0:TL, :].rearrange("p (t n) -> p t n", t=TT)
        rk = R[:, 0:KD * N].rearrange("p (k n) -> p k n", k=KD)
        rz = R[:, 0:4 * N].rearrange("p (k n) -> p k n", k=4)
        wadj = [f[0:TL, 0:5 * N].rearrange("p (t n) -> p t n", t=5) for f in (F0, F1)]
        c_all = TC[:, :].bitcast(U16)[0:TL, 0:TT * N]
        wt = R[:, 0:2 * KD * D]
        masks = R[:, KD * N:].bitcast(BF16)[:, 0:5 * N].rearrange("p (k n) -> p k n", k=5)
        free = KD * N + 5 * N // 2
        vst = R[0:TL, free:free + TT * P].rearrange("p (t d) -> p t d", t=TT)
        diag = [R[0:TL, free + TT * P + h * TL:free + TT * P + (h + 1) * TL] for h in range(2)]
        wsl = [sb(f"weights{s}", [P, KE * P]) for s in range(2)]
        ys = [sb(f"ystage{s}", [P, N]) for s in range(2)]
        hs = [sb(f"hstage{s}", [P, TT * P]) for s in range(2)]
        hst = [h[0:TL, :].rearrange("p (t d) -> p t d", t=TT) for h in hs]
        kst = sb("kstage", [P, N])
        gstage = [kst[:, :], TC[:, TT * N // 2:TT * N // 2 + N]]
        cols = sb("cols", [P, NCOL])
        ident = sb("ident", [P, P])
        iota = sb("iota", [P, N], F16)
        wd = sb("wd", [P, KD, BOT])
        w3 = sb("w3", [P, 2, 4])
        wm2 = sb("wm2", [P, 3, 8])
        dif = kst[0:4, 0:2 * P].rearrange("p (k c) -> p k c", k=2)
        small = sb("small", [P, 800])
        used = [0]

        def piece(n):
            used[0] += n
            assert used[0] <= 800
            return small[:, used[0] - n:used[0]]

        mv, var, rs, rs2 = piece(2 * TT), piece(TT), piece(TT), piece(TT)
        mvt = mv[0:TL, :].rearrange("p (t c) -> p t c", c=2)
        dinv, deg, g4, gbias = piece(TT), piece(TT), piece(4), piece(2)
        deg3, g43 = piece(3 * TT), piece(3 * 4)
        mm3, nb, rsum, rinv = piece(8), piece(2), piece(8), piece(2)
        ad, mneg, zs = piece(TT), piece(2), piece(4)
        qs = [[piece(TL) for _ in range(2)] for _ in range(2)]
        stat = small[0:TL, used[0] - 4 * TL:used[0] - 4 * TL + 18 * TT]
        stats = stat.rearrange("p (t h c) -> p t h c", t=TT, h=3)
        lg, pr, t8, oh = qs[0][0][:, 0:80], qs[0][1][:, 0:80], qs[1][0][:, 0:80], qs[1][1][:, 0:80]
        att_v = qs[1][1][:, 80:80 + 4 * KD]
        m10 = piece(40)
        ones = piece(16)

        jp = [ctx.enter_context(nc.psum_tensor(f"job_banks{s}", [P, 3, 512], F32)) for s in range(2)]
        up = [ctx.enter_context(nc.psum_tensor(f"unit_bank{b}", [P, 512], F32)) for b in range(2)]

        c_dram = nc.dram_tensor("c_dram", [TL, TT * N], U16, kind="Internal").ap()
        x_dram = nc.dram_tensor("x_dram", [TL, TT * D], F32, kind="Internal").ap()
        stream_dram = nc.dram_tensor("stream_dram", [N, D], F32, kind="Internal").ap()
        y_dram = nc.dram_tensor("y_dram", [SLOTS * P, D], F32, kind="Internal").ap()

        w_down = [R[:, 0:KE * D], F0[:, 0:KE * D]]
        w_up = [R[:, KE * D:2 * KE * D], F1[:, 0:KE * D]]
        x_rows = wsl[1][:, 0:D]
        x_feat = kst[:, 0:KD * P]
        z_feat = wsl[0][:, 0:KE * P]
        y_rows = ys[0][:, 0:D]
        before = hs[0][0:TL, D:D + 2 * TL]
        token_no = hs[1][0:TL, D:D + TT]
        places = hs[1][0:TL, D + 16:D + 16 + CHOICES * TT].bitcast(I32)
        first_slot = hs[1][0:1, D + 40:D + 40 + EXPERTS + 2].bitcast(I32)
        members = hs[1][:, D + 64:D + 64 + SLOTS + 2].bitcast(I32)
        member = hs[1][:, D + 100:D + 101].bitcast(I32)
        hot_row = [f[0:TL, KE * D:KE * D + TT * P // 2].bitcast(F16).rearrange("p (t c) -> p t c", t=TT) for f in (F0, F1)]
        hot_slot = ys[1][0:TL, 0:CHOICES * TT * (SLOTS + 2) // 2].bitcast(F16).rearrange("p (i s) -> p i s", i=CHOICES * TT)
        y_got = [(R if i < 16 else F0)[0:TL, i % 16 * D:i % 16 * D + D] for i in range(CHOICES * TT)]

        def col(name, k=0, n=1, rows=P):
            at = COL[name] + k
            return cols[0:rows, bass.ds(at, n)]

        def att_pair(layer, k):
            at = COL[f"as{layer + 1}"] + k
            return cols[:, at:at + KD + 1:KD]

        def tok(t, n=TL):
            return bass.ds(t * TL, n)

        src_i = ys[0][:, :].bitcast(I32)[0:TL, 0:ET]
        dst_i = ys[0][:, :].bitcast(I32)[0:TL, ET:2 * ET]
        ew = ys[0][0:TL, 2 * ET:3 * ET]
        srcf = ys[0][0:TL, 3 * ET:4 * ET]
        dstf = ys[0][0:TL, 4 * ET:5 * ET]
        wpart = [ys[0][0:TL, (5 + k) * ET:(6 + k) * ET] for k in range(2)]
        wthird = ys[1][0:TL, 0:ET]
        wb = ys[1][0:TL, ET:2 * ET].bitcast(BF16)[:, 0:ET]
        reached = R[0:TL, 0:(TT + 1) * ET // 2].bitcast(BF16)
        in_bucket = R[0:TL, 1000:1000 + TT * ET // 2].bitcast(BF16)
        one16 = R[0:TL, 2000:2001].bitcast(BF16)[:, 0:1]
        held_all, tmp_all = F1[0:1, 0:3 * ET], F1[0:1, 3 * ET:6 * ET]
        bf = hs[0][0:1, 0:64]
        bounds = hs[0][0:1, 64:128].bitcast(I32)
        hot_src = [hs[s][:, :].bitcast(BF16)[0:TL, 256:256 + N] for s in range(2)]
        hot_dst = [hs[s][:, :].bitcast(BF16)[0:TL, 1600:1600 + 4 * TL].rearrange("p (q d) -> p q d", q=4)
                   for s in range(2)]
        zrow = kst[0:1, 560:780].bitcast(BF16)
        tq = kst[0:1, 1000:1250]

        def view(bank, n, width, rows=TL):
            return bank[0:rows, :].rearrange("p (j c) -> p j c", j=4)[:, 0:n, 0:width]

        block = ctx.enter_context(nc.Block())

        @block.sync
        def _(sp):
            E = Side(sp, S)

            weighted = [0, 0]

            def load(src, kt, back=None):
                s = E.next_job()
                if back is None:
                    E.JD[s].wait(sp)
                else:
                    E.JD[s].wait(sp, back=back[s])
                E.W[s].inc(sp.dma_start(wsl[s][:, 0:kt * P], src), 16)
                E.JD[s].add(3)
                E.JO[s].add(3)

            def stream(name, first=0, n=None):
                jobs, kt = STREAMED[name]
                n = n or jobs
                looped = (n - 2) // 2 * 2 if n >= 6 else 0
                back = [t.count - w for t, w in zip(E.JD, weighted)]
                for j in range(first, first + min(2, n)):
                    load(A[name][j], kt, back)
                if looped:
                    with E.loop(looped // 2, jobs=2, weights=2) as i:
                        load(A[name][bass.ds(i * 2 + (first + 2), 1)].rearrange("o p f -> p (o f)"), kt)
                        load(A[name][bass.ds(i * 2 + (first + 3), 1)].rearrange("o p f -> p (o f)"), kt)
                for j in range(first + 2 + looped, first + n):
                    load(A[name][j], kt)
                weighted[:] = [t.count for t in E.JD]

            for dst, name in ((src_i, "src"), (dst_i, "dst"), (ew, "ew"), (iota[:, :], "iota"), (tq[:, 0:ET], "pairno")):
                sp.dma_start(dst, A[name]).then_inc(S["edges_in"], 16)
            sp.dma_start(ident[:, :], A["ident"]).then_inc(S["consts_in"], 16)
            sp.dma_start(cols[:, :], A["cols"]).then_inc(S["consts_in"], 16)
            sp.dma_start(xt, A["x"]).then_inc(S["x_in"], 16)
            for dst, name in ((wd[:, :, :], "wd"), (w3[:, :, :], "w3"), (wm2[:, :, :], "wm2")):
                sp.dma_start(dst, A[name]).then_inc(S["small_in"], 16)
            E.skip("matrices", "w_transpose", "rows", "adapter")
            stream("w1")
            E.skip("pair", "pair")
            stream("w2")
            if BLOCKS > 1:
                E.skip("rows")
                for name in ("r_in", "r_o1", "r_o2"):
                    stream(name)
                E.skip("logits", "masks")
                stream("wqkv")
                E.skip("attention")
                stream("wo")
                E.skip("rows")
                stream("fc1")
                stream("fc2")
                E.skip("rows")
                stream("lra_down")
                stream("lra_up")
            if BLOCKS > 2:
                E.skip("rows")
                for name in ("gat_w1", "gat_w2"):
                    E.skip("att")
                    stream(name)
                    E.skip("agg0")
            if BLOCKS > 3:
                def expert_weights(h, dst_src):
                    for dst, src in dst_src:
                        sp.dma_start(dst, src).then_inc(S[f"expert_w{h}"], 16)

                def down(e):
                    return A["down"][bass.ds(e, 1)].rearrange("o p f -> p (o f)")

                def up_of(e):
                    return A["up"][bass.ds(e, 1)].rearrange("o p f -> p (o f)")

                aggregated = [t.count for t in E.JD]
                E.skip("rows")
                stream("m_w1", 0, 2)
                for slot, n in enumerate(aggregated):
                    sp.wait_ge(S[f"job_done{slot}"], n)
                expert_weights(0, [(w_down[0], A["down"][0]), (w_up[0], A["up"][0])])
                stream("m_w1", 2, 1)
                E.skip("gates")
                for t in E.JD:
                    t.wait(sp)
                expert_weights(1, [(w_down[1], A["down"][1]), (w_up[1], A["up"][1])])
                sp.wait_ge(S["route_ready"], 1)
                sp.wait_ge(S["stream_saved"], 16)
                empty = sp.value_load(first_slot[0:1, EXPERTS + 1:EXPERTS + 2], min_val=1, max_val=SLOTS - 1)
                with sp.Fori(1, empty + 1) as k:
                    sp.dma_start(y_dram[bass.ds(SLOTS * P - k * P, P), :], stream_dram[0:P, :]).then_inc(S["y_filled"], 16)
                with sp.Fori(1, EXPERTS // 2) as i:
                    for h in range(2):
                        sp.wait_ge(S["expert_done"], i * 2 + (h - 1))
                        expert_weights(h, [(w_down[h], down(i * 2 + h)), (w_up[h], up_of(i * 2 + h))])
                with sp.Fori(0, TT) as t:
                    sp.wait_ge(S["out_tile"], t + 1)
                    sp.dma_start(out[:, bass.ds(t, 1), :], xt[:, bass.ds(t, 1), :]).then_inc(S["out_stored"], 16)
                sp.wait_ge(S["out_stored"], 16 * TT)
            else:
                sp.wait_ge(S["x_done"], BLOCKS)
                sp.dma_start(out, xt).then_inc(S["out_stored"], 16)
                sp.wait_ge(S["out_stored"], 16)

        @block.tensor
        def _(pe):
            E = Side(pe, S)

            def job(lhs, kts, rhs, m=P, weights=True):
                s = E.next_job()
                if weights:
                    E.W[s].add(16)
                    E.W[s].wait(pe)
                E.JO[s].wait(pe)
                for c, (at, n) in enumerate(CH):
                    for k in range(kts):
                        mm = nc.tensor.matmul(jp[s][0:m, c, 0:n], lhs(s, k), rhs(k, at, n), start=(k == 0),
                                              stop=(k == kts - 1))
                    E.JD[s].inc(mm)
                E.JO[s].add(3)
                return s

            def unit(blocks):
                b = E.next_unit()
                E.TO[b].wait(pe)
                for o, x in blocks:
                    k = x.shape[0]
                    tr = nc.tensor.transpose(o(up[b]), x, ident[0:k, 0:k])
                E.TD[b].inc(tr)
                E.TO[b].add(1)

            def on(f):
                return lambda k, at, n: f[:, k, bass.ds(at, n)]

            def slot_w(s, k):
                return wsl[s][:, bass.ts(k, P)]

            def back(s, stage=ys):
                for g, n in GROUPS:
                    unit([(lambda bank, j=j: bank[0:TL, bass.ts(j, P)], stage[s][:, tok(g + j)]) for j in range(n)])

            def square(s):
                for g, n in GROUPS:
                    unit([(lambda bank, j=j: bank[0:TL, j * P:j * P + TL], ys[s][0:TL, tok(g + j)]) for j in range(n)])

            rows = Tally(S["row_ready"])

            def rows_to_features():
                with E.loop(TT // 2, jobs=2, extra=[(rows, 2)]):
                    for y in range(2):
                        s = E.next_job()
                        rows.add(1)
                        rows.wait(pe)
                        E.JO[s].wait(pe)
                        for j in range(KD):
                            tr = nc.tensor.transpose(jp[s][:, j // 3, j % 3 * P:j % 3 * P + TL], ys[y][0:TL, bass.ts(j, P)],
                                                     ident[0:TL, 0:TL])
                        E.JD[s].inc(tr, 3)
                        E.JO[s].add(3)
                E.wait_all_out()

            def jobs(n, kts, f):
                looped = n // 2 * 2 if n >= 4 else 0
                if looped:
                    with E.loop(looped // 2, jobs=2, weights=2):
                        for _ in range(2):
                            job(slot_w, kts, on(f))
                for _ in range(n - looped):
                    job(slot_w, kts, on(f))
                E.wait_all_out()

            def jobs_back(kts, f):
                with E.loop(3, jobs=2, weights=2, units=6):
                    for s in [job(slot_w, kts, on(f)) for _ in range(2)]:
                        E.JO[s].wait(pe)
                        back(s)
                E.wait_all_out()

            def agg():
                return job(lambda s, k: hst[s][:, k, :], TT, lambda k, at, n: r10[:, k, bass.ds(at, n)], weights=False)

            pe.wait_ge(S["consts_in"], 32)
            pe.wait_ge(S["tiles_hot"], 1)
            for g, n in BUCKETS:
                b = E.next_unit()
                E.TO[b].wait(pe)
                E.TD[b].inc(nc.tensor.matmul(up[b][0:1, 0:n * ET], one16, in_bucket[:, g * ET:(g + n) * ET],
                                             start=True, stop=True))
                E.TO[b].add(1)
            pe.wait_ge(S["bounds_ready"], 1)
            with E.loop(TT, jobs=2) as b:
                first = pe.value_load(bounds[0:1, bass.ds(b + 30, 1)], min_val=1, max_val=TT * EQ)
                end = pe.value_load(bounds[0:1, bass.ds(b + 40, 1)], min_val=2, max_val=TT * EQ + 1)
                for s in range(2):
                    E.JO[s].wait(pe)
                    for c, (at, n) in enumerate(CH):
                        nc.tensor.matmul(jp[s][0:TL, c, 0:n], zrow[:, 0:TL], zrow[:, 0:n], start=True, stop=False,
                                         skip_group_check=True)
                with pe.Fori(first, end) as turn:
                    for s in range(2):
                        pe.wait_ge(S[f"pair_hot{s}"], turn)
                        for k in range(4):
                            for c, (at, n) in enumerate(CH):
                                mm = nc.tensor.matmul(jp[min(k, 1)][0:TL, c, 0:n], hot_dst[s][:, k, :],
                                                      hot_src[s][:, bass.ds(at, n)], start=False, stop=False,
                                                      skip_group_check=True)
                        mm.then_inc(S[f"pair_used{s}"], 1)
                for s in range(2):
                    for c, (at, n) in enumerate(CH):
                        E.JD[s].inc(nc.tensor.matmul(jp[s][0:TL, c, 0:n], zrow[:, 0:TL], zrow[:, 0:n], start=False,
                                                     stop=True, skip_group_check=True))
                    E.JO[s].add(3)
            E.job += 2 * (TT - 1)
            scaled = Tally(S["scaled"])
            with E.loop(TT // 2, jobs=2, extra=[(scaled, 2)]):
                for y in range(2):
                    s = E.next_job()
                    scaled.add(1)
                    scaled.wait(pe)
                    E.JO[s].wait(pe)
                    for j in range(TT):
                        tr = nc.tensor.transpose(jp[s][0:TL, j // 4, j % 4 * P:j % 4 * P + TL], ys[y][0:TL, tok(j)], ident[0:TL, 0:TL])
                    E.JD[s].inc(tr, 3)
                    E.JO[s].add(3)
            rows_to_features()
            pe.wait_ge(S["small_in"], 48)
            job(lambda s, k: wd[:, k, :], KD, on(f0), m=BOT, weights=False)
            E.wait_all_out()
            pe.wait_ge(S["wu_in"], 32)
            for m in range(KD):
                job(lambda s, k: hs[1][0:BOT, bass.ts(m, P)], 1, lambda k, at, n: hs[0][0:BOT, bass.ds(at, n)],
                    weights=False)
            E.wait_all_out()
            for _ in range(2):
                job(slot_w, KD, on(f1))
            for _ in range(2):
                for s in (E.slot(0), E.slot(1)):
                    E.JO[s].wait(pe)
                    back(s)
                E.wait_all_out()
                for _ in range(2):
                    agg()
            E.wait_all_out()
            jobs_back(2, f0)
            if BLOCKS > 1:
                rows_to_features()
                pe.wait_ge(S["affine_act"], 1)
                pe.wait_ge(S["affine_dve"], 1)
                jobs(4, KD, f1)
                pe.wait_ge(S["g_ready"], 1)
                with E.loop(2, jobs=2, weights=2, units=2):
                    for _ in range(2):
                        s, b = E.slot(), E.next_unit()
                        E.W[s].add(16)
                        E.W[s].wait(pe)
                        E.TO[b].wait(pe)
                        for k in range(4):
                            mm = nc.tensor.matmul(up[b][:, 0:1], slot_w(s, 4 + k), g4[:, k:k + 1], start=(k == 0), stop=(k == 3))
                        E.TD[b].inc(mm)
                        E.TO[b].add(1)
                        job(slot_w, 4, on(rz), weights=False)
                E.wait_all_out()
                jobs(2, 4, f1)
                job(lambda s, k: w3[:, k, :], 2, on(rz), m=4, weights=False)
                E.wait_all_out()
                for k in range(2):
                    job(lambda s, _: dif[:, k, :], 1, lambda _, at, n: hs[0][0:4, bass.ds(at, n)], weights=False)
                pe.wait_ge(S["affine_act"], 2)
                pe.wait_ge(S["affine_dve"], 2)
                with E.loop(6, jobs=2, weights=2):
                    for _ in range(2):
                        job(slot_w, KD, on(f0))
                jobs_back(KD, f0)
                sl = [E.slot(0), E.slot(1)]
                q_in, v_in, norm = Tally(S["q_staged"]), Tally(S["v_staged"]), Tally(S["norm_ready"])

                def scores(h, ts, c, hp):
                    s = sl[h]
                    if c == 0:
                        E.JO[s].wait(pe)
                        E.JO[s].add(3)
                    at, n = CH[c]
                    E.JD[s].inc(nc.tensor.matmul(jp[s][0:TL, c, 0:n], qs[ts][h], rk[:, bass.ds(hp, 1), bass.ds(at, n)],
                                                 start=True, stop=True))

                def two_tiles(hp, pair_ends=False, ends=False):
                    for u in range(4):
                        h, nts = u % 2, (u // 2 + 1) % 2
                        ahead = not (ends and u >= 2)
                        if ahead and h == 0:
                            q_in.add(2)
                            q_in.wait(pe)
                        norm.add(1)
                        norm.wait(pe)
                        for c, (g, n) in enumerate(GROUPS):
                            b = c % 2
                            E.TO[b].wait(pe)
                            for j in range(n):
                                mm = nc.tensor.matmul(up[b][0:TL, j * P:j * P + TL], ys[h][0:TL, tok(g + j)], diag[h],
                                                      start=True, stop=True)
                            E.TD[b].inc(mm)
                            E.TO[b].add(1)
                            if ahead:
                                scores(h, nts, c, hp + 1 if pair_ends and u >= 2 else hp)
                        E.TO[1].wait(pe)
                        E.TO[0].wait(pe)
                        v_in.wait(pe)
                        for k in range(TT):
                            mm = nc.tensor.matmul(up[1][:, 0:TL], vst[:, k, :], hst[h][:, k, 0:TL], start=(k == 0), stop=(k == TT - 1))
                        E.TD[1].inc(mm)
                        E.TO[1].add(1)

                def pair(hp, ends):
                    v_in.add(1)
                    with repeat(pe, 4, list(zip(tallies, [6, 6, 6, 6, 8, 8, 8, 8, 4, 0, 4]))):
                        two_tiles(hp)
                    two_tiles(hp, True, ends)

                tallies = [E.JD[0], E.JD[1], E.JO[0], E.JO[1], E.TD[0], E.TO[0], E.TD[1], E.TO[1], q_in, v_in, norm]
                E.wait_all_out()
                q_in.add(2)
                q_in.wait(pe)
                for h in range(2):
                    for c in range(3):
                        scores(h, 0, c, 0)
                with repeat(pe, HP - 1, list(zip(tallies, [30, 30, 30, 30, 40, 40, 40, 40, 20, 1, 20]))) as hp:
                    pair(hp, False)
                pair(HP - 1, True)
                E.wait_all_out()
                jobs_back(KD, f0)
                rows_to_features()
                pe.wait_ge(S["affine_act"], 3)
                pe.wait_ge(S["affine_dve"], 3)
                jobs(3, KD, f0)
                jobs_back(3, f1)
                rows_to_features()
                jobs(6, KD, f0)
                jobs_back(KD, f1)
            if BLOCKS > 2:
                pe.wait_ge(S["wt_in"], 16)
                for layer in range(2):
                    b = E.next_unit()
                    E.TO[b].wait(pe)
                    for m in range(KD):
                        for k in range(KD):
                            mm = nc.tensor.matmul(up[b][:, 2 * m:2 * m + 2], wt[:, (layer * KD + k) * D + m * P:(layer * KD + k) * D + (m + 1) * P],
                                                  att_pair(layer, k), start=(k == 0), stop=(k == KD - 1))
                    E.TD[b].inc(mm)
                    E.TO[b].add(1)
                rows_to_features()
                staged, alpha = Tally(S["h_staged"]), Tally(S["alpha_ready"])
                for layer in range(2):
                    pe.wait_ge(S["att_ready"], layer + 1)
                    job(lambda s, k: att_v[:, 2 * (layer * KD + k):2 * (layer * KD + k) + 2], KD, on(f0), m=2, weights=False)
                    E.wait_all_out()
                    job(lambda s, k: hs[0][0:2, 0:P], 1, lambda k, at, n: hs[1][0:2, bass.ds(at, n)], weights=False)
                    unit([(lambda bank, t=t: bank[0:TL, 2 * t:2 * t + 2], hs[1][0:2, tok(t)]) for t in range(TT)])

                    def job_and_tiles():
                        job(slot_w, KD, on(f0))
                        for s in range(2):
                            alpha.add(1)
                            alpha.wait(pe)
                            square(s)

                    with E.loop(2, jobs=2, weights=2, units=12, extra=[(alpha, 4)]):
                        job_and_tiles()
                        job_and_tiles()
                    job_and_tiles()
                    job(slot_w, KD, on(f0))
                    E.wait_all_out()
                    with E.loop(3, jobs=2, units=12 if layer else 6, extra=[(staged, 2)]):
                        for h in range(2):
                            staged.add(1)
                            staged.wait(pe)
                            back(E.slot(h), gstage)
                        E.TO[0].wait(pe)
                        E.TO[1].wait(pe)
                        done = [agg() for _ in range(2)]
                        if layer:
                            for s in done:
                                E.JO[s].wait(pe)
                                back(s)
                    E.wait_all_out()
            if BLOCKS > 3:
                rows_to_features()
                jobs(3, KD, f0)
                job(lambda s, k: wm2[:, k, :], 3, on(f1), m=8, weights=False)
                E.wait_all_out()
                unit([(lambda bank, t=t: bank[0:TL, t * 8:t * 8 + 8], ys[0][0:8, tok(t)]) for t in range(TT)])
                pe.wait_ge(S["chosen"], 1)
                pe.wait_ge(S["rows_in"], 64)
                E.TO[0].wait(pe)
                E.TO[1].wait(pe)
                nc.tensor.matmul(up[1][0:TL, 0:80], before[:, 0:TL], oh[0:TL, :], start=True, stop=True)
                nc.tensor.matmul(up[1][0:TL, 80:160], before[:, TL:2 * TL], oh[0:TL, :], start=True, stop=True).then_inc(
                    S["chosen"], 1)
                pe.wait_ge(S["one_hot"], 1)
                for i in range(CHOICES * TT):
                    mm = nc.tensor.matmul(up[0][:, 0:SLOTS + 2], hot_row[i // TT][:, i % TT, :], hot_slot[:, i, :],
                                          start=(i == 0), stop=(i == CHOICES * TT - 1))
                mm.then_inc(S["one_hot"], 1)

                def turn_rows():
                    for k in range(KD):
                        o = jp[0][:, 2, k * P:(k + 1) * P] if k < 4 else jp[1][:, 2, (k - 4) * P:(k - 3) * P]
                        tr = nc.tensor.transpose(o, x_rows[:, bass.ts(k, P)], ident[:, :])
                    tr.then_inc(S["x_turned"], 1)

                pe.wait_ge(S["x_gathered"], 16)
                turn_rows()
                pe.wait_ge(S["route_ready"], 1)
                with pe.Fori(0, EXPERTS // 2) as i:
                    for h in range(2):
                        first = pe.value_load(first_slot[0:1, bass.ds(i * 2 + h, 1)], min_val=1, max_val=SLOTS - 1)
                        end = pe.value_load(first_slot[0:1, bass.ds(i * 2 + h + 1, 1)], min_val=2, max_val=SLOTS)
                        pe.wait_ge(S[f"expert_w{h}"], i * 32 + 32)
                        pe.sem_inc(Tally.passed[pe.engine], 1)
                        with pe.Fori(first, end) as s:
                            pe.wait_ge(S["xt_ready"], s)
                            for j in range(KE):
                                for k in range(KD):
                                    mm = nc.tensor.matmul(jp[0][:, j // 4, j % 4 * P:(j % 4 + 1) * P],
                                                          w_down[h][:, bass.ts(j * KD + k, P)], x_feat[:, bass.ts(k, P)],
                                                          start=(k == 0), stop=(k == KD - 1))
                                if j % 4 == 3:
                                    mm.then_inc(S[f"down_done{j // 4}"], 1)
                            pe.wait_ge(S["x_gathered"], s * 16 + 16)
                            turn_rows()
                            pe.wait_ge(S["z_ready"], s)
                            pe.wait_ge(S["y_ready"], s)
                            for c in range(2):
                                for k in range(KE):
                                    mm = nc.tensor.matmul(jp[1][:, c, 0:D // 2], z_feat[:, bass.ts(k, P)],
                                                          w_up[h][:, bass.ds(k * D + c * (D // 2), D // 2)],
                                                          start=(k == 0), stop=(k == KE - 1))
                                mm.then_inc(S[f"up_done{c}"], 1)
                        pe.wait_ge(S["up_done1"], end)
                        pe.sem_inc(S["expert_done"], 1)

        @block.scalar
        def _(act):
            E = Side(act, S)

            def take(write):
                s = E.next_job()
                for c, (at, n) in enumerate(CH):
                    E.wait_chunk(s)
                    E.JO[s].inc(write(s, jp[s][:, c, 0:n], at, n))

            def take_unit(write):
                b = E.next_unit()
                E.wait_unit(b)
                E.TO[b].inc(write(up[b]))
                return b

            def move(o, i, func=ACT.Copy, **kw):
                return nc.scalar.activation(o, i, func, **kw)

            def rows_out(f):
                with E.loop(TT // 2, jobs=2) as i:
                    for h in range(2):
                        s = E.next_job()
                        E.JD[s].add(3)
                        E.JD[s].wait(act, alone=True)
                        E.JO[s].inc(move(f[:, 0:KD, bass.ds(i * (2 * TL) + h * TL, TL)].rearrange("p (b j) c -> p b j c", b=2),
                                         jp[s][:, 0:2, 0:3 * P].rearrange("p b (j c) -> p b j c", j=3)[:, :, :, 0:TL]), 3)

            def squares_out():
                for s in range(2):
                    for g, n in GROUPS:
                        take_unit(lambda bank: move(r10[:, g:g + n, bass.ds(squares_out.i * (2 * TL) + s * TL, TL)],
                                                    view(bank, n, TL)))

            def root(k):
                act.wait_ge(S["var_ready"], k)
                nc.scalar.activation(var[0:TL, :], var[0:TL, :], ACT.Sqrt).then_inc(S["root_ready"], 1)

            def row(f, m, at, n):
                return f[:, m, bass.ds(at, n)] if isinstance(m, int) else f[:, bass.ds(m, 1), bass.ds(at, n)]

            def to_rows(f, n, func, name=None, sums=None):
                def one(m):
                    kw = {"bias": col(name, m)} if name else {}
                    if sums is None:
                        take(lambda s, bank, at, w: move(row(f, m, at, w), bank, func, **kw))
                    else:
                        take(lambda s, bank, at, w: move(row(f, m, at, w), bank, func, **kw,
                                                         accum_out=sums[:, bass.ds(m * 3 + at // CH[0][1], 1)]))
                looped = n // 2 * 2 if n >= 4 else 0
                if looped:
                    with E.loop(looped // 2, jobs=2) as i:
                        one(i * 2)
                        one(i * 2 + 1)
                for m in range(looped, n):
                    one(m)

            def staged(func, name, m):
                kw = {"bias": col(name, m)} if name else {}
                take(lambda s, bank, at, w: move(ys[s][:, bass.ds(at, w)], bank, func, **kw))

            def staged_pairs(name):
                with E.loop(3, jobs=2, units=6) as i:
                    for h in range(2):
                        staged(ACT.Identity if name else ACT.Copy, name, i * 2 + h)
                    E.skip_in_loop(units=6)

            act.wait_ge(S["consts_in"], 32)
            E.skip("counts")
            for half in range(2):
                w5 = wadj[half]
                with E.loop(5, jobs=2) as b:
                    take(lambda s, bank, at, n: move(cnt[:, bass.ds(b + 5 * half, 1), bass.ds(at, n)], bank[0:TL, :]))
                    take(lambda s, bank, at, n: move(w5[:, bass.ds(b, 1), bass.ds(at, n)], bank[0:TL, :], accum_out=deg3[
                        0:TL, bass.ds(b * 3 + (15 * half + at // CH[0][1]), 1)]))
            act.wait_ge(S["deg_ready"], 1)
            nc.scalar.activation(dinv[0:TL, :], deg[0:TL, :], ACT.Sqrt).then_inc(S["deg_root"], 1)
            with E.loop(TT // 2, jobs=2) as i:
                for h in range(2):
                    s = E.next_job()
                    E.JD[s].add(3)
                    E.JD[s].wait(act, alone=True)
                    at = bass.ds(i * (2 * TL) + h * TL, TL)
                    E.JO[s].inc(move(r10[:, 0:8, at].rearrange("p (b j) c -> p b j c", b=2),
                                     jp[s][0:TL, 0:2, :].rearrange("p b (j c) -> p b j c", j=4)[:, :, :, 0:TL]), 2)
                    E.JO[s].inc(move(r10[:, 8:TT, at], jp[s][0:TL, 2, 0:2 * P].rearrange("p (j c) -> p j c", j=2)[:, :, 0:TL]))
            root(1)
            act.wait_ge(S["scaled"], TT)
            rows_out(f0)
            take(lambda s, bank, at, n: move(hs[0][0:BOT, bass.ds(at, n)], bank[0:BOT, :], ACT.Relu, bias=col("bd", rows=BOT)))
            E.skip_in_loop(jobs=6)
            for m in range(2):
                staged(ACT.Copy, None, m)
            E.skip("pair_back")
            for m in range(2):
                staged(ACT.Relu, "gb1", m)
            E.skip("pair_back")
            to_rows(f0, 2, ACT.Copy)
            staged_pairs("gb2")
            if BLOCKS > 1:
                root(2)
                root(3)
                rows_out(f0)
                for t in E.JO:
                    t.wait(act)
                for name in ("r", "l1"):
                    for k in range(4, KD):
                        a = move((f1 if name == "r" else f0)[:, k, :], f0[:, k, :], ACT.Identity, bias=col(f"{name}_b", k),
                                 scale=col(f"{name}_g", k))
                    a.then_inc(S["affine_act"], 1)
                to_rows(rz, 4, ACT.Gelu, "r_in_b", sums=g43)
                with E.loop(2, jobs=2, units=2) as i:
                    for h in range(2):
                        b = take_unit(lambda bank: move(gbias[:, h:h + 1], bank[:, 0:1], ACT.Identity, bias=col("r_o1_b", i * 2 + h)))
                        E.TO[b].wait(act)
                        take(lambda s, bank, at, n: move(f1[:, bass.ds(i * 2 + h, 1), bass.ds(at, n)], bank, ACT.Gelu,
                                                         bias=gbias[:, h:h + 1]))
                to_rows(rz, 2, ACT.Gelu, "r_o2_b")
                take(lambda s, bank, at, n: move(hs[0][0:4, bass.ds(at, n)], bank[0:4, :], ACT.Identity, bias=col("r_o3_b", rows=4)))
                E.skip("masks")
                to_rows(f1, 6, ACT.Identity, "bq")
                to_rows(rk, 6, ACT.Identity, "bk")
                staged_pairs("bv")
                sl = [E.slot(0), E.slot(1)]
                peak = Tally(S["max_ready"])

                def exps(h):
                    s = sl[h]
                    peak.add(1)
                    peak.wait(act)
                    E.JD[s].add(3)
                    E.JO[s].inc(nc.scalar.activation(
                        ys[h][0:TL, 0:2 * CH[0][1]].rearrange("p (c n) -> p c n", c=2), jp[s][0:TL, 0:2, 0:CH[0][1]], ACT.Exp,
                        bias=nb[0:TL, h:h + 1], scale=HD ** -0.5, accum_out=rsum[0:TL, 2 * h:2 * h + 1]))
                    at, n = CH[2]
                    E.JO[s].inc(nc.scalar.activation(
                        ys[h][0:TL, at:at + n], jp[s][0:TL, 2, 0:n], ACT.Exp,
                        bias=nb[0:TL, h:h + 1], scale=HD ** -0.5, accum_out=rsum[0:TL, 2 * h + 1:2 * h + 2]), 2)

                def two_tiles(ends=False):
                    g, n = GROUPS[1]
                    for u in range(4):
                        E.TD[1].add(1)
                        E.TD[1].wait(act, alone=True)
                        E.TO[1].inc(move(hst[u % 2][:, g:g + n, 0:TL], view(up[1], n, TL)))
                        E.TD[1].add(1)
                        E.TO[1].add(1)
                        if not (ends and u >= 2):
                            exps(u % 2)

                def pair(ends):
                    with repeat(act, 4, list(zip(tallies, [6, 6, 6, 6, 8, 8, 4]))):
                        two_tiles()
                    two_tiles(ends)

                tallies = [E.JD[0], E.JD[1], E.JO[0], E.JO[1], E.TD[1], E.TO[1], peak]
                exps(0)
                exps(1)
                with repeat(act, HP - 1, list(zip(tallies, [30, 30, 30, 30, 40, 40, 20]))):
                    pair(False)
                pair(True)
                E.TD[0].add(40 * HP)
                E.TO[0].add(40 * HP)
                E.skip("pairs3_back")
                root(4)
                rows_out(f0)
                for t in E.JO:
                    t.wait(act)
                for k in range(4, KD):
                    a = move(f0[:, k, :], f0[:, k, :], ACT.Identity, bias=col("l2_b", k), scale=col("l2_g", k))
                a.then_inc(S["affine_act"], 1)
                to_rows(f1, 3, ACT.Gelu, "fc1_b")
                E.skip("pairs3_back")
                rows_out(f0)
                E.skip("pairs3")
                staged_pairs(None)
            if BLOCKS > 2:
                root(5)
                E.skip("vectors")
                rows_out(f0)
                e_in, p_out = Tally(S["e_ready"]), Tally(S["p_ready"])
                for layer in range(2):
                    take(lambda s, bank, at, n: move(hs[1][0:2, bass.ds(at, n)], bank[0:2, :]))
                    take(lambda s, bank, at, n: move(kst[:, bass.ds(at, n)], bank))
                    E.skip_in_loop(units=1)

                    def job_and_tiles(i):
                        for s in range(2):
                            e_in.add(1)
                            e_in.wait(act)
                            p_out.inc(nc.scalar.activation(hs[s][0:TL, 0:N], hs[s][0:TL, 0:N], ACT.Exp, bias=mneg[0:TL, s:s + 1]))
                        take(lambda s, bank, at, n: move(row(f1, i, at, n), bank))
                        squares_out.i = i
                        squares_out()

                    with E.loop(2, jobs=2, units=12, extra=[(e_in, 4), (p_out, 4)]) as i:
                        job_and_tiles(i * 2)
                        job_and_tiles(i * 2 + 1)
                    job_and_tiles(4)
                    take(lambda s, bank, at, n: move(row(f1, 5, at, n), bank))
                    with E.loop(3, jobs=2, units=12 if layer else 6) as i:
                        E.skip_in_loop(units=6)
                        for h in range(2):
                            if layer:
                                staged(ACT.Identity, "gat_b2", i * 2 + h)
                            else:
                                take(lambda s, bank, at, n: move(f0[:, bass.ds(i * 2 + h, 1), bass.ds(at, n)], bank, ACT.Relu,
                                                                 bias=col("gat_b1", i * 2 + h)))
                        if layer:
                            E.skip_in_loop(units=6)
            if BLOCKS > 3:
                root(6)
                rows_out(f0)
                to_rows(f1, 3, ACT.Gelu, "m_b1")
                take(lambda s, bank, at, n: move(ys[0][0:8, bass.ds(at, n)], bank[0:8, :], ACT.Identity, bias=col("m_b2", rows=8)))
                E.skip_in_loop(units=1)
                act.wait_ge(S["lg_ready"], 1)
                nc.scalar.activation(lg[0:TL, :], lg[0:TL, :], ACT.Exp).then_inc(S["lg_exp"], 1)
                act.wait_ge(S["route_ready"], 1)
                with act.Fori(0, EXPERTS // 2) as i:
                    for h in range(2):
                        first = act.value_load(first_slot[0:1, bass.ds(i * 2 + h, 1)], min_val=1, max_val=SLOTS - 1)
                        end = act.value_load(first_slot[0:1, bass.ds(i * 2 + h + 1, 1)], min_val=2, max_val=SLOTS)
                        with act.Fori(first, end) as s:
                            for c in range(2):
                                act.wait_ge(S[f"down_done{c}"], s)
                                act.sem_inc(Tally.passed[act.engine], 1)
                                for j in range(4 * c, 4 * c + 4):
                                    g = move(z_feat[:, bass.ts(j, P)], jp[0][:, c, j % 4 * P:(j % 4 + 1) * P], ACT.Gelu,
                                             bias=col("down_b", i * (2 * KE) + h * KE + j))
                            g.then_inc(S["z_ready"], 1)
                root(7)
                act.wait_ge(S["shift_ready"], 1)
                for t in range(TT):
                    move(t0[:, t, :], t0[:, t, :], ACT.Identity, bias=rs2[0:TL, t:t + 1], scale=rs[0:TL, t:t + 1]).then_inc(
                        S["normal_ready"], 1)

        @block.vector
        def _(dve):
            E = Side(dve, S)
            V = nc.vector
            chain = Tally(S["dve_chain"])

            def then(instruction):
                chain.inc(instruction)
                chain.wait(dve)

            def take(write):
                s = E.next_job()
                for c, (at, n) in enumerate(CH):
                    E.wait_chunk(s)
                    E.JO[s].inc(write(s, jp[s][:, c, 0:n], at, n))
                return s

            def take_unit(write):
                b = E.next_unit()
                E.wait_unit(b)
                E.TO[b].inc(write(up[b]))
                return b

            rows = Tally(S["row_ready"])

            def chunk_stats(src, i):
                for t in range(TT):
                    b = V.bn_stats(stats[:, t, bass.ds(i, 1), :], src[:, t, bass.ds(i * (2 * P), 2 * P)])
                return b

            def root_of(k):
                V.tensor_scalar(var[0:TL, :], var[0:TL, :], LN_EPS, None, ALU.add).then_inc(S["var_ready"], 1)
                dve.wait_ge(S["root_ready"], k)
                then(V.reciprocal(rs[0:TL, :], var[0:TL, :]))

            def stats_of(src, k, have=False):
                if not have:
                    E.wait_all_out()
                    for i in range(3):
                        b = chunk_stats(src, i)
                    then(b)
                for t in range(TT):
                    b = V.bn_aggr(mvt[:, t, :], stat[:, 18 * t:18 * t + 18])
                then(b)
                then(V.tensor_copy(var[0:TL, :], mvt[:, :, 1]))
                root_of(k)

            def normal(o, src, t):
                return V.tensor_scalar(o, src, mvt[:, t, 0:1], rs[0:TL, t:t + 1], ALU.subtract, ALU.mult)

            def stage_rows(src, norm=True, scale=rs):
                E.wait_done()
                with E.loop(TT // 2, jobs=2, extra=[(rows, 2)]) as i:
                    for s in range(2):
                        t = i * 2 + s
                        E.JD[E.slot()].wait(dve)
                        x = src[:, bass.ds(t, 1), :]
                        o = ys[s][0:TL, 0:D]
                        if norm:
                            m = mvt[:, bass.ds(t, 1), 0]
                            rows.inc(V.tensor_scalar(o, x, m, scale[0:TL, bass.ds(t, 1)], ALU.subtract, ALU.mult))
                        else:
                            rows.inc(V.tensor_copy(o, x))
                        E.skip_in_loop(jobs=1)

            def add_back(x):
                with E.loop(3, jobs=2, units=6, extra=[(chain, 1)]) as i:
                    E.skip_in_loop(jobs=2)
                    add_pair(x, i)
                    settled_stats(x, i)

            def add_pair(x, i):
                for h in range(2):
                    for g, n in GROUPS:
                        xs = x[:, g:g + n, bass.ds(i * (2 * P) + h * P, P)]
                        take_unit(lambda bank: V.tensor_tensor(xs, xs, view(bank, n, P), ALU.add))

            def settled_stats(x, i):
                for t in E.TO:
                    t.wait(dve, alone=True)
                then(chunk_stats(x, i))

            for b in range(2):
                V.memset(gbias[:, b:b + 1], 0.0).then_inc(S[f"job_out{b}"], 3)
                V.memset(mneg[:, b:b + 1], 0.0).then_inc(S[f"unit_out{b}"], 1)
                V.memset(nb[:, b:b + 1], 0.0).then_inc(S[f"pair_used{b}"], 1)
            V.memset(zrow, 0.0)
            V.memset(one16, 1.0)
            then(V.memset(ones[:, :], 1.0))
            dve.wait_ge(S["edges_in"], 80)
            V.tensor_copy(srcf, src_i)
            then(V.tensor_copy(dstf, dst_i))
            for b in range(TT + 1):
                i = V.tensor_scalar(reached[:, b * ET:(b + 1) * ET], dstf, float(b * TL), None, ALU.is_ge)
            then(i)
            i = V.tensor_tensor(in_bucket, reached[:, 0:TT * ET], reached[:, ET:(TT + 1) * ET], ALU.subtract)
            i.then_inc(S["tiles_hot"], 1)
            then(V.tensor_copy(wb, ew))
            then(V.tensor_copy(wpart[0], wb))
            then(V.tensor_tensor(wthird, ew, wpart[0], ALU.subtract))
            then(V.tensor_copy(wb, wthird))
            then(V.tensor_copy(wpart[1], wb))
            then(V.tensor_tensor(wthird, wthird, wpart[1], ALU.subtract))
            for g, n in BUCKETS:
                held = held_all[:, 0:n * ET].rearrange("p (b t) -> p b t", b=n)
                no = tq[:, 0:ET].rearrange("p (o t) -> p o t", o=1).to_broadcast([1, n, ET])
                b = take_unit(lambda bank: V.tensor_scalar(held_all[:, 0:n * ET], bank[0:1, 0:n * ET], 0.0, None, ALU.is_gt))
                E.TO[b].wait(dve)
                tmp = tmp_all[:, 0:n * ET].rearrange("p (b t) -> p b t", b=n)
                then(V.scalar_tensor_tensor(tmp, no, 1.0, held, ALU.add, ALU.mult))
                then(V.tensor_reduce(bf[:, 10 + g:10 + g + n], tmp, AX.X, ALU.max))
                then(V.scalar_tensor_tensor(tmp, no, -1000.0, held, ALU.add, ALU.mult))
                then(V.tensor_reduce(bf[:, g:g + n], tmp, AX.X, ALU.min))
            lo_f, hi_f, n_f, cum = bf[:, 0:10], bf[:, 10:20], bf[:, 30:40], bf[:, 40:50]
            then(V.tensor_scalar(lo_f, lo_f, 1000.0, float(EQ - 1), ALU.add, ALU.min))
            then(V.scalar_tensor_tensor(hi_f, lo_f, 1.0, hi_f, ALU.add, ALU.max))
            then(V.tensor_tensor(n_f, hi_f, lo_f, ALU.subtract))
            then(V.tensor_tensor_scan(cum, ones[0:1, 0:10], n_f, 0.0, ALU.mult, ALU.add))
            then(V.tensor_tensor(cum, cum, n_f, ALU.subtract))
            then(V.tensor_scalar(cum, cum, 1.0, None, ALU.add))
            then(V.scalar_tensor_tensor(bf[:, 20:30], lo_f, float(TT * EQ), cum, ALU.add, ALU.subtract))
            then(V.tensor_tensor(bf[:, 50:60], cum, n_f, ALU.add))
            then(V.tensor_copy(bounds[:, 20:30], bf[:, 20:30]))
            then(V.tensor_copy(bounds[:, 30:50], bf[:, 40:60]))
            V.memset(zs[:, 0:1], 0.0).then_inc(S["bounds_ready"], 1)
            dve.wait_ge(S["x_in"], 16)
            with repeat(dve, TT, []) as b:
                first = dve.value_load(bounds[0:1, bass.ds(b + 30, 1)], min_val=1, max_val=TT * EQ)
                end = dve.value_load(bounds[0:1, bass.ds(b + 40, 1)], min_val=2, max_val=TT * EQ + 1)
                shift = dve.value_load(bounds[0:1, bass.ds(b + 20, 1)], min_val=0, max_val=TT * EQ + EQ)
                with dve.Fori(first, end) as turn:
                    pair = nc.s_assert_within(turn + shift - TT * EQ, 0, EQ - 1, skip_runtime_bounds_check_because=
                                              "a bucket's turns run over its range of pairs, within 0 to EQ - 1")
                    for s in range(2):
                        e = bass.ds(pair * 2 + s, 1)
                        dve.wait_ge(S[f"pair_used{s}"], turn)
                        V.tensor_scalar(hot_src[s], iota[0:TL, :], srcf[:, e], None, ALU.is_equal)
                        here = iota[0:TL, bass.ds(b * TL, TL)]
                        V.tensor_scalar(hot_dst[s][:, 0, :], here, dstf[:, e], None, ALU.is_equal)
                        for k, w in enumerate((wpart[0], wpart[1], wthird)):
                            i = V.tensor_scalar(hot_dst[s][:, 1 + k, :], here, dstf[:, e], w[:, e], ALU.is_equal, ALU.mult)
                        i.then_inc(S[f"pair_hot{s}"], 1)
                for h in range(3):
                    V.bn_stats(stats[:, bass.ds(b, 1), h, :], xt[:, bass.ds(b, 1), 2 * h * P:2 * (h + 1) * P])
            E.skip("matrices")
            E.wait_all_out()
            id_t = ident[0:TL, 0:TL]
            then(V.tensor_reduce(deg[0:TL, :], deg3[0:TL, :].rearrange("p (t c) -> p t c", c=3), AX.X, ALU.add))
            V.tensor_scalar(deg[0:TL, :], deg[0:TL, :], 1.0, None, ALU.add).then_inc(S["deg_ready"], 1)
            for t in range(TT):
                dg = wadj[t // 5][:, t % 5, tok(t)]
                i = V.tensor_tensor(dg, dg, id_t, ALU.add)
            then(i)
            dve.wait_ge(S["deg_root"], 1)
            then(V.reciprocal(dinv[0:TL, :], dinv[0:TL, :]))
            scaled = Tally(S["scaled"])
            E.wait_done()
            for t in range(TT):
                if t >= 2:
                    E.JD[E.slot()].wait(dve)
                scaled.inc(V.tensor_scalar(ys[t % 2][0:TL, :], wadj[t // 5][:, t % 5, :], dinv[0:TL, t:t + 1], None, ALU.mult))
                E.skip_in_loop(jobs=1)
            stats_of(xt, 1, have=True)
            stage_rows(xt)
            for t in range(TT):
                dg = cnt[:, t, tok(t)]
                i = V.tensor_tensor(dg, dg, id_t, ALU.add)
            i.then_inc(S["c_ready"], 1)
            E.skip_in_loop(jobs=1)
            for m in range(KD):
                take(lambda s, bank, at, n: V.scalar_tensor_tensor(f1[:, m, bass.ds(at, n)], bank, col("bu", m),
                                                                   f0[:, m, bass.ds(at, n)], ALU.add, ALU.add))

            def features_staged(s, scale=None):
                for g, n in GROUPS:
                    if scale is None:
                        take_unit(lambda bank: V.tensor_copy(hst[s][:, g:g + n, :], view(bank, n, P)))
                    else:
                        sc = scale[0:TL, g:g + n].rearrange("p (t o) -> p t o", o=1).to_broadcast([TL, n, P])
                        take_unit(lambda bank: V.tensor_tensor(hst[s][:, g:g + n, :], view(bank, n, P), sc, ALU.mult))

            E.skip("pair")
            for _ in range(2):
                for s in (E.slot(0), E.slot(1)):
                    features_staged(s, dinv)
                E.skip("pair")
            add_back(xt)
            V.memset(zs[:, 0:1], 0.0).then_inc(S["x_done"], 1)
            if BLOCKS > 1:
                stats_of(xt, 2, have=True)
                then(V.tensor_tensor(var[0:TL, :], mvt[:, :, 1], rs[0:TL, :], ALU.mult))
                then(V.tensor_tensor(var[0:TL, :], var[0:TL, :], rs[0:TL, :], ALU.mult))
                then(V.tensor_copy(rs2[0:TL, :], rs[0:TL, :]))
                root_of(3)
                then(V.tensor_tensor(var[0:TL, :], rs[0:TL, :], rs2[0:TL, :], ALU.mult))
                then(V.tensor_copy(rs[0:TL, :], rs2[0:TL, :]))
                then(V.tensor_copy(rs2[0:TL, :], var[0:TL, :]))
                dve.wait_ge(S["c_saved"], 16)
                stage_rows(xt, scale=rs2)
                E.wait_all_out()
                for k in range(4):
                    i = V.tensor_scalar(f1[:, k, :], f0[:, k, :], col("r_g", k), col("r_b", k), ALU.mult, ALU.add)
                i.then_inc(S["affine_dve"], 1)
                for k in range(4):
                    i = V.tensor_scalar(f0[:, k, :], f0[:, k, :], col("l1_g", k), col("l1_b", k), ALU.mult, ALU.add)
                i.then_inc(S["affine_dve"], 1)
                for t in range(TT):
                    normal(t0[:, t, :], xt[:, t, :], t)
                E.skip("r_in")
                E.wait_all_out()
                then(V.tensor_reduce(g4, g43.rearrange("p (k c) -> p k c", c=3), AX.X, ALU.add))
                then(V.tensor_tensor(g4, g4, rz[:, 0:4, 0], ALU.subtract))
                V.tensor_scalar(g4, g4, 1.0 / (N - 1), None, ALU.mult).then_inc(S["g_ready"], 1)
                E.skip("r_o1", "r_o2", "logits")
                for k in range(2):
                    take(lambda s, bank, at, n: V.tensor_scalar(masks[:, k, bass.ds(at, n)], bank, 0.0, None, ALU.is_gt))
                E.wait_all_out()
                then(V.memset(masks[:, 0:2, 0:1], 1.0))
                then(V.tensor_scalar(masks[:, 2, :], masks[:, 0, :], -1.0, 1.0, ALU.mult, ALU.add))
                V.tensor_scalar(masks[:, 4, :], masks[:, 1, :], -1.0, 1.0, ALU.mult, ALU.add)
                then(V.tensor_tensor(masks[:, 3, :], masks[:, 2, :], masks[:, 1, :], ALU.mult))
                then(V.tensor_tensor(masks[:, 2, :], masks[:, 2, :], masks[:, 4, :], ALU.mult))
                then(V.tensor_tensor(masks[:, 4, :], masks[:, 4, :], masks[:, 0, :], ALU.mult))
                for ts in range(2):
                    for h in range(2):
                        V.memset(qs[ts][h], 0.0)
                E.skip("qk")
                dve.wait_ge(S["x_saved"], 16)
                with E.loop(3, jobs=2, units=6) as i:
                    E.skip_in_loop(jobs=2)
                    for h in range(2):
                        for g, n in GROUPS:
                            take_unit(lambda bank: V.tensor_copy(xt[:, g:g + n, bass.ds(i * (2 * P) + h * P, P)], view(bank, n, P)))
                sl = [E.slot(0), E.slot(1)]
                peak, norm, v_out = Tally(S["max_ready"]), Tally(S["norm_ready"]), Tally(S["v_staged"])
                n0 = CH[0][1]

                def maximum(h):
                    s = sl[h]
                    E.JD[s].add(2)
                    E.JD[s].wait(dve)
                    V.tensor_reduce(mm3[0:TL, 2 * h:2 * h + 1], jp[s][0:TL, 0:2, 0:n0], AX.XY, ALU.max)
                    E.JD[s].add(1)
                    E.JD[s].wait(dve)
                    then(V.tensor_reduce(mm3[0:TL, 2 * h + 1:2 * h + 2], jp[s][0:TL, 2, 0:CH[2][1]], AX.X, ALU.max))
                    peak.inc(V.tensor_scalar(nb[0:TL, h:h + 1], mm3[0:TL, 2 * h:2 * h + 1], mm3[0:TL, 2 * h + 1:2 * h + 2],
                                             -(HD ** -0.5), ALU.max, ALU.mult))
                    E.JO[s].add(3)

                def scale(h):
                    E.JO[sl[h]].wait(dve)
                    then(V.tensor_tensor(rinv[0:TL, h:h + 1], rsum[0:TL, 2 * h:2 * h + 1], rsum[0:TL, 2 * h + 1:2 * h + 2], ALU.add))
                    then(V.reciprocal(rinv[0:TL, h:h + 1], rinv[0:TL, h:h + 1]))
                    norm.inc(V.tensor_scalar(diag[h], ident[0:TL, 0:TL], rinv[0:TL, h:h + 1], None, ALU.mult))

                def two_tiles(hp, i, ends=False):
                    for u in range(4):
                        ts, h = u // 2, u % 2
                        for c, (g, n) in enumerate(GROUPS):
                            E.TD[c % 2].add(1)
                            if c == 1:
                                E.TO[1].add(1)
                                continue
                            E.TD[0].wait(dve)
                            E.TO[0].inc(V.tensor_copy(hst[h][:, g:g + n, 0:TL], view(up[0], n, TL)))
                        if not (ends and u == 3):
                            scale((u + 1) % 2)
                        if not (ends and u >= 2):
                            maximum(h)
                        E.TD[1].add(1)
                        E.TD[1].wait(dve)
                        mine = slice(h * HD, h * HD + HD)
                        E.TO[1].inc(V.tensor_copy(f0[mine, bass.ds(hp, 1), bass.ds(i * (2 * TL) + ts * TL, TL)], up[1][mine, 0:TL]))

                def pair(hp, ends):
                    v_out.inc(V.tensor_copy(vst, xt[:, :, bass.ds(hp * P, P)]))
                    with repeat(dve, 4, list(zip(tallies, [6, 6, 6, 6, 8, 8, 8, 8, 4, 4, 0, 12]))) as i:
                        two_tiles(hp, i)
                    two_tiles(hp, 4, ends)

                tallies = [E.JD[0], E.JD[1], E.JO[0], E.JO[1], E.TD[0], E.TO[0], E.TD[1], E.TO[1], peak, norm, v_out, chain]
                for t in E.TO:
                    t.wait(dve)
                maximum(0)
                maximum(1)
                scale(0)
                with repeat(dve, HP - 1, list(zip(tallies, [30, 30, 30, 30, 40, 40, 40, 40, 20, 20, 1, 60]))) as hp:
                    pair(hp, False)
                pair(HP - 1, True)

                def masked_back(name, mask, with_stats):
                    with E.loop(3, jobs=2, units=6, extra=[(chain, int(with_stats))]) as i:
                        for h in range(2):
                            take(lambda s, bank, at, n: V.scalar_tensor_tensor(
                                ys[s][:, bass.ds(at, n)], bank, col(name, i * 2 + h), masks[:, mask, bass.ds(at, n)],
                                ALU.add, ALU.mult))
                        add_pair(t0, i)
                        if with_stats:
                            settled_stats(t0, i)

                masked_back("bo", 0, True)
                stats_of(t0, 4, have=True)
                stage_rows(t0)
                E.wait_all_out()
                for k in range(4):
                    i = V.tensor_scalar(f0[:, k, :], f0[:, k, :], col("l2_g", k), col("l2_b", k), ALU.mult, ALU.add)
                i.then_inc(S["affine_dve"], 1)
                E.skip("fc1")
                masked_back("fc2_b", 1, False)
                E.wait_all_out()
                stage_rows(t0, norm=False)
                with E.loop(3, jobs=2) as i:
                    for h in range(2):
                        take(lambda s, bank, at, n: V.tensor_tensor(f1[:, bass.ds(i * 2 + h, 1), bass.ds(at, n)], bank,
                                                                    masks[:, bass.ds(i + 2, 1), bass.ds(at, n)], ALU.mult))
                dve.wait_ge(S["x_back"], 16)
                with E.loop(3, jobs=2, units=6, extra=[(chain, 2)]) as i:
                    E.skip_in_loop(jobs=2)
                    add_pair(t0, i)
                    for t in E.TO:
                        t.wait(dve, alone=True)
                    x = xt[:, :, bass.ds(i * (2 * P), 2 * P)]
                    then(V.tensor_tensor(x, x, t0[:, :, bass.ds(i * (2 * P), 2 * P)], ALU.add))
                    then(chunk_stats(xt, i))
                V.memset(zs[:, 0:1], 0.0).then_inc(S["x_done"], 1)
            if BLOCKS > 2:
                stats_of(xt, 5, have=True)
                for layer in range(2):
                    b = take_unit(lambda bank: V.tensor_copy(att_v[:, layer * 2 * KD:(layer + 1) * 2 * KD], bank[:, 0:2 * KD]))
                stage_rows(xt)
                staged = Tally(S["h_staged"])
                e_out, p_in, alpha = Tally(S["e_ready"]), Tally(S["p_ready"]), Tally(S["alpha_ready"])
                for layer in range(2):
                    E.wait_done()
                    for t in E.TO:
                        t.wait(dve)
                    V.tensor_copy(hs[0][0:2, 0:P], ident[0:2, 0:1].to_broadcast([2, P])).then_inc(S["att_ready"], 1)
                    E.skip_in_loop(jobs=2)
                    b = take_unit(lambda bank: V.tensor_copy(ad[0:TL, :], bank[0:TL, 1:2 * TT:2]))
                    E.wait_all_out()
                    E.wait_done()
                    if layer == 0:
                        dve.wait_ge(S["c_back"], 16)
                    with E.loop(TT // 2, units=6, extra=[(e_out, 2), (p_in, 2), (alpha, 2), (chain, 14)]) as i:
                        for s in range(2):
                            t = i * 2 + s
                            h, c = hs[s][0:TL, 0:N], cnt[:, bass.ds(t, 1), :]
                            then(V.tensor_scalar(h, c, 0.0, -BIG, ALU.is_equal, ALU.mult))
                            then(V.tensor_tensor(h, h, kst[0:TL, :], ALU.add))
                            then(V.tensor_scalar(h, h, ad[0:TL, bass.ds(t, 1)], None, ALU.add, ALU.max, accum_out=zs[0:TL, s:s + 1]))
                            then(V.scalar_tensor_tensor(h, h, 0.2, h, ALU.mult, ALU.max))
                            then(V.scalar_tensor_tensor(zs[0:TL, 2 + s:3 + s], zs[0:TL, s:s + 1], 0.2, zs[0:TL, s:s + 1], ALU.mult, ALU.max))
                            e_out.inc(V.tensor_scalar(mneg[0:TL, s:s + 1], zs[0:TL, 2 + s:3 + s], -1.0, None, ALU.mult))
                        for s in range(2):
                            t = i * 2 + s
                            p_in.add(1)
                            p_in.wait(dve, alone=True)
                            if s == 0:
                                E.TD[0].wait(dve, alone=True)
                                E.TD[1].wait(dve, alone=True)
                            then(V.scalar_tensor_tensor(ys[s][0:TL, :], hs[s][0:TL, 0:N], 1.0, cnt[:, bass.ds(t, 1), :],
                                                        ALU.mult, ALU.mult, accum_out=rinv[0:TL, s:s + 1]))
                            then(V.reciprocal(zs[0:TL, s:s + 1], rinv[0:TL, s:s + 1]))
                            alpha.inc(V.tensor_scalar(ys[s][0:TL, :], ys[s][0:TL, :], zs[0:TL, s:s + 1], None, ALU.mult))
                        E.skip_in_loop(units=6)
                    E.skip("pairs3")
                    E.wait_all_out()

                    def stage_pair(i):
                        for h in range(2):
                            staged.inc(V.tensor_copy(gstage[E.slot(h)], f1[:, i * 2 + h, :]))

                    stage_pair(0)
                    for i in range(3):
                        for h in range(2):
                            features_staged(E.slot(h))
                        if i < 2:
                            stage_pair(i + 1)
                        if layer and i:
                            then(chunk_stats(xt, i - 1))
                        E.skip_in_loop(jobs=2)
                        if layer:
                            add_pair(xt, i)
                    if layer:
                        settled_stats(xt, 2)
                V.memset(zs[:, 0:1], 0.0).then_inc(S["x_done"], 1)
            if BLOCKS > 3:
                stats_of(xt, 6, have=True)
                stage_rows(xt)
                for t in range(TT):
                    normal(t0[:, t, :], xt[:, t, :], t)
                V.memset(zs[:, 1:2], 0.0).then_inc(S["stream_ready"], 1)
                E.skip("m_w1")
                E.skip_in_loop(jobs=1)
                b = take_unit(lambda bank: V.tensor_copy(lg[0:TL, :], bank[0:TL, 0:8 * TT]))
                E.TO[b].wait(dve)
                lg3, pr3, t3, oh3 = [x[0:TL, :].rearrange("p (t e) -> p t e", t=TT) for x in (lg, pr, t8, oh)]
                top = m10[0:TL, 0:TT]

                def wide(x):
                    return x.rearrange("p (t o) -> p t o", o=1).to_broadcast([TL, TT, EXPERTS])

                number = iota[0:TL, 0:EXPERTS].rearrange("p (o e) -> p o e", o=1).to_broadcast([TL, TT, EXPERTS])
                then(V.tensor_reduce(top, lg3, AX.X, ALU.max))
                V.tensor_tensor(lg3, lg3, wide(top), ALU.subtract).then_inc(S["lg_ready"], 1)
                dve.wait_ge(S["lg_exp"], 1)
                then(V.tensor_reduce(top, lg3, AX.X, ALU.add))
                then(V.reciprocal(m10[0:TL, 10:20], top))
                then(V.tensor_tensor(lg3, lg3, wide(m10[0:TL, 10:20]), ALU.mult))
                then(V.tensor_copy(pr3, lg3))
                hot = [lg3, t3]
                gates = m10[0:TL, 0:CHOICES * TT]
                for c in range(CHOICES):
                    top = gates[:, c * TT:(c + 1) * TT]
                    then(V.tensor_reduce(top, pr3, AX.X, ALU.max))
                    then(V.tensor_tensor(t3, pr3, wide(top), ALU.not_equal))
                    then(V.scalar_tensor_tensor(t3, t3, 100.0, number, ALU.mult, ALU.add))
                    then(V.tensor_reduce(m10[0:TL, 20:30], t3, AX.X, ALU.min))
                    then(V.tensor_tensor(hot[c], number, wide(m10[0:TL, 20:30]), ALU.is_equal))
                    if c == 0:
                        then(V.scalar_tensor_tensor(pr3, hot[0], -4.0, pr3, ALU.mult, ALU.add))
                V.tensor_tensor(oh3, hot[0], hot[1], ALU.add).then_inc(S["chosen"], 1)
                room = [ys[1][0:TL, 700 + k * 80:780 + k * 80] for k in range(3)]
                rank, upto, scratch = [x.rearrange("p (t e) -> p t e", t=TT) for x in room]
                fine = hs[1][0:TL, D + 110:D + 310]
                dve.wait_ge(S["chosen"], 2)
                V.tensor_copy(rank, up[1][0:TL, 0:80].rearrange("p (t e) -> p t e", t=TT))
                then(V.tensor_copy(scratch, up[1][0:TL, 80:160].rearrange("p (t e) -> p t e", t=TT)))
                then(V.memset(upto[:, 0, :], 0.0))
                for t in range(1, TT):
                    then(V.tensor_tensor(upto[:, t, :], upto[:, t - 1, :], scratch[:, t - 1, :], ALU.add))
                small8 = fine[:, 160:200]
                load, slots, cum, begin = [small8[:, k * 8:k * 8 + 8] for k in range(4)]
                V.tensor_tensor(rank, rank, upto, ALU.add)
                then(V.tensor_tensor(load, upto[:, TT - 1, :], scratch[:, TT - 1, :], ALU.add))
                steps = iota[0:TL, 0:(TT - 1) * P + 1:P]
                cmp = fine[:, 0:80].rearrange("p (e k) -> p e k", e=EXPERTS)
                then(V.tensor_tensor(cmp, load.rearrange("p (e k) -> p e k", k=1).to_broadcast([TL, EXPERTS, TT]),
                                     steps.rearrange("p (e k) -> p e k", e=1).to_broadcast([TL, EXPERTS, TT]), ALU.is_gt))
                then(V.tensor_reduce(slots, cmp, AX.X, ALU.add))
                then(V.tensor_scalar(slots, slots, 1.0, None, ALU.max))
                then(V.tensor_tensor_scan(cum, ones[0:TL, 0:EXPERTS], slots, 0.0, ALU.mult, ALU.add))
                then(V.tensor_tensor(begin, cum, slots, ALU.subtract))
                then(V.tensor_scalar(begin, begin, 1.0, None, ALU.add))
                V.tensor_copy(first_slot[:, 0:EXPERTS], begin[0:1, :])
                then(V.tensor_scalar(cum, cum, 1.0, None, ALU.add))
                then(V.tensor_copy(first_slot[:, EXPERTS:EXPERTS + 1], cum[0:1, EXPERTS - 1:EXPERTS]))
                then(V.tensor_scalar(cum, cum, -1.0, float(SLOTS + 1), ALU.mult, ALU.add))
                V.tensor_copy(first_slot[:, EXPERTS + 1:EXPERTS + 2], cum[0:1, EXPERTS - 1:EXPERTS])
                base, order, count, row, place = [ys[1][0:TL, 940 + k * 20:960 + k * 20] for k in range(5)]
                starts = begin.rearrange("p (t e) -> p t e", t=1).to_broadcast([TL, TT, EXPERTS])
                for c in range(CHOICES):
                    mine = slice(c * TT, (c + 1) * TT)
                    then(V.tensor_tensor(scratch, hot[c], starts, ALU.mult))
                    then(V.tensor_reduce(base[:, mine], scratch, AX.X, ALU.add))
                    then(V.tensor_tensor(scratch, hot[c], rank, ALU.mult))
                    then(V.tensor_reduce(order[:, mine], scratch, AX.X, ALU.add))
                cmp = ys[1][0:TL, 1040:1240].rearrange("p (i k) -> p i k", k=TT)
                then(V.tensor_tensor(cmp, order.rearrange("p (i k) -> p i k", k=1).to_broadcast([TL, CHOICES * TT, TT]),
                                     steps.rearrange("p (i k) -> p i k", i=1).to_broadcast([TL, CHOICES * TT, TT]), ALU.is_ge))
                then(V.tensor_reduce(count, cmp, AX.X, ALU.add))
                then(V.tensor_scalar(count, count, -1.0, None, ALU.add))
                then(V.scalar_tensor_tensor(row, count, -float(P), order, ALU.mult, ALU.add))
                then(V.tensor_tensor(base, base, count, ALU.add))
                then(V.tensor_scalar(place, base, -1.0, float(P), ALU.add, ALU.mult))
                then(V.tensor_tensor(place, place, row, ALU.add))
                V.tensor_copy(places, place)
                wide_slot = [TL, CHOICES * TT, SLOTS + 2]
                V.tensor_tensor(hot_slot, base.rearrange("p (i k) -> p i k", k=1).to_broadcast(wide_slot),
                                iota[0:TL, 1:SLOTS + 3].rearrange("p (i k) -> p i k", i=1).to_broadcast(wide_slot), ALU.is_equal)
                dve.wait_ge(S["rows_in"], 64)
                for i in range(CHOICES * TT):
                    hr = V.tensor_scalar(hot_row[i // TT][:, i % TT, :], iota[0:TL, 0:P], row[:, i:i + 1],
                                         token_no[:, i % TT:i % TT + 1], ALU.is_equal, ALU.mult)
                hr.then_inc(S["one_hot"], 1)
                g2 = gates.rearrange("p (c t) -> p c t", c=CHOICES)
                total = m10[0:TL, 20:30]
                then(V.tensor_tensor(total, gates[:, 0:TT], gates[:, TT:2 * TT], ALU.add))
                then(V.tensor_scalar(total, total, 1e-8, None, ALU.add))
                then(V.reciprocal(total, total))
                V.tensor_tensor(g2, g2, total.rearrange("p (c t) -> p c t", c=1).to_broadcast([TL, CHOICES, TT]), ALU.mult)
                dve.wait_ge(S["one_hot"], 2)
                V.tensor_copy(members, up[0][:, 0:SLOTS + 2]).then_inc(S["route_ready"], 1)
                dve.wait_ge(S["route_ready"], 1)

                def features():
                    V.tensor_copy(x_feat[:, 0:4 * P], jp[0][:, 2, :])
                    V.tensor_copy(x_feat[:, 4 * P:KD * P], jp[1][:, 2, 0:2 * P]).then_inc(S["xt_ready"], 1)

                V.memset(zs[:, 0:1], 0.0).then_inc(S["y_ready"], 1)
                V.memset(zs[:, 2:3], 0.0).then_inc(S["y_free"], 1)
                V.memset(zs[:, 3:4], 0.0).then_inc(S["up_done1"], 1)
                dve.wait_ge(S["x_turned"], 1)
                features()
                for t in range(TT):
                    V.tensor_tensor(xt[:, t, :], xt[:, t, :], hs[1][0:TL, 0:D], ALU.add)
                end = dve.value_load(first_slot[0:1, EXPERTS:EXPERTS + 1], min_val=2, max_val=SLOTS)
                with dve.Fori(1, end) as s:
                    dve.wait_ge(S["x_turned"], s + 1)
                    features()
                    dve.wait_ge(S["y_free"], s)
                    for c in range(2):
                        dve.wait_ge(S[f"up_done{c}"], s + c)
                        o = V.tensor_copy(y_rows[:, c * (D // 2):(c + 1) * (D // 2)], jp[1][:, c, 0:D // 2])
                    o.then_inc(S["y_ready"], 1)
                for i in range(CHOICES * TT):
                    c, t = i % 2, i // 2
                    if i % 4 == 0:
                        dve.wait_ge(S[f"y_gathered{i // 4}"], 64)
                    k = c * TT + t
                    then(V.scalar_tensor_tensor(t0[:, t, :], y_got[k], gates[:, k:k + 1], t0[:, t, :], ALU.mult, ALU.add))
                    if c == 1:
                        for h in range(3):
                            b = V.bn_stats(stats[:, t, h, :], t0[:, t, 2 * h * P:2 * (h + 1) * P])
                then(b)
                stats_of(t0, 7, have=True)
                V.scalar_tensor_tensor(rs2[0:TL, :], mvt[:, :, 0], -1.0, rs[0:TL, :], ALU.mult, ALU.mult).then_inc(S["shift_ready"], 1)
                for t in range(TT):
                    dve.wait_ge(S["normal_ready"], t + 1)
                    then(V.tensor_tensor(t0[:, t, :], t0[:, t, :], hs[0][0:TL, 0:D], ALU.mult))
                    V.tensor_tensor(xt[:, t, :], xt[:, t, :], t0[:, t, :], ALU.add).then_inc(S["out_tile"], 1)

        @block.gpsimd
        def _(pool):
            E = Side(pool, S)
            E.skip("counts", "matrices")
            for t in E.JD:
                t.wait(pool)
            pool.dma_start(hs[1][0:BOT, 0:D], A["wu"]).then_inc(S["wu_in"], 16)
            pool.dma_start(dif, A["dif"]).then_inc(S["wu_in"], 16)
            pool.wait_ge(S["c_ready"], 1)
            pool.dma_start(c_dram, c_all).then_inc(S["c_saved"], 16)
            E.skip("w_transpose", "rows", "adapter", "pair", "pair_back", "pair", "pair_back", "pair", "pairs3_back")
            if BLOCKS > 1:
                pool.wait_ge(S["x_done"], 1)
                pool.dma_start(x_dram, X[0:TL, :]).then_inc(S["x_saved"], 16)
                E.skip("rows", "r_in", "r_o1", "r_o2", "logits", "masks", "qk", "pairs3_back")
                E.wait_all_out()
                q_out = Tally(S["q_staged"])
                done = [Tally(S["job_done0"], E.JD[0].count - 3), Tally(S["job_done1"], E.JD[1].count - 3)]
                with repeat(pool, HP, [(q_out, 20), (done[0], 30), (done[1], 30)]) as hp:
                    with repeat(pool, TT // 2, [(q_out, 4), (done[0], 6), (done[1], 6)]) as i:
                        for ts in range(2):
                            for d in done:
                                d.wait(pool)
                                d.add(3)
                            for h in range(2):
                                mine = slice(h * HD, h * HD + HD)
                                q_out.inc(nc.gpsimd.tensor_copy(
                                    qs[ts][h][mine, :], f1[mine, bass.ds(hp, 1), bass.ds(i * (2 * TL) + ts * TL, TL)]))
                                q_out.wait(pool, alone=True)
                E.skip("attention")
                for t in E.TD:
                    t.wait(pool)
                pool.dma_start(X[0:TL, :], x_dram).then_inc(S["x_back"], 16)
                E.skip("pairs3_back", "rows", "fc1", "pairs3_back", "rows", "pairs3")
                for t in E.JO:
                    t.wait(pool)
                if BLOCKS > 2:
                    pool.dma_start(wt.rearrange("p (l f) -> p l f", l=2), A["gat_wt"]).then_inc(S["wt_in"], 16)
                E.skip("pairs3_back")
                pool.wait_ge(S["x_done"], 2)
                pool.wait_ge(S["c_saved"], 16)
                pool.dma_start(c_all, c_dram).then_inc(S["c_back"], 16)
            if BLOCKS > 2:
                E.skip("vectors", "rows")
                for layer in range(2):
                    E.skip("att", "alpha", "pairs3", f"agg{layer}")
            if BLOCKS > 3:
                E.wait_done()
                pool.dma_start(hs[0][0:TL, 0:D], A["gamma"].to_broadcast([TL, D])).then_inc(S["rows_in"], 16)
                pool.dma_start(hs[1][0:TL, 0:D], A["beta"].to_broadcast([TL, D])).then_inc(S["rows_in"], 16)
                pool.dma_start(before, A["before"]).then_inc(S["rows_in"], 16)
                pool.dma_start(token_no, A["token_no"]).then_inc(S["rows_in"], 16)
                pool.wait_ge(S["stream_ready"], 1)
                pool.dma_start(stream_dram.rearrange("(t p) d -> p t d", p=TL), t0).then_inc(S["stream_saved"], 16)
                pool.wait_ge(S["route_ready"], 1)
                pool.wait_ge(S["stream_saved"], 16)

                def gather(slot, s):
                    nc.gpsimd.tensor_copy(member, members[:, bass.ds(slot, 1)]).then_inc(S["member_ready"], 1)
                    pool.wait_ge(S["member_ready"], s)
                    pool.sem_inc(Tally.passed[pool.engine], 1)
                    nc.gpsimd.indirect_dma_start(x_rows, None, stream_dram, bass.IndirectOffsetOnAxis(ap=member, axis=0)).then_inc(
                        S["x_gathered"], 16)

                gather(0, 1)
                pool.wait_ge(S["x_turned"], 1)
                gather(1, 2)
                end = pool.value_load(first_slot[0:1, EXPERTS:EXPERTS + 1], min_val=2, max_val=SLOTS)
                empty = pool.value_load(first_slot[0:1, EXPERTS + 1:EXPERTS + 2], min_val=1, max_val=SLOTS - 1)
                with pool.Fori(1, end) as s:
                    pool.wait_ge(S["x_turned"], s + 1)
                    gather(s + 1, s + 2)
                    pool.wait_ge(S["y_ready"], s + 1)
                    pool.dma_start(y_dram[bass.ds(s * P - P, P), :], y_rows).then_inc(S["y_saved"], 16)
                    pool.wait_ge(S["y_saved"], s * 16)
                    pool.sem_inc(S["y_free"], 1)
                pool.wait_ge(S["y_free"], end)
                pool.wait_ge(S["y_filled"], empty * 16)
                pool.wait_ge(S["x_gathered"], end * 16 + 16)
                pool.sem_inc(Tally.passed[pool.engine], 1)
                for i in range(CHOICES * TT):
                    k = i % 2 * TT + i // 2
                    nc.gpsimd.indirect_dma_start(y_got[k], None, y_dram, bass.IndirectOffsetOnAxis(ap=places[:, k:k + 1], axis=0)).then_inc(
                        S[f"y_gathered{i // 4}"], 16)


def kernel(**inputs):
    import concourse.bacc as bacc
    from concourse.bass_utils import run_bass_kernel_spmd

    a = {k: np.ascontiguousarray(v) for k, v in inputs.items()}

    def tiles(w):
        k, m = w.shape
        return np.ascontiguousarray(w.reshape(k // P, P, m // P, P).transpose(2, 1, 0, 3).reshape(m // P, P, k))

    def narrow(w):
        return np.ascontiguousarray(w.reshape(-1, P, w.shape[1]).transpose(1, 0, 2))

    def edges(e):
        return np.ascontiguousarray(e.reshape(ET, TL).T)

    f, g, m = "L0_ffn_", "L0_gnn_", "L1_ffn_"
    vec = {"bd": a[g + "bd"], "bu": a[g + "bu"], "gb1": a[g + "b1"], "gb2": a[g + "b2"], "r_g": a[f + "r_ln_g"],
           "r_b": a[f + "r_ln_b"], "l1_g": a[f + "ln1_g"], "l1_b": a[f + "ln1_b"], "r_in_b": a[f + "r_in_b"],
           "r_o1_b": a[f + "r_o1_b"], "r_o2_b": a[f + "r_o2_b"], "r_o3_b": a[f + "r_o3_b"], "bq": a[f + "bq"],
           "bk": a[f + "bk"], "bv": a[f + "bv"], "bo": a[f + "bo"], "l2_g": a[f + "ln2_g"], "l2_b": a[f + "ln2_b"],
           "fc1_b": a[f + "fc1_b"], "fc2_b": a[f + "fc2_b"], "as1": a["L1_gnn_att_src1"], "ad1": a["L1_gnn_att_dst1"],
           "gat_b1": a["L1_gnn_b1"], "as2": a["L1_gnn_att_src2"], "ad2": a["L1_gnn_att_dst2"], "gat_b2": a["L1_gnn_b2"],
           "m_b1": a[m + "b1"], "m_b2": a[m + "b2"], "down_b": a[m + "down_b"].reshape(-1)}
    cols = np.zeros((P, NCOL), np.float32)
    for name, n in VECTORS:
        v = vec[name]
        if v.size < P:
            cols[:v.size, COL[name]] = v
        else:
            cols[:, COL[name]:COL[name] + n] = v.reshape(n, P).T
    dif = np.zeros((4, 2, P), np.float32)
    for k in range(2):
        dif[2 * k, k], dif[2 * k + 1, k] = -1.0, 1.0
    arrays = {
        "src": edges(a["src"]), "dst": edges(a["dst"]), "ew": edges(a["edge_weight"]),
        "iota": np.ascontiguousarray(np.broadcast_to(np.arange(N, dtype=np.float16), (P, N))),
        "pairno": (np.arange(ET) // 2).astype(np.float32).reshape(1, ET),
        "ident": np.eye(P, dtype=np.float32), "cols": cols, "dif": dif,
        "x": np.ascontiguousarray(a["x"].reshape(TT, TL, D).transpose(1, 0, 2)),
        "wd": narrow(a[g + "Wd"]), "w3": narrow(a[f + "r_o3_w"].T), "wm2": narrow(a[m + "w2"]), "wu": a[g + "Wu"],
        "w1": tiles(a[g + "W1"]), "w2": tiles(a[g + "W2"]), "r_in": tiles(a[f + "r_in_w"].T),
        "r_o1": tiles(a[f + "r_o1_w"].T), "r_o2": tiles(a[f + "r_o2_w"].T),
        "wqkv": np.concatenate([tiles(a[f + w].T) for w in ("wq", "wk", "wv")]), "wo": tiles(a[f + "wo"].T),
        "fc1": tiles(a[f + "fc1_w"].T), "fc2": tiles(a[f + "fc2_w"].T),
        "lra_down": tiles(a[f + "lra_down"].reshape(D, D).T),
        "lra_up": tiles(a[f + "lra_up"].transpose(0, 2, 1).reshape(D, D)),
        "gat_wt": np.stack([narrow(a[f"L1_gnn_W{k}"].T).reshape(P, KD * D) for k in (1, 2)], 1),
        "gat_w1": tiles(a["L1_gnn_W1"]), "gat_w2": tiles(a["L1_gnn_W2"]), "m_w1": tiles(a[m + "w1"]),
        "down": tiles(a[m + "down_w"].transpose(1, 0, 2).reshape(D, EXPERTS * DE)).reshape(EXPERTS, KE, P, D)
        .transpose(0, 2, 1, 3).reshape(EXPERTS, P, KE * D),
        "up": a[m + "up_w"].reshape(EXPERTS, KE, P, D).transpose(0, 2, 1, 3).reshape(EXPERTS, P, KE * D),
        "before": np.concatenate([np.triu(np.ones((TL, TL), np.float32), 1), np.ones((TL, TL), np.float32)], 1),
        "token_no": np.ascontiguousarray(np.arange(N, dtype=np.float32).reshape(TT, TL).T),
        "gamma": a[m + "gamma"].reshape(1, D), "beta": a[m + "beta"].reshape(1, D),
    }
    nc = bacc.Bacc("TRN2", target_bir_lowering=False, num_devices=1)
    A = {k: nc.dram_tensor(f"in_{k}", v.shape, mybir.dt.from_np(v.dtype), kind="ExternalInput").ap() for k, v in arrays.items()}
    out = nc.dram_tensor("result", (TL, TT, D), F32, kind="ExternalOutput").ap()
    build(nc, A, out)
    r = run_bass_kernel_spmd(nc, [{f"in_{k}": v for k, v in arrays.items()}], core_ids=[0])
    return r.results[0]["result"].transpose(1, 0, 2).reshape(N, D)
```
